# Optimizing a Trainium2 kernel written in Bass

```python
import numpy as np
import jax
import jax.numpy as jnp

def _softmax(x, axis=-1):
    return jax.nn.softmax(x, axis=axis)

def _gelu(x):
    return jax.nn.gelu(x, approximate=True)

def _silu(x):
    return jax.nn.silu(x)

def _sigmoid(x):
    return jax.nn.sigmoid(x)

def _layernorm(x, axis=-1, eps=1e-05):
    m = jnp.mean(x, axis=axis, keepdims=True)
    v = jnp.var(x, axis=axis, keepdims=True)
    return (x - m) / jnp.sqrt(v + eps)

def _scatter_add(tgt, idx, src, axis=0):
    return tgt.at[idx].add(src)

def _segment_sum(src, seg, n):
    return jax.ops.segment_sum(src, seg, n)
kernel_name = 'mk_gps_d2_gnn_r8_020aed'

def setup_inputs(seed: int=0):
    np.random.seed(seed)
    _w = jnp.asarray

    def _rec_inputs():
        import jax
        import jax.numpy as jnp
        _gk = jax.random.key(seed)
        x = -0.0001394 + 0.9999 * jax.random.normal(jax.random.fold_in(_gk, 1), (1250, 768), jnp.float32)
        src = jax.random.randint(jax.random.fold_in(_gk, 2), (20000,), 0, 1250, jnp.int32)
        dst = jnp.minimum((1250 * jax.random.uniform(jax.random.fold_in(_gk, 3), (20000,)) ** 2.0).astype(jnp.int32), 9999)
        _o = jnp.argsort(dst, stable=True)
        src = src[_o]
        dst = dst[_o]
        edge_weight = jax.random.uniform(jax.random.fold_in(_gk, 12), (20000,), jnp.float32, 0.0, 0.999998)
        return (x, src, dst, edge_weight)
    x, src, dst, edge_weight = _rec_inputs()

    def _L0_gnn_setup():
        import jax, jax.numpy as jnp
        import numpy as np
        N = 6250
        E = 62500
        D = 768
        H = 256
        R = 32

        def _gcn(x, W, b, row, col, ew):
            x = x @ W
            n = x.shape[0]
            deg = jax.ops.segment_sum(ew, col, num_segments=n) + 1.0
            dinv = jax.lax.rsqrt(deg)
            norm = dinv[row] * ew * dinv[col]
            agg = jax.ops.segment_sum(norm[:, None] * x[row], col, num_segments=n)
            return agg + (dinv * dinv)[:, None] * x + b
        key = jax.random.key(seed)
        ks = jax.random.split(key, 8)
        d = D // R
        w = lambda k, sh: jax.random.normal(k, sh, jnp.float32) * 0.05
        return {'x': jax.random.normal(ks[0], (N, D), jnp.float32), 'edge_index': jax.random.randint(ks[1], (2, E), 0, N), 'edge_weight': jax.random.uniform(ks[2], (E,), jnp.float32), 'Wd': w(ks[3], (D, d)), 'bd': jnp.zeros((d,), jnp.float32), 'Wu': w(ks[4], (d, D)), 'bu': jnp.zeros((D,), jnp.float32), 'W1': w(ks[5], (D, H)), 'b1': jnp.zeros((H,), jnp.float32), 'W2': w(ks[6], (H, D)), 'b2': jnp.zeros((D,), jnp.float32)}
    _L0_gnn_all = _L0_gnn_setup()
    _L0_gnn_in = {k: v for k, v in _L0_gnn_all.items() if k in ('Wd', 'bd', 'Wu', 'bu', 'W1', 'b1', 'W2', 'b2')}
    del _L0_gnn_all

    def _L0_mix_setup():
        import jax, jax.numpy as jnp
        import numpy as np
        DIM = 768
        NUM_HEADS = 12
        HEAD_DIM = DIM // NUM_HEADS
        ORDER = 2
        SCALE = HEAD_DIM ** (-0.5)
        key = jax.random.key(seed)
        k_x, k_qkv, k_pw, k_pb = jax.random.split(key, 4)
        B, N = (16, 577)
        x = jax.random.normal(k_x, (B, N, DIM), dtype=jnp.float32)
        qkv_w = jax.random.normal(k_qkv, (3 * DIM, DIM), dtype=jnp.float32) * 0.02
        proj_w = jax.random.normal(k_pw, (DIM, DIM), dtype=jnp.float32) * 0.02
        proj_b = jax.random.normal(k_pb, (DIM,), dtype=jnp.float32) * 0.02
        return {'x': x, 'qkv_w': qkv_w, 'proj_w': proj_w, 'proj_b': proj_b}
    _L0_mix_all = _L0_mix_setup()
    _L0_mix_in = {k: v for k, v in _L0_mix_all.items() if k in ('qkv_w', 'proj_w', 'proj_b')}
    del _L0_mix_all

    def _L0_ffn_setup():
        import jax, jax.numpy as jnp
        import numpy as np
        import math
        B, T, C = (8, 256, 768)
        E = 3
        HD = C // E
        TOPK = 2
        NGLOB = 4

        def _masked_softmax(att, mask):
            att = jnp.where(mask, -jnp.inf, att)
            return jax.nn.softmax(att, axis=-1)
        key = jax.random.key(seed)
        ks = jax.random.split(key, 16)
        s = 0.02
        return {'x': jax.random.normal(ks[0], (B, T, C), jnp.float32), 'Wqk': jax.random.normal(ks[1], (C, 2 * C), jnp.float32) * s, 'bqk': jnp.zeros((2 * C,), jnp.float32), 'Wv': jax.random.normal(ks[2], (E, C, HD), jnp.float32) * s, 'bv': jnp.zeros((E, HD), jnp.float32), 'conv_w': jax.random.normal(ks[3], (HD, 1, 3), jnp.float32) * s, 'conv_b': jnp.zeros((HD,), jnp.float32), 'glob': jax.random.normal(ks[4], (NGLOB, HD), jnp.float32) * 0.02, 'pos_bias': jnp.zeros((64, 64), jnp.float32), 'Wg1': jax.random.normal(ks[5], (C, 32), jnp.float32) * s, 'bg1': jnp.zeros((32,), jnp.float32), 'Wg2': jax.random.normal(ks[6], (32, E), jnp.float32) * s, 'bg2': jnp.zeros((E,), jnp.float32), 'Wp': jax.random.normal(ks[7], (C, C), jnp.float32) * s, 'bp': jnp.zeros((C,), jnp.float32)}
    _L0_ffn_all = _L0_ffn_setup()
    _L0_ffn_in = {k: v for k, v in _L0_ffn_all.items() if k in ('Wqk', 'bqk', 'Wv', 'bv', 'conv_w', 'conv_b', 'glob', 'pos_bias', 'Wg1', 'bg1', 'Wg2', 'bg2', 'Wp', 'bp')}
    del _L0_ffn_all

    def _L1_gnn_setup():
        import jax, jax.numpy as jnp
        import numpy as np
        N_NODES = 1250
        N_EDGES = 12500
        DIM = 768
        NEG_SLOPE = 0.2

        def gat_conv(x, src, dst, W, att_src, att_dst, bias, num_nodes):
            h = x @ W
            a_s = h @ att_src
            a_d = h @ att_dst
            e = jax.nn.leaky_relu(a_s[src] + a_d[dst], NEG_SLOPE)
            m = jax.ops.segment_max(e, dst, num_segments=num_nodes)
            e = jnp.exp(e - m[dst])
            denom = jax.ops.segment_sum(e, dst, num_segments=num_nodes)
            alpha = e / denom[dst]
            msg = alpha[:, None] * h[src]
            out = jax.ops.segment_sum(msg, dst, num_segments=num_nodes)
            return out + bias
        key = jax.random.key(seed)
        ks = jax.random.split(key, 12)
        s = 1.0 / np.sqrt(DIM)
        inp = {'x': jax.random.normal(ks[0], (N_NODES, DIM), dtype=jnp.float32), 'edge_index': jax.random.randint(ks[1], (2, N_EDGES), 0, N_NODES, dtype=jnp.int64), 'W1': jax.random.normal(ks[2], (DIM, DIM), dtype=jnp.float32) * s, 'att_src1': jax.random.normal(ks[3], (DIM,), dtype=jnp.float32) * s, 'att_dst1': jax.random.normal(ks[4], (DIM,), dtype=jnp.float32) * s, 'b1': jnp.zeros((DIM,), dtype=jnp.float32), 'W2': jax.random.normal(ks[5], (DIM, DIM), dtype=jnp.float32) * s, 'att_src2': jax.random.normal(ks[6], (DIM,), dtype=jnp.float32) * s, 'att_dst2': jax.random.normal(ks[7], (DIM,), dtype=jnp.float32) * s, 'b2': jnp.zeros((DIM,), dtype=jnp.float32)}
        return inp
    _L1_gnn_all = _L1_gnn_setup()
    _L1_gnn_in = {k: v for k, v in _L1_gnn_all.items() if k in ('W1', 'att_src1', 'att_dst1', 'b1', 'W2', 'att_src2', 'att_dst2', 'b2')}
    del _L1_gnn_all

    def _L1_mix_setup():
        import jax, jax.numpy as jnp
        import numpy as np
        FEATS = 768
        HEAD = 12

        def _phi(t):
            return jax.nn.elu(t) + 1.0
        key = jax.random.key(seed)
        ks = jax.random.split(key, 9)
        f = FEATS
        s = 1.0 / np.sqrt(f)
        x = jax.random.normal(ks[0], (4, 512, f), dtype=jnp.float32)
        Wq = jax.random.normal(ks[1], (f, f), dtype=jnp.float32) * s
        bq = jax.random.normal(ks[2], (f,), dtype=jnp.float32) * 0.01
        Wk = jax.random.normal(ks[3], (f, f), dtype=jnp.float32) * s
        bk = jax.random.normal(ks[4], (f,), dtype=jnp.float32) * 0.01
        Wv = jax.random.normal(ks[5], (f, f), dtype=jnp.float32) * s
        bv = jax.random.normal(ks[6], (f,), dtype=jnp.float32) * 0.01
        Wo = jax.random.normal(ks[7], (f, f), dtype=jnp.float32) * s
        bo = jax.random.normal(ks[8], (f,), dtype=jnp.float32) * 0.01
        return {'x': x, 'Wq': Wq, 'bq': bq, 'Wk': Wk, 'bk': bk, 'Wv': Wv, 'bv': bv, 'Wo': Wo, 'bo': bo}
    _L1_mix_all = _L1_mix_setup()
    _L1_mix_in = {k: v for k, v in _L1_mix_all.items() if k in ('Wq', 'bq', 'Wk', 'bk', 'Wv', 'bv', 'Wo', 'bo')}
    del _L1_mix_all

    def _L1_ffn_setup():
        import jax, jax.numpy as jnp
        import numpy as np
        DIM = 768
        NUM_EXPERTS = 8
        TOP_K = 2
        MLP_RATIO = 4
        CAPACITY_RATIO = 1.25
        key = jax.random.key(seed)
        ks = jax.random.split(key, 6)
        B, N, C = (16, 1024, DIM)
        H = MLP_RATIO * C
        s_in = 1.0 / np.sqrt(C)
        s_h = 1.0 / np.sqrt(H)
        return {'x': jax.random.normal(ks[0], (B, N, C), dtype=jnp.float32), 'Wg': jax.random.normal(ks[1], (C, NUM_EXPERTS), dtype=jnp.float32) * s_in, 'W1': jax.random.normal(ks[2], (NUM_EXPERTS, C, H), dtype=jnp.float32) * s_in, 'b1': jnp.zeros((NUM_EXPERTS, H), dtype=jnp.float32), 'W2': jax.random.normal(ks[3], (NUM_EXPERTS, H, C), dtype=jnp.float32) * s_h, 'b2': jnp.zeros((NUM_EXPERTS, C), dtype=jnp.float32)}
    _L1_ffn_all = _L1_ffn_setup()
    _L1_ffn_in = {k: v for k, v in _L1_ffn_all.items() if k in ('Wg', 'W1', 'b1', 'W2', 'b2')}
    del _L1_ffn_all
    return {'x': x, 'src': src, 'dst': dst, 'edge_weight': edge_weight, 'L0_gnn_Wd': _L0_gnn_in['Wd'], 'L0_gnn_bd': _L0_gnn_in['bd'], 'L0_gnn_Wu': _L0_gnn_in['Wu'], 'L0_gnn_bu': _L0_gnn_in['bu'], 'L0_gnn_W1': _L0_gnn_in['W1'], 'L0_gnn_b1': _L0_gnn_in['b1'], 'L0_gnn_W2': _L0_gnn_in['W2'], 'L0_gnn_b2': _L0_gnn_in['b2'], 'L0_mix_qkv_w': _L0_mix_in['qkv_w'], 'L0_mix_proj_w': _L0_mix_in['proj_w'], 'L0_mix_proj_b': _L0_mix_in['proj_b'], 'L0_ffn_Wqk': _L0_ffn_in['Wqk'], 'L0_ffn_bqk': _L0_ffn_in['bqk'], 'L0_ffn_Wv': _L0_ffn_in['Wv'], 'L0_ffn_bv': _L0_ffn_in['bv'], 'L0_ffn_conv_w': _L0_ffn_in['conv_w'], 'L0_ffn_conv_b': _L0_ffn_in['conv_b'], 'L0_ffn_glob': _L0_ffn_in['glob'], 'L0_ffn_pos_bias': _L0_ffn_in['pos_bias'], 'L0_ffn_Wg1': _L0_ffn_in['Wg1'], 'L0_ffn_bg1': _L0_ffn_in['bg1'], 'L0_ffn_Wg2': _L0_ffn_in['Wg2'], 'L0_ffn_bg2': _L0_ffn_in['bg2'], 'L0_ffn_Wp': _L0_ffn_in['Wp'], 'L0_ffn_bp': _L0_ffn_in['bp'], 'L1_gnn_W1': _L1_gnn_in['W1'], 'L1_gnn_att_src1': _L1_gnn_in['att_src1'], 'L1_gnn_att_dst1': _L1_gnn_in['att_dst1'], 'L1_gnn_b1': _L1_gnn_in['b1'], 'L1_gnn_W2': _L1_gnn_in['W2'], 'L1_gnn_att_src2': _L1_gnn_in['att_src2'], 'L1_gnn_att_dst2': _L1_gnn_in['att_dst2'], 'L1_gnn_b2': _L1_gnn_in['b2'], 'L1_mix_Wq': _L1_mix_in['Wq'], 'L1_mix_bq': _L1_mix_in['bq'], 'L1_mix_Wk': _L1_mix_in['Wk'], 'L1_mix_bk': _L1_mix_in['bk'], 'L1_mix_Wv': _L1_mix_in['Wv'], 'L1_mix_bv': _L1_mix_in['bv'], 'L1_mix_Wo': _L1_mix_in['Wo'], 'L1_mix_bo': _L1_mix_in['bo'], 'L1_ffn_Wg': _L1_ffn_in['Wg'], 'L1_ffn_W1': _L1_ffn_in['W1'], 'L1_ffn_b1': _L1_ffn_in['b1'], 'L1_ffn_W2': _L1_ffn_in['W2'], 'L1_ffn_b2': _L1_ffn_in['b2']}

def reference(x, src, dst, edge_weight, L0_gnn_Wd, L0_gnn_bd, L0_gnn_Wu, L0_gnn_bu, L0_gnn_W1, L0_gnn_b1, L0_gnn_W2, L0_gnn_b2, L0_mix_qkv_w, L0_mix_proj_w, L0_mix_proj_b, L0_ffn_Wqk, L0_ffn_bqk, L0_ffn_Wv, L0_ffn_bv, L0_ffn_conv_w, L0_ffn_conv_b, L0_ffn_glob, L0_ffn_pos_bias, L0_ffn_Wg1, L0_ffn_bg1, L0_ffn_Wg2, L0_ffn_bg2, L0_ffn_Wp, L0_ffn_bp, L1_gnn_W1, L1_gnn_att_src1, L1_gnn_att_dst1, L1_gnn_b1, L1_gnn_W2, L1_gnn_att_src2, L1_gnn_att_dst2, L1_gnn_b2, L1_mix_Wq, L1_mix_bq, L1_mix_Wk, L1_mix_bk, L1_mix_Wv, L1_mix_bv, L1_mix_Wo, L1_mix_bo, L1_ffn_Wg, L1_ffn_W1, L1_ffn_b1, L1_ffn_W2, L1_ffn_b2):
    import jax
    import jax.numpy as jnp

    def _L0_gnn_ref(x, edge_index, edge_weight, Wd, bd, Wu, bu, W1, b1, W2, b2):
        import jax, jax.numpy as jnp
        import numpy as np
        N = 6250
        E = 62500
        D = 768
        H = 256
        R = 32

        def _gcn(x, W, b, row, col, ew):
            x = x @ W
            n = x.shape[0]
            deg = jax.ops.segment_sum(ew, col, num_segments=n) + 1.0
            dinv = jax.lax.rsqrt(deg)
            norm = dinv[row] * ew * dinv[col]
            agg = jax.ops.segment_sum(norm[:, None] * x[row], col, num_segments=n)
            return agg + (dinv * dinv)[:, None] * x + b
        h = jax.nn.relu(x @ Wd + bd) @ Wu + bu + x
        row, col = (edge_index[0], edge_index[1])
        h = jax.nn.relu(_gcn(h, W1, b1, row, col, edge_weight))
        h = _gcn(h, W2, b2, row, col, edge_weight)
        return h

    def _L0_mix_ref(x, qkv_w, proj_w, proj_b):
        import jax, jax.numpy as jnp
        import numpy as np
        DIM = 768
        NUM_HEADS = 12
        HEAD_DIM = DIM // NUM_HEADS
        ORDER = 2
        SCALE = HEAD_DIM ** (-0.5)
        B, N, C = x.shape
        qkv = jnp.einsum('bnc,oc->bno', x, qkv_w)
        qkv = qkv.reshape(B, N, 3, NUM_HEADS, HEAD_DIM).transpose(2, 0, 3, 1, 4)
        q, k, v = (qkv[0], qkv[1], qkv[2])
        q = q * SCALE
        qk = jnp.einsum('bhnd,bhmd->bhnm', q, k)
        attn = jnp.ones_like(qk)
        x_power = jnp.ones_like(qk)
        factorial = 1.0
        for i in range(1, ORDER + 1):
            if i > 1:
                factorial *= i
            attn = attn + x_power / factorial
            x_power = x_power * qk
        attn = jax.nn.relu(attn)
        attn = attn / jnp.sum(attn, axis=-1, keepdims=True)
        out = jnp.einsum('bhnm,bhmd->bhnd', attn, v)
        out = out.transpose(0, 2, 1, 3).reshape(B, N, C)
        out = jnp.einsum('bnc,oc->bno', out, proj_w) + proj_b
        return out

    def _L0_ffn_ref(x, Wqk, bqk, Wv, bv, conv_w, conv_b, glob, pos_bias, Wg1, bg1, Wg2, bg2, Wp, bp):
        import jax, jax.numpy as jnp
        import numpy as np
        import math
        B, T, C = (8, 256, 768)
        E = 3
        HD = C // E
        TOPK = 2
        NGLOB = 4

        def _masked_softmax(att, mask):
            att = jnp.where(mask, -jnp.inf, att)
            return jax.nn.softmax(att, axis=-1)
        Bx, Tx, Cx = x.shape
        scale = 1.0 / math.sqrt(HD)
        gate = jax.nn.softmax(jax.nn.relu(x @ Wg1 + bg1) @ Wg2 + bg2, axis=-1)
        top_w, top_i = jax.lax.top_k(gate, TOPK)
        top_w = jax.nn.softmax(top_w, axis=-1)
        qk = x @ Wqk + bqk
        q, k = (qk[..., :Cx], qk[..., Cx:])
        q = q.reshape(Bx, Tx, E, HD)
        k = k.reshape(Bx, Tx, E, HD)
        rows = jnp.arange(Tx)[:, None]
        ys = []
        for e in range(E):
            qe = q[:, :, e]
            ke = k[:, :, e]
            ve = x @ Wv[e] + bv[e]
            if e == 0:
                qc = jnp.transpose(qe, (0, 2, 1))
                qc = jax.lax.conv_general_dilated(qc, conv_w, window_strides=(1,), padding=((1, 1),), feature_group_count=HD, dimension_numbers=('NCH', 'OIH', 'NCH'))
                qe = jnp.transpose(qc + conv_b[None, :, None], (0, 2, 1))
            elif e == 1:
                gb = jnp.broadcast_to(glob[None], (Bx, NGLOB, HD))
                ke = jnp.concatenate([ke, gb], axis=1)
                ve = jnp.concatenate([ve, gb], axis=1)
            att = jnp.einsum('btd,bsd->bts', qe, ke) * scale
            if e == 2 and Tx <= 64:
                att = att + pos_bias[:Tx, :Tx][None]
            S = att.shape[-1]
            mask = jnp.arange(S)[None, :] > rows
            att = _masked_softmax(att, mask[None])
            ys.append(jnp.einsum('bts,bsd->btd', att, ve))
        ys = jnp.stack(ys, axis=2)
        w_e = jnp.sum(jax.nn.one_hot(top_i, E, dtype=x.dtype) * top_w[..., None], axis=-2)
        combined = (ys * w_e[..., None]).reshape(Bx, Tx, Cx)
        return combined @ Wp + bp

    def _L1_gnn_ref(x, edge_index, W1, att_src1, att_dst1, b1, W2, att_src2, att_dst2, b2):
        import jax, jax.numpy as jnp
        import numpy as np
        N_NODES = 1250
        N_EDGES = 12500
        DIM = 768
        NEG_SLOPE = 0.2

        def gat_conv(x, src, dst, W, att_src, att_dst, bias, num_nodes):
            h = x @ W
            a_s = h @ att_src
            a_d = h @ att_dst
            e = jax.nn.leaky_relu(a_s[src] + a_d[dst], NEG_SLOPE)
            m = jax.ops.segment_max(e, dst, num_segments=num_nodes)
            e = jnp.exp(e - m[dst])
            denom = jax.ops.segment_sum(e, dst, num_segments=num_nodes)
            alpha = e / denom[dst]
            msg = alpha[:, None] * h[src]
            out = jax.ops.segment_sum(msg, dst, num_segments=num_nodes)
            return out + bias
        n = x.shape[0]
        loops = jnp.arange(n, dtype=edge_index.dtype)
        src = jnp.concatenate([edge_index[0], loops])
        dst = jnp.concatenate([edge_index[1], loops])
        h = gat_conv(x, src, dst, W1, att_src1, att_dst1, b1, n)
        h = jax.nn.relu(h)
        out = gat_conv(h, src, dst, W2, att_src2, att_dst2, b2, n)
        return out

    def _L1_mix_ref(x, Wq, bq, Wk, bk, Wv, bv, Wo, bo):
        import jax, jax.numpy as jnp
        import numpy as np
        FEATS = 768
        HEAD = 12

        def _phi(t):
            return jax.nn.elu(t) + 1.0
        b, n, f = x.shape
        h = HEAD
        d = f // h

        def heads(t):
            return t.reshape(b, n, h, d).transpose(0, 2, 1, 3)
        q = _phi(heads(x @ Wq + bq))
        k = _phi(heads(x @ Wk + bk))
        v = heads(x @ Wv + bv)
        kv = jnp.einsum('bhnd,bhne->bhde', k, v)
        ksum = k.sum(axis=2)
        z = 1.0 / jnp.einsum('bhld,bhd->bhl', q, ksum)
        num = jnp.einsum('bhld,bhde->bhle', q, kv)
        normed = num * z[..., None]
        out = normed.transpose(0, 2, 1, 3).reshape(b, n, f)
        return out @ Wo + bo

    def _L1_ffn_ref(x, Wg, W1, b1, W2, b2):
        import jax, jax.numpy as jnp
        import numpy as np
        DIM = 768
        NUM_EXPERTS = 8
        TOP_K = 2
        MLP_RATIO = 4
        CAPACITY_RATIO = 1.25
        B, N, C = x.shape
        E = W1.shape[0]
        K = TOP_K
        T = B * N
        cap = int(CAPACITY_RATIO * T * K / E)
        xf = x.reshape(T, C)
        logits = xf @ Wg
        topv, topi = jax.lax.top_k(logits, K)
        w = jax.nn.softmax(topv, axis=-1)
        priority = w[:, 0]
        order = jnp.argsort(-priority)
        e_ids = topi[order].reshape(T * K)
        w_ord = w[order].reshape(T * K)
        tok_rep = jnp.repeat(order, K)
        oh = jax.nn.one_hot(e_ids, E, dtype=jnp.int32)
        pos = (jnp.cumsum(oh, axis=0) * oh).sum(-1) - 1
        keep = pos < cap
        slot = jnp.where(keep, e_ids * cap + pos, E * cap)
        buf = jnp.zeros((E * cap + 1, C), xf.dtype).at[slot].set(xf[tok_rep])
        buf_e = buf[:E * cap].reshape(E, cap, C)
        h = jax.nn.gelu(jnp.einsum('ecd,edh->ech', buf_e, W1) + b1[:, None, :], approximate=False)
        out = jnp.einsum('ech,ehd->ecd', h, W2) + b2[:, None, :]
        out_flat = jnp.concatenate([out.reshape(E * cap, C), jnp.zeros((1, C), xf.dtype)], axis=0)
        y_assign = out_flat[slot] * (w_ord * keep.astype(xf.dtype))[:, None]
        y = jnp.zeros((T, C), xf.dtype).at[tok_rep].add(y_assign)
        return y.reshape(B, N, C)
    edge_index = jnp.stack([src, dst])
    xn = _layernorm(x, axis=-1)
    x = x + _L0_gnn_ref(xn, edge_index, edge_weight, L0_gnn_Wd, L0_gnn_bd, L0_gnn_Wu, L0_gnn_bu, L0_gnn_W1, L0_gnn_b1, L0_gnn_W2, L0_gnn_b2) + _L0_mix_ref(xn[None], L0_mix_qkv_w, L0_mix_proj_w, L0_mix_proj_b)[0]
    x = x + _L0_ffn_ref(_layernorm(x, axis=-1)[None], L0_ffn_Wqk, L0_ffn_bqk, L0_ffn_Wv, L0_ffn_bv, L0_ffn_conv_w, L0_ffn_conv_b, L0_ffn_glob, L0_ffn_pos_bias, L0_ffn_Wg1, L0_ffn_bg1, L0_ffn_Wg2, L0_ffn_bg2, L0_ffn_Wp, L0_ffn_bp)[0]
    xn = _layernorm(x, axis=-1)
    x = x + _L1_gnn_ref(xn, edge_index, L1_gnn_W1, L1_gnn_att_src1, L1_gnn_att_dst1, L1_gnn_b1, L1_gnn_W2, L1_gnn_att_src2, L1_gnn_att_dst2, L1_gnn_b2) + _L1_mix_ref(xn[None], L1_mix_Wq, L1_mix_bq, L1_mix_Wk, L1_mix_bk, L1_mix_Wv, L1_mix_bv, L1_mix_Wo, L1_mix_bo)[0]
    x = x + _L1_ffn_ref(_layernorm(x, axis=-1)[None], L1_ffn_Wg, L1_ffn_W1, L1_ffn_b1, L1_ffn_W2, L1_ffn_b2)[0]
    return x

_drawn_inputs = setup_inputs


def setup_inputs(seed=0):
    import zlib

    import numpy as np

    out = dict(_drawn_inputs(seed))
    spreads = {'L0_gnn_bd': (0.0, 0.1),
     'L0_gnn_bu': (0.0, 0.1),
     'L0_gnn_b1': (0.0, 0.1),
     'L0_gnn_b2': (0.0, 0.1),
     'L0_ffn_bqk': (0.0, 0.412),
     'L0_ffn_bv': (0.0, 0.1),
     'L0_ffn_conv_b': (0.0, 0.8),
     'L0_ffn_pos_bias': (0.0, 0.1),
     'L0_ffn_bg1': (0.0, 1.221),
     'L0_ffn_bg2': (0.0, 0.1),
     'L0_ffn_bp': (0.0, 0.1),
     'L1_gnn_b1': (0.0, 0.1),
     'L1_gnn_b2': (0.0, 0.1),
     'L1_ffn_b1': (0.0, 0.1),
     'L1_ffn_b2': (0.0, 0.1)}
    factors = {'L0_ffn_Wqk': 3.237,
     'L0_ffn_conv_w': 8.0,
     'L1_mix_bq': 200.0,
     'L1_mix_bk': 200.0,
     'L1_gnn_att_dst2': 2.839,
     'L1_mix_Wq': 4.388,
     'L1_mix_Wk': 4.312}
    for name, (base, spread) in spreads.items():
        noise = np.random.default_rng([zlib.crc32(name.encode()), seed]).standard_normal(out[name].shape)
        drawn = base * np.exp(spread * noise) if base else spread * noise
        out[name] = jnp.asarray(drawn.astype(out[name].dtype))
    for name, factor in factors.items():
        out[name] = (out[name] * factor).astype(out[name].dtype)
    return out
```

```python
from contextlib import ExitStack

import numpy as np

import concourse.bass as bass
from concourse import mybir

F32 = mybir.dt.float32
BF16 = mybir.dt.bfloat16
I32 = mybir.dt.int32
ALU = mybir.AluOpType
ACT = mybir.ActivationFunctionType
AX = mybir.AxisListType.X

N, D = 1250, 768
P = 125
T = N // P
KC = D // 128
HALF = D // 2
CH = [(0, 417), (417, 417), (834, 416)]
EDGES = 20000
GPC = 14
CHUNKS = 12
GROUPS = GPC * CHUNKS
PADDED = GROUPS * P
CW = GPC * P
TRASH = N * N + P
MAIN = N * N + 500
TABLE = MAIN + 16
NEG = -1e30
EPS = 1e-5
ONE = 1
H0 = 12
PAIRS = H0 // 2
HD = D // H0
E0 = 3
HE = D // E0
E1 = 8
HID = 4 * D
HB = HID // 128
CAP = int(1.25 * N * 2 / E1)
SUB = 78
NS = CAP // SUB
SLOTS = E1 * CAP
assert N == T * P and PADDED >= EDGES and NS * SUB == CAP and MAIN % P == 0


class Chain:

    def __init__(self, eng, sem, base=0):
        self.eng, self.sem, self.base, self.n = eng, sem, base, 0

    def __call__(self, ins):
        self.n += 1
        ins.then_inc(self.sem, 1)
        self.eng.wait_ge(self.sem, self.base + self.n)


SEMAPHORES = set()


class Scope:

    def __init__(self, nc, ctx, stage):
        self.nc, self.ctx, self.stage = nc, ctx, stage

    def sb(self, name, shape, dt=F32):
        return self.ctx.enter_context(self.nc.sbuf_tensor(f"{self.stage}_{name}", shape, dt))

    def ps(self, name, shape, dt=F32):
        return self.ctx.enter_context(self.nc.psum_tensor(f"{self.stage}_{name}", shape, dt))

    def sem(self, name):
        sem = self.ctx.enter_context(self.nc.semaphore(f"{self.stage}_{name}"))
        SEMAPHORES.add(sem.num)
        return sem


def bcast_rows(ap, p, n):
    return bass.AP(ap.tensor, ap.offset, [[0, p], [1, n]])


def stage_start(nc, g):
    with ExitStack() as ctx:
        s = Scope(nc, ctx, "start")
        zeros = s.sb("zeros", [P, MAIN // P // 4])
        made, chain, x_in, zeroed = s.sem("made"), s.sem("chain"), s.sem("x_in"), s.sem("zeroed")
        block = ctx.enter_context(nc.Block())

        @block.vector
        def _(dve):
            nc.vector.memset(zeros[:], 0.0).then_inc(made, 1)
            nc.vector.memset(g.zero_tail[:], 0.0)
            nc.vector.memset(g.ones[:], 1.0)
            nc.vector.memset(g.two[:], 2.0)
            nc.vector.memset(g.eps[:], EPS)
            nc.vector.memset(g.halves[:], 0.0).then_inc(made, 1)
            dve.wait_ge(made, 2)
            nc.vector.memset(g.halves[0:64, 0:64], 1.0)
            nc.vector.memset(g.halves[64:128, 64:128], 1.0)
            for before, E in ((g.before3, E0), (g.before8, E1)):
                for e in range(E):
                    if e:
                        nc.vector.memset(before[:, e * E:e * E + e], 1.0)
                    nc.vector.memset(before[:, e * E + e:(e + 1) * E], 0.0)

        @block.gpsimd
        def _(pool):
            step = Chain(pool, chain)
            step(nc.gpsimd.memset(g.ident[:], 0.0))
            nc.gpsimd.affine_select(out=g.ident[:], in_=g.ident[:], compare_op=ALU.not_equal, fill=1.0, base=0,
                                    pattern=[[-1, 128]], channel_multiplier=1)
            step(nc.gpsimd.memset(g.lower[:], 1.0))
            nc.gpsimd.affine_select(out=g.lower[:], in_=g.lower[:], compare_op=ALU.is_gt, fill=0.0, base=0,
                                    pattern=[[-1, P]], channel_multiplier=1)
            step(nc.gpsimd.memset(g.causal[:], 0.0))
            nc.gpsimd.affine_select(out=g.causal[:], in_=g.causal[:], compare_op=ALU.is_ge, fill=NEG, base=0,
                                    pattern=[[-1, P]], channel_multiplier=1)

        @block.sync
        def _(sp):
            sp.dma_start(g.X[:], g.x.rearrange("(t p) d -> p t d", p=P)).then_inc(x_in, 16)
            sp.wait_ge(made, 1)
            for table in (g.ew_table, g.cnt_table):
                v = table[0:MAIN].rearrange("(q p) o -> q (p o)", q=4).rearrange("q (p f) -> q p f", p=P)
                for q in range(4):
                    sp.dma_start(v[q], zeros[:]).then_inc(zeroed, 16)
            sp.wait_ge(x_in, 16)
            sp.wait_ge(zeroed, 8 * 16)


def stage_norm(nc, g, name, keep=None):
    with ExitStack() as ctx:
        s = Scope(nc, ctx, name)
        xn = s.sb("xn", [P, T, D])
        stats = s.sb("stats", [P, T, 2, 6])
        mv = s.sb("mv", [P, T, 2])
        std = s.sb("std", [P, T])
        rstd = s.sb("rstd", [P, T])
        flip = [s.ps(f"flip{i}", [128, 512]) for i in range(4)]
        stats_in, var_in, std_in, rstd_in = s.sem("stats"), s.sem("var"), s.sem("std"), s.sem("rstd")
        normed, flipped, moved, kept = s.sem("normed"), s.sem("flipped"), s.sem("moved"), s.sem("kept")
        block = ctx.enter_context(nc.Block())

        @block.vector
        def _(dve):
            for t in range(T):
                for h in range(2):
                    last = nc.vector.bn_stats(stats[:, t, h, :], g.X[:, t, h * HALF:(h + 1) * HALF])
            last.then_inc(stats_in, 1)
            dve.wait_ge(stats_in, 1)
            for t in range(T):
                last = nc.vector.bn_aggr(mv[:, t, :], stats[:, t, :, :])
            last.then_inc(var_in, 1)
            dve.wait_ge(std_in, 1)
            nc.vector.reciprocal(rstd[:], std[:]).then_inc(rstd_in, 1)
            dve.wait_ge(rstd_in, 1)
            for t in range(T):
                nc.vector.tensor_scalar(xn[:, t, :], g.X[:, t, :], mv[:, t, 0:1], rstd[:, t:t + 1],
                                        ALU.subtract, ALU.mult).then_inc(normed, 1)

        @block.scalar
        def _(act):
            act.wait_ge(var_in, 1)
            nc.scalar.activation(std[:], mv[:, :, 1], ACT.Sqrt, bias=g.eps[0:P, :]).then_inc(std_in, 1)
            for n in range(2 * T):
                t, h = divmod(n, 2)
                act.wait_ge(flipped, n + 1)
                nc.scalar.activation(g.XT[:, 3 * h:3 * h + 3, t * P:(t + 1) * P],
                                     flip[n % 4][:, 0:3 * P].rearrange("p (k c) -> p k c", k=3),
                                     ACT.Copy).then_inc(moved, 1)

        @block.tensor
        def _(pe):
            for n in range(2 * T):
                t, h = divmod(n, 2)
                if h == 0:
                    pe.wait_ge(normed, t + 1)
                if n >= 4:
                    pe.wait_ge(moved, n - 3)
                for k in range(3):
                    f = (3 * h + k) * 128
                    last = nc.tensor.transpose(flip[n % 4][:, k * P:(k + 1) * P], xn[:, t, f:f + 128],
                                               g.ident[0:P, 0:P])
                last.then_inc(flipped, 1)

        @block.sync
        def _(sp):
            if keep is not None:
                sp.wait_ge(normed, T)
                sp.dma_start(keep.rearrange("(t p) d -> p t d", p=P), xn[:]).then_inc(kept, 16)
                sp.wait_ge(kept, 16)


def stage_poly_mix(nc, g):
    NSCORE = 2 * 3 * T
    NEV = 6 + T + NSCORE
    with ExitStack() as ctx:
        s = Scope(nc, ctx, "mix0")
        w = s.sb("w", [128, KC, 384])
        qT, kT = s.sb("qT", [128, N]), s.sb("kT", [128, N])
        v1 = s.sb("v1", [P, T, 2, 128])
        attn = s.sb("attn", [P, 4, 417])
        rden = s.sb("rden", [128, 2, 417])
        key_cols, keys, ew_cols = s.sb("key_cols", [P, 2, GROUPS], I32), s.sb("keys", [P, GROUPS]), None
        rows_i, rows_w = s.sb("rows_i", [P, 2, CW], I32), s.sb("rows_w", [P, CW])
        key_row, same, part = s.sb("key_row", [P, CW]), s.sb("same", [P, CW]), s.sb("part", [P, CW])
        val_w, val_c = s.sb("val_w", [P, 2, GPC]), s.sb("val_c", [P, 2, GPC])
        dup, away, idxf = s.sb("dup", [P, GPC]), s.sb("away", [P, GPC]), s.sb("idxf", [P, GPC])
        idx = s.sb("idx", [P, 2, GPC], I32)
        trash_i, trash = s.sb("trash_i", [P, 1], I32), s.sb("trash", [P, 1])
        ring = [s.ps(f"ring{i}", [128, 512]) for i in range(4)]
        out = [s.ps(f"out{i}", [128, 512]) for i in range(2)]
        w_in, made, taken, weighed, normed = (s.sem(x) for x in ("w_in", "made", "taken", "weighed", "normed"))
        cols_in, rows_in, rows_used, ready, chain = (s.sem(x) for x in ("cols_in", "rows_in", "rows_used", "ready", "chain"))
        trash_in, ones_in, landed = (s.sem(x) for x in ("trash_in", "ones_in", "landed"))
        put_w, put_c = g.put_w, g.put_c
        block = ctx.enter_context(nc.Block())

        @block.sync
        def _(sp):
            sp.dma_start(w[:], g.mix0_w[0]).then_inc(w_in, 16)
            sp.dma_start(key_cols[:], g.edge_cols).then_inc(cols_in, 16)

            def load_rows(c):
                for n in range(2):
                    sp.dma_start(rows_i[:, n, :], bass.AP(g.edge_rows.tensor, c * CW + n * PADDED, [[0, P], [1, CW]])
                                 ).then_inc(rows_in, 16)
                sp.dma_start(rows_w[:], bass.AP(g.edge_w.tensor, c * CW, [[0, P], [1, CW]])).then_inc(rows_in, 16)

            load_rows(0)
            with sp.Fori(0, PAIRS - 1) as i:
                sp.wait_ge(rows_used, i * 2 + 1)
                load_rows(i * 2 + 1)
                sp.wait_ge(made, i * NEV + 6 + T)
                sp.dma_start(w[:], g.mix0_w[bass.ds(i + 1, 1)].rearrange("o p k f -> (o p) k f")).then_inc(w_in, 16)
                sp.wait_ge(rows_used, i * 2 + 2)
                load_rows(i * 2 + 2)
            sp.wait_ge(rows_used, CHUNKS - 1)
            load_rows(CHUNKS - 1)

        @block.tensor
        def _(pe):
            for count in (weighed,):
                pe.sem_inc(count, 1)
            pe.wait_ge(ones_in, 1)
            with pe.Fori(0, PAIRS) as i:
                pe.wait_ge(w_in, i * 16 + 16)

                def room(n):
                    pe.wait_ge(taken, ONE + i * NEV + max(n - 3, 0))

                n = 0
                for m in range(2):
                    for c0, cn in CH:
                        room(n)
                        for k in range(KC):
                            last = nc.tensor.matmul(ring[n % 4][:, 0:cn], w[:, k, m * 128:(m + 1) * 128],
                                                    g.XT[:, k, c0:c0 + cn], start=(k == 0), stop=(k == KC - 1))
                        last.then_inc(made, 1)
                        n += 1
                for t in range(T):
                    room(n)
                    for k in range(KC):
                        last = nc.tensor.matmul(ring[n % 4][0:P, 0:128], g.XT[:, k, t * P:(t + 1) * P],
                                                w[:, k, 256:384], start=(k == 0), stop=(k == KC - 1))
                    last.then_inc(made, 1)
                    n += 1

                def score(m):
                    h, c, j = m // (3 * T), m // T % 3, m % T
                    c0, cn = CH[c]
                    if m == 0:
                        pe.wait_ge(taken, ONE + i * NEV + 6 + T)
                    else:
                        room(6 + T + m)
                    nc.tensor.matmul(ring[(6 + T + m) % 4][0:P, 0:cn], kT[64 * h:64 * h + 64, j * P:(j + 1) * P],
                                     qT[64 * h:64 * h + 64, c0:c0 + cn], start=True, stop=True).then_inc(made, 1)

                def weigh(m):
                    h, c, j = m // (3 * T), m // T % 3, m % T
                    cn = CH[c][1]
                    if j == 0:
                        pe.wait_ge(normed, ONE + i * 6 + max(m // T - 1, 0))
                    pe.wait_ge(taken, ONE + i * NEV + 6 + T + m + 1)
                    nc.tensor.matmul(out[m // T % 2][:, 0:cn], v1[:, j, h, :], attn[:, m % 4, 0:cn],
                                     start=(j == 0), stop=(j == T - 1)).then_inc(weighed, 1)

                for m in range(NSCORE + 2):
                    if m < NSCORE:
                        score(m)
                    if m >= 2:
                        weigh(m - 2)

        @block.scalar
        def _(act):
            for count in (taken,):
                act.sem_inc(count, 1)
            with act.Fori(0, PAIRS) as i:
                n = 0
                for m in range(2):
                    for c0, cn in CH:
                        act.wait_ge(made, i * NEV + n + 1)
                        nc.scalar.activation((qT, kT)[m][:, c0:c0 + cn], ring[n % 4][:, 0:cn], ACT.Copy,
                                             scale=(HD ** -0.5 / 2, 1.0)[m]).then_inc(taken, 1)
                        n += 1
                for t in range(T):
                    act.wait_ge(made, i * NEV + n + 1)
                    nc.scalar.activation(v1[:, t, 0, 0:64], ring[n % 4][0:P, 0:64], ACT.Copy)
                    nc.scalar.activation(v1[:, t, 1, 64:128], ring[n % 4][0:P, 64:128], ACT.Copy).then_inc(taken, 1)
                    n += 1
                for m in range(NSCORE):
                    cn = CH[m // T % 3][1]
                    act.wait_ge(made, i * NEV + n + 1)
                    act.wait_ge(weighed, ONE + i * NSCORE + max(m - 3, 0))
                    nc.scalar.activation(attn[:, m % 4, 0:cn], ring[n % 4][0:P, 0:cn], ACT.Relu,
                                         bias=g.two[0:P, :]).then_inc(taken, 1)
                    n += 1

        @block.vector
        def _(dve):
            for count in (normed,):
                dve.sem_inc(count, 1)
            nc.vector.memset(v1[:, :, 0, 64:128], 1.0)
            nc.vector.memset(v1[:, :, 1, 0:64], 1.0).then_inc(ones_in, 1)
            dve.wait_ge(cols_in, 16)
            dve.wait_ge(trash_in, 1)
            first = Chain(dve, chain)
            nc.vector.tensor_copy(trash[:], trash_i[:])
            first(nc.vector.scalar_tensor_tensor(keys[:], key_cols[:, 0, :], float(N), key_cols[:, 1, :],
                                                 ALU.mult, ALU.add))
            LINKS = 2 * 7 + 6
            with dve.Fori(0, PAIRS) as i:
                step = Chain(dve, chain, 1 + i * LINKS)

                def chunk(b):
                    cols = keys[:, bass.ds((i * 2 + b) * GPC, GPC)]
                    rows = lambda a: a[:].rearrange("p (g e) -> p g e", g=GPC)
                    dve.wait_ge(rows_in, i * 96 + 48 * (b + 1))
                    step(nc.vector.scalar_tensor_tensor(key_row[:], rows_i[:, 0, :], float(N), rows_i[:, 1, :],
                                                        ALU.mult, ALU.add))
                    step(nc.vector.tensor_tensor(rows(same), rows(key_row),
                                                 cols.unsqueeze(2).broadcast_to([P, GPC, P]), ALU.is_equal))
                    step(nc.vector.tensor_tensor(part[:], same[:], rows_w[:], ALU.mult))
                    dve.wait_ge(put_w, 16 + i * 2 * GPC * 16)
                    dve.wait_ge(put_c, 16 + i * 2 * GPC * 16)
                    nc.vector.tensor_reduce(val_w[:, b, :], rows(part), AX, ALU.add).then_inc(rows_used, 1)
                    step(nc.vector.tensor_reduce(val_c[:, b, :], rows(same), AX, ALU.add))
                    step(nc.vector.tensor_tensor(rows(part), rows(same),
                                                 g.lower[:].unsqueeze(1).broadcast_to([P, GPC, P]), ALU.mult))
                    nc.vector.tensor_scalar(away[:], cols, trash[:, 0:1], -1.0, ALU.subtract, ALU.mult)
                    step(nc.vector.tensor_reduce(dup[:], rows(part), AX, ALU.max))
                    step(nc.vector.tensor_tensor(away[:], away[:], dup[:], ALU.mult))
                    nc.vector.tensor_tensor(idx[:, b, :], away[:], cols, ALU.add).then_inc(ready, 1)

                def norm(hc):
                    h, (c0, cn) = hc // 3, CH[hc % 3]
                    num, den = slice(64 * h, 64 * h + 64), slice(64 - 64 * h, 128 - 64 * h)
                    dve.wait_ge(weighed, ONE + i * NSCORE + T * (hc + 1))
                    step(nc.vector.reciprocal(rden[num, hc % 2, 0:cn], out[hc % 2][den, 0:cn]))
                    nc.vector.tensor_tensor(g.OT[num, bass.ds(i, 1), c0:c0 + cn].rearrange("p o c -> p (o c)"),
                                            out[hc % 2][num, 0:cn], rden[num, hc % 2, 0:cn], ALU.mult).then_inc(normed, 1)

                chunk(0)
                norm(0)
                norm(1)
                chunk(1)
                for hc in range(2, 6):
                    norm(hc)
                assert step.n == LINKS, step.n

        @block.gpsimd
        def _(pool):
            nc.gpsimd.iota(trash_i[:], pattern=[[0, 1]], base=TRASH, channel_multiplier=1).then_inc(trash_in, 1)
            pool.dma_start(g.ew_table[MAIN:TABLE].rearrange("(a n) o -> a (n o)", a=1), g.zero_tail[:]).then_inc(put_w, 16)
            pool.dma_start(g.cnt_table[MAIN:TABLE].rearrange("(a n) o -> a (n o)", a=1), g.zero_tail[:]).then_inc(put_c, 16)
            with pool.Fori(0, PAIRS) as i:
                for b in range(2):
                    pool.wait_ge(ready, i * 2 + b + 1)
                    for n in range(GPC):
                        done = 16 + (i * 2 * GPC + b * GPC + n) * 16
                        cell = bass.IndirectOffsetOnAxis(ap=idx[:, b, n:n + 1], axis=0)
                        for table, val, put in ((g.ew_table, val_w, put_w), (g.cnt_table, val_c, put_c)):
                            pool.wait_ge(put, done)
                            pool.sem_inc(landed, 1)
                            pool.indirect_dma_start(out=table, out_offset=cell, in_=val[:, b, n:n + 1], in_offset=None,
                                                    compute_op=ALU.add).then_inc(put, 16)
            pool.wait_ge(put_w, 16 + GROUPS * 16)
            pool.wait_ge(put_c, 16 + GROUPS * 16)


def stage_clear(nc, g):
    done = sorted(SEMAPHORES)
    with ExitStack() as ctx:
        block = ctx.enter_context(nc.Block())

        @block.gpsimd
        def _(pool):
            pool.sem_clear(range(done[0], done[-1] + 1))


def stage_tok_linear(nc, g, name, src, w_dram, bias):
    with ExitStack() as ctx:
        s = Scope(nc, ctx, name)
        w, b = s.sb("w", [128, KC, D]), s.sb("b", [P, D])
        acc = [s.ps(f"acc{i}", [P, 512]) for i in range(4)]
        w_in, b_in, biased, made, added = (s.sem(x) for x in ("w_in", "b_in", "biased", "made", "added"))
        block = ctx.enter_context(nc.Block())

        @block.sync
        def _(sp):
            sp.dma_start(w[:], w_dram.rearrange("(k p) m -> p k m", p=128)).then_inc(w_in, 16)
            sp.dma_start(b[:], bcast_rows(bias, P, D)).then_inc(b_in, 16)

        @block.tensor
        def _(pe):
            pe.wait_ge(w_in, 16)
            for n in range(2 * T):
                t, h = divmod(n, 2)
                if n >= 4:
                    pe.wait_ge(added, n - 3)
                for k in range(KC):
                    last = nc.tensor.matmul(acc[n % 4][:, 0:HALF], src[:, k, t * P:(t + 1) * P],
                                            w[:, k, h * HALF:(h + 1) * HALF], start=(k == 0), stop=(k == KC - 1))
                last.then_inc(made, 1)

        @block.vector
        def _(dve):
            dve.wait_ge(b_in, 16)
            nc.vector.tensor_tensor(g.X[:], g.X[:], b[:].unsqueeze(1).broadcast_to([P, T, D]), ALU.add).then_inc(biased, 1)
            dve.wait_ge(biased, 1)
            for n in range(2 * T):
                t, h = divmod(n, 2)
                dve.wait_ge(made, n + 1)
                x = g.X[:, t, h * HALF:(h + 1) * HALF]
                nc.vector.tensor_tensor(x, acc[n % 4][:, 0:HALF], x, ALU.add).then_inc(added, 1)


def stage_gcn(nc, g):
    H = 256
    R = 24
    with ExitStack() as ctx:
        s = Scope(nc, ctx, "gcn")
        A = s.sb("A", [P, T, N])
        wd, wu, w1, w2 = s.sb("wd", [128, KC, R]), s.sb("wu", [R, D]), s.sb("w1", [128, KC, H]), s.sb("w2", [128, 2, D])
        bd, bu, b1, b2 = s.sb("bd", [R, 1]), s.sb("bu", [128, KC]), s.sb("b1", [P, H]), s.sb("b2", [P, D])
        down = s.sb("down", [R, N])
        h1, h2, sumT = s.sb("h1", [P, T, H]), s.sb("h2", [P, T, H]), s.sb("sumT", [128, 2, N])
        act_in = s.sb("act_in", [P, 2, H])
        deg, std, dinv = s.sb("deg", [P, N]), s.sb("std", [P, T]), s.sb("dinv", [P, T])
        uT = g.OT
        ring = [s.ps(f"ring{i}", [128, 512]) for i in range(4)]
        deg_ps = s.ps("deg_ps", [P, 512])
        A_in, wd_in, wu_in, w1_in, w2_in, b_in = (s.sem(x) for x in ("A_in", "wd_in", "wu_in", "w1_in", "w2_in", "b_in"))
        made, taken, h1_in, h2_in = (s.sem(x) for x in ("made", "taken", "h1_in", "h2_in"))
        chain, deg_in, degs, std_in, dinv_in, biased = (s.sem(x) for x in ("chain", "deg_in", "degs", "std_in", "dinv_in", "biased"))
        block = ctx.enter_context(nc.Block())
        D0 = 3
        U0 = D0 + 3 * KC
        H1 = U0 + T
        H2 = H1 + T
        S0 = H2 + 6

        @block.sync
        def _(sp):
            sp.dma_start(wd[:], g.gcn_wd.rearrange("(k p) m -> p k m", p=128)).then_inc(wd_in, 16)
            sp.dma_start(bd[:], g.gcn_bd).then_inc(b_in, 16)
            sp.dma_start(wu[:], g.gcn_wu).then_inc(wu_in, 16)
            sp.dma_start(bu[:], g.gcn_bu).then_inc(b_in, 16)
            sp.dma_start(w1[:], g.gcn_w1.rearrange("(k p) m -> p k m", p=128)).then_inc(w1_in, 16)
            sp.dma_start(b1[:], bcast_rows(g.gcn_b1, P, H)).then_inc(b_in, 16)
            sp.dma_start(b2[:], bcast_rows(g.gcn_b2, P, D)).then_inc(b_in, 16)
            sp.dma_start(A[:], g.ew_table[0:N * N].rearrange("(t p d) o -> p t (d o)", p=P, d=N)).then_inc(A_in, 16)
            sp.dma_start(w2[:], g.gcn_w2.rearrange("(k p) m -> p k m", p=128)).then_inc(w2_in, 16)

        @block.tensor
        def _(pe):
            n = [0]

            def tile(rows, cols):
                if n[0] >= 4:
                    pe.wait_ge(taken, n[0] - 3)
                return ring[n[0] % 4][0:rows, 0:cols]

            def done(ins):
                ins.then_inc(made, 1)
                n[0] += 1

            pe.wait_ge(wd_in, 16)
            for c0, cn in CH:
                o = tile(R, cn)
                for k in range(KC):
                    last = nc.tensor.matmul(o, wd[:, k, :], g.XT[:, k, c0:c0 + cn], start=(k == 0), stop=(k == KC - 1))
                done(last)
            pe.wait_ge(wu_in, 16)
            pe.wait_ge(taken, D0)
            for m in range(KC):
                for c0, cn in CH:
                    done(nc.tensor.matmul(tile(128, cn), wu[:, m * 128:(m + 1) * 128], down[:, c0:c0 + cn],
                                          start=True, stop=True))
            pe.wait_ge(w1_in, 16)
            pe.wait_ge(taken, U0)
            for t in range(T):
                o = tile(P, H)
                for k in range(KC):
                    last = nc.tensor.matmul(o, uT[:, k, t * P:(t + 1) * P], w1[:, k, :], start=(k == 0), stop=(k == KC - 1))
                done(last)
            pe.wait_ge(deg_in, 1)
            for t in range(T):
                last = nc.tensor.matmul(deg_ps[:, t:t + 1], deg[:, t * P:(t + 1) * P], g.ones[0:P, 0:1],
                                        start=True, stop=True)
            last.then_inc(degs, 1)
            pe.wait_ge(h1_in, T)
            for d in range(T):
                o = tile(P, H)
                for j in range(T):
                    last = nc.tensor.matmul(o, A[:, j, d * P:(d + 1) * P], h1[:, j, :], start=(j == 0), stop=(j == T - 1))
                done(last)
            pe.wait_ge(h2_in, T)
            for f in range(2):
                for c0, cn in CH:
                    o = tile(128, cn)
                    for j in range(T):
                        last = nc.tensor.matmul(o, h2[:, j, f * 128:(f + 1) * 128], A[:, j, c0:c0 + cn],
                                                start=(j == 0), stop=(j == T - 1))
                    done(last)
            pe.wait_ge(w2_in, 16)
            pe.wait_ge(taken, S0)
            for t in range(T):
                for h in range(2):
                    o = tile(P, HALF)
                    for k in range(2):
                        last = nc.tensor.matmul(o, sumT[:, k, t * P:(t + 1) * P], w2[:, k, h * HALF:(h + 1) * HALF],
                                                start=(k == 0), stop=(k == 1))
                    done(last)

        @block.scalar
        def _(act):
            act.wait_ge(b_in, 4 * 16)
            for n, (c0, cn) in enumerate(CH):
                act.wait_ge(made, n + 1)
                nc.scalar.activation(down[:, c0:c0 + cn], ring[n % 4][0:R, 0:cn], ACT.Relu, bias=bd[:]).then_inc(taken, 1)
            act.wait_ge(degs, 1)
            nc.scalar.activation(std[:], deg_ps[:, 0:T], ACT.Sqrt).then_inc(std_in, 1)
            for f in range(6):
                n = H2 + f
                c0, cn = CH[f % 3]
                act.wait_ge(made, n + 1)
                act.wait_ge(taken, n)
                nc.scalar.activation(sumT[:, f // 3, c0:c0 + cn], ring[n % 4][:, 0:cn], ACT.Copy).then_inc(taken, 1)

        @block.vector
        def _(dve):
            step = Chain(dve, chain)
            dve.wait_ge(taken, D0)
            dve.wait_ge(b_in, 4 * 16)
            for n in range(D0, U0):
                m, c = divmod(n - D0, 3)
                c0, cn = CH[c]
                dve.wait_ge(made, n + 1)
                nc.vector.scalar_tensor_tensor(uT[:, m, c0:c0 + cn], ring[n % 4][:, 0:cn], bu[:, m:m + 1],
                                               g.XT[:, m, c0:c0 + cn], ALU.add, ALU.add).then_inc(taken, 1)
            dve.wait_ge(A_in, 16)
            for t in range(T):
                last = nc.vector.tensor_tensor(A[:, t, t * P:(t + 1) * P], A[:, t, t * P:(t + 1) * P],
                                               g.ident[0:P, 0:P], ALU.add)
            step(last)
            nc.vector.tensor_reduce(deg[:], A[:].rearrange("p t d -> p d t"), AX, ALU.add).then_inc(deg_in, 1)
            for n in range(U0, H1):
                dve.wait_ge(made, n + 1)
                nc.vector.tensor_copy(h1[:, n - U0, :], ring[n % 4][0:P, 0:H]).then_inc(taken, 1)
            dve.wait_ge(std_in, 1)
            step(nc.vector.reciprocal(dinv[:], std[:]))
            dve.wait_ge(taken, H1)
            for t in range(T):
                nc.vector.tensor_scalar(h1[:, t, :], h1[:, t, :], dinv[:, t:t + 1], None, ALU.mult).then_inc(h1_in, 1)
            nc.vector.tensor_tensor(g.X[:], g.X[:], b2[:].unsqueeze(1).broadcast_to([P, T, D]), ALU.add).then_inc(biased, 1)
            for n in range(H1, H2):
                d = n - H1
                dve.wait_ge(made, n + 1)
                nc.vector.scalar_tensor_tensor(act_in[:, d % 2, :], ring[n % 4][0:P, 0:H], dinv[:, d:d + 1], b1[:],
                                               ALU.mult, ALU.add).then_inc(taken, 1)
                dve.wait_ge(taken, n + 1)
                nc.vector.tensor_scalar(h2[:, d, :], act_in[:, d % 2, :], 0.0, dinv[:, d:d + 1], ALU.max, ALU.mult).then_inc(h2_in, 1)
            dve.wait_ge(biased, 1)
            for n in range(S0, S0 + 2 * T):
                t, h = divmod(n - S0, 2)
                dve.wait_ge(made, n + 1)
                x = g.X[:, t, h * HALF:(h + 1) * HALF]
                nc.vector.scalar_tensor_tensor(x, ring[n % 4][0:P, 0:HALF], dinv[:, t:t + 1], x, ALU.mult, ALU.add).then_inc(taken, 1)


def stage_gate(nc, g):
    with ExitStack() as ctx:
        s = Scope(nc, ctx, "gate")
        w1, w2, b1, b2 = s.sb("w1", [128, KC, 32]), s.sb("w2", [32, E0]), s.sb("b1", [32, 1]), s.sb("b2", [P, E0])
        hT = s.sb("hT", [32, N])
        z, ez = s.sb("z", [P, T, E0]), s.sb("ez", [P, T, E0])
        col = s.sb("col", [P, T])
        cmp_, same = s.sb("cmp", [P, T, E0, E0]), s.sb("same", [P, T, E0, E0])
        ps = [s.ps(f"ps{i}", [128, 512]) for i in range(3)]
        logits = s.ps("logits", [P, 512])
        w_in, made, h_in, logits_in, chain, asked, answered = (s.sem(x) for x in ("w_in", "made", "h_in", "logits_in", "chain", "asked", "answered"))
        block = ctx.enter_context(nc.Block())

        @block.sync
        def _(sp):
            sp.dma_start(w1[:], g.gate_w1.rearrange("(k p) m -> p k m", p=128)).then_inc(w_in, 16)
            sp.dma_start(w2[:], g.gate_w2).then_inc(w_in, 16)
            sp.dma_start(b1[:], g.gate_b1).then_inc(w_in, 16)
            sp.dma_start(b2[:], bcast_rows(g.gate_b2, P, E0)).then_inc(w_in, 16)

        @block.tensor
        def _(pe):
            pe.wait_ge(w_in, 64)
            for c, (c0, cn) in enumerate(CH):
                for k in range(KC):
                    last = nc.tensor.matmul(ps[c][0:32, 0:cn], w1[:, k, :], g.XT[:, k, c0:c0 + cn],
                                            start=(k == 0), stop=(k == KC - 1))
                last.then_inc(made, 1)
            pe.wait_ge(h_in, 3)
            for t in range(T):
                last = nc.tensor.matmul(logits[:, t * E0:(t + 1) * E0], hT[:, t * P:(t + 1) * P], w2[:], start=True, stop=True)
            last.then_inc(logits_in, 1)

        @block.scalar
        def _(act):
            for c, (c0, cn) in enumerate(CH):
                act.wait_ge(made, c + 1)
                nc.scalar.activation(hT[:, c0:c0 + cn], ps[c][0:32, 0:cn], ACT.Relu, bias=b1[:]).then_inc(h_in, 1)
            for r in range(2):
                act.wait_ge(asked, r + 1)
                nc.scalar.activation(ez[:], z[:], ACT.Exp).then_inc(answered, 1)

        @block.vector
        def _(dve):
            step = Chain(dve, chain)
            per_token = col[:].unsqueeze(2).broadcast_to([P, T, E0])
            dve.wait_ge(logits_in, 1)
            step(nc.vector.tensor_tensor(z[:], logits[:, 0:T * E0].rearrange("p (t e) -> p t e", e=E0),
                                         b2[:].unsqueeze(1).broadcast_to([P, T, E0]), ALU.add))
            step(nc.vector.tensor_reduce(col[:], z[:], AX, ALU.max))
            nc.vector.tensor_tensor(z[:], z[:], per_token, ALU.subtract).then_inc(asked, 1)
            dve.wait_ge(answered, 1)
            step(nc.vector.tensor_reduce(col[:], ez[:], AX, ALU.add))
            step(nc.vector.reciprocal(col[:], col[:]))
            step(nc.vector.tensor_tensor(z[:], ez[:], per_token, ALU.mult))
            rank_of(nc, g, step, z, cmp_, same, g.gate, E0)
            step(nc.vector.tensor_scalar(g.gate[:], g.gate[:], 1.5, None, ALU.is_lt))
            step(nc.vector.tensor_reduce(col[:], z[:], AX, ALU.max))
            nc.vector.tensor_tensor(z[:], z[:], per_token, ALU.subtract).then_inc(asked, 1)
            dve.wait_ge(answered, 2)
            step(nc.vector.tensor_tensor(g.gate[:], g.gate[:], ez[:], ALU.mult))
            step(nc.vector.tensor_reduce(col[:], g.gate[:], AX, ALU.add))
            step(nc.vector.reciprocal(col[:], col[:]))
            step(nc.vector.tensor_tensor(g.gate[:], g.gate[:], per_token, ALU.mult))


def rank_of(nc, g, step, z, cmp_, same, rank, E):
    shape = [P, T, E, E]
    other, own = z[:].unsqueeze(2).broadcast_to(shape), z[:].unsqueeze(3).broadcast_to(shape)
    nc.vector.tensor_tensor(cmp_[:], other, own, ALU.is_gt)
    step(nc.vector.tensor_tensor(same[:], other, own, ALU.is_equal))
    before = {E0: g.before3, E1: g.before8}[E][:].rearrange("p (a b) -> p a b", a=E).unsqueeze(1).broadcast_to(shape)
    step(nc.vector.tensor_tensor(same[:], same[:], before, ALU.mult))
    step(nc.vector.tensor_tensor(cmp_[:], cmp_[:], same[:], ALU.add))
    step(nc.vector.tensor_reduce(rank[:], cmp_[:], AX, ALU.add))


def stage_experts0(nc, g):
    SC = HE ** -0.5
    KCH = [(0, 512), (512, 512), (1024, N - 1024)]
    with ExitStack() as ctx:
        s = Scope(nc, ctx, "exp0")
        w, par, bv = s.sb("w", [128, KC, 3 * HE]), s.sb("par", [128, 12]), s.sb("bv", [P, HE])
        q, qc = s.sb("q", [128, 2, N + 2]), s.sb("qc", [128, 2, N])
        kT, v = s.sb("kT", [128, 2, N]), s.sb("v", [P, T, HE])
        prob, probT = s.sb("prob", [P, 2, N]), s.sb("probT", [P, T, P])
        mx, nmx, total, r = s.sb("mx", [P, T]), s.sb("nmx", [P, T]), s.sb("total", [P, T]), s.sb("r", [P, T])
        score = s.ps("score", [P, 3 * 512])
        flip = [s.ps(f"flip{i}", [128, 512]) for i in range(3)]
        y = [s.ps(f"y{i}", [128, 512]) for i in range(2)]
        PROJ = 12 + T
        names = "w_in made taken scored masked probs scaled flipped unflipped summed stored chain q_in conv_in edges b_in"
        (w_in, made, taken, scored, masked, probs, scaled, flipped, unflipped, summed, stored, chain, q_in, conv_in,
         edges, b_in) = (s.sem(x) for x in names.split())
        NF = sum(-(-(t + 1) // 4) for t in range(T))
        ring = [flip[0], flip[1], flip[2], y[0]]
        block = ctx.enter_context(nc.Block())

        @block.sync
        def _(sp):
            sp.dma_start(w[:], g.exp0_w[0]).then_inc(w_in, 16)
            sp.dma_start(par[:], g.exp0_par[0]).then_inc(b_in, 16)
            sp.dma_start(bv[:], bass.AP(g.exp0_bv.tensor, 0, [[0, P], [1, HE]])).then_inc(b_in, 16)
            with sp.Fori(0, E0 - 1) as e:
                sp.wait_ge(taken, ONE + e * PROJ + PROJ)
                sp.dma_start(w[:], g.exp0_w[bass.ds(e + 1, 1)].rearrange("o p k f -> (o p) k f")).then_inc(w_in, 16)
                sp.wait_ge(conv_in, e * 2 + 2)
                sp.dma_start(par[:], g.exp0_par[bass.ds(e + 1, 1)].rearrange("o p f -> (o p) f")).then_inc(b_in, 16)
                sp.dma_start(bv[:], g.exp0_bv[bass.ds(e + 1, 1)].broadcast_to([P, HE])).then_inc(b_in, 16)

        @block.tensor
        def _(pe):
            for count in (summed, flipped):
                pe.sem_inc(count, 1)
            with pe.Fori(0, E0) as e:
                pe.wait_ge(w_in, e * 16 + 16)
                pe.wait_ge(stored, ONE + e * 2 * T)
                pe.wait_ge(unflipped, ONE + e * NF)
                n = 0

                def room():
                    pe.wait_ge(taken, ONE + e * PROJ + max(n - 3, 0))

                for m in range(4):
                    for c0, cn in CH:
                        room()
                        for k in range(KC):
                            last = nc.tensor.matmul(ring[n % 4][:, 0:cn],
                                                    w[:, k, m * 128:(m + 1) * 128], g.XT[:, k, c0:c0 + cn],
                                                    start=(k == 0), stop=(k == KC - 1))
                        last.then_inc(made, 1)
                        n += 1
                for t in range(T):
                    room()
                    for k in range(KC):
                        last = nc.tensor.matmul(ring[n % 4][0:P, 0:HE], g.XT[:, k, t * P:(t + 1) * P], w[:, k, 2 * HE:3 * HE],
                                                start=(k == 0), stop=(k == KC - 1))
                    last.then_inc(made, 1)
                    n += 1
                pe.wait_ge(taken, ONE + e * PROJ + PROJ)
                pe.wait_ge(conv_in, e * 2 + 2)

                def scores(t):
                    pe.wait_ge(probs, ONE + e * T + t)
                    for c0, cn in KCH:
                        cn = min(cn, (t + 1) * P - c0)
                        if cn <= 0:
                            continue
                        for m in range(2):
                            last = nc.tensor.matmul(score[:, c0:c0 + cn], qc[:, m, t * P:(t + 1) * P], kT[:, m, c0:c0 + cn],
                                                    start=(m == 0), stop=(m == 1))
                    last.then_inc(scored, 1)

                nf = 0
                scores(0)
                for t in range(T):
                    if t + 1 < T:
                        scores(t + 1)
                    pe.wait_ge(scaled, e * T + t + 1)
                    for j0 in range(0, t + 1, 4):
                        js = range(j0, min(j0 + 4, t + 1))
                        pe.wait_ge(unflipped, ONE + e * NF + max(nf - 2, 0))
                        for j in js:
                            last = nc.tensor.transpose(flip[nf % 3][0:P, (j - j0) * P:(j - j0 + 1) * P],
                                                       prob[:, t % 2, j * P:(j + 1) * P], g.ident[0:P, 0:P])
                        last.then_inc(flipped, 1)
                        nf += 1
                    pe.wait_ge(unflipped, ONE + e * NF + nf)
                    pe.wait_ge(stored, ONE + e * 2 * T + 2 * t)
                    for m in range(2):
                        for j in range(t + 1):
                            last = nc.tensor.matmul(y[m][:, 0:P], v[:, j, m * 128:(m + 1) * 128], probT[:, j, :],
                                                    start=(j == 0), stop=(j == t))
                        last.then_inc(summed, 1)
                assert nf == NF

        @block.scalar
        def _(act):
            for count in (stored, taken, probs):
                act.sem_inc(count, 1)
            def put_y(e, t, m):
                act.wait_ge(summed, ONE + e * 2 * T + 2 * t + m + 1)
                nc.scalar.activation(g.OT[:, bass.ds(e * 2 + m, 1), t * P:(t + 1) * P].rearrange("p o c -> p (o c)"),
                                     y[m][:, 0:P], ACT.Copy).then_inc(stored, 1)

            act.wait_ge(edges, 1)
            with act.Fori(0, E0) as e:
                act.wait_ge(b_in, e * 32 + 32)
                for n in range(12):
                    m, c = divmod(n, 3)
                    c0, cn = CH[c]
                    act.wait_ge(made, e * PROJ + n + 1)
                    dst = q[:, m, 1 + c0:1 + c0 + cn] if m < 2 else kT[:, m - 2, c0:c0 + cn]
                    nc.scalar.activation(dst, ring[n % 4][:, 0:cn], ACT.Identity, bias=par[:, m:m + 1]).then_inc(taken, 1)
                for t in range(T):
                    act.wait_ge(masked, e * T + t + 1)
                    act.wait_ge(flipped, ONE + e * NF + sum(-(-(u + 1) // 4) for u in range(t - 1)))
                    nc.scalar.activation(prob[:, t % 2, 0:(t + 1) * P], score[:, 0:(t + 1) * P], ACT.Exp,
                                         bias=nmx[:, t:t + 1], scale=SC, accum_out=total[:, t:t + 1]).then_inc(probs, 1)
                    for m in range(2):
                        if t:
                            put_y(e, t - 1, m)
                for m in range(2):
                    put_y(e, T - 1, m)

        @block.vector
        def _(dve):
            for count in (unflipped,):
                dve.sem_inc(count, 1)
            nc.vector.memset(q[:, :, 0:1], 0.0)
            nc.vector.memset(q[:, :, N + 1:N + 2], 0.0).then_inc(edges, 1)
            LINKS = 4 + T * 4
            with dve.Fori(0, E0) as e:
                step = Chain(dve, chain, e * LINKS)
                dve.wait_ge(b_in, e * 32 + 32)
                dve.wait_ge(taken, ONE + e * PROJ + 12)
                for n in range(12, PROJ):
                    dve.wait_ge(made, e * PROJ + n + 1)
                    nc.vector.tensor_tensor(v[:, n - 12, :], ring[n % 4][0:P, 0:HE], bv[:], ALU.add).then_inc(taken, 1)
                for m in range(2):
                    step(nc.vector.tensor_scalar(qc[:, m, :], q[:, m, 0:N], par[:, 4 + m:5 + m], par[:, 10 + m:11 + m],
                                                 ALU.mult, ALU.add))
                    step(nc.vector.scalar_tensor_tensor(qc[:, m, :], q[:, m, 1:N + 1], par[:, 6 + m:7 + m], qc[:, m, :],
                                                        ALU.mult, ALU.add))
                    nc.vector.scalar_tensor_tensor(qc[:, m, :], q[:, m, 2:N + 2], par[:, 8 + m:9 + m], qc[:, m, :],
                                                   ALU.mult, ALU.add).then_inc(conv_in, 1)
                nf = 0

                def top(t):
                    n = (t + 1) * P
                    dve.wait_ge(scored, e * T + t + 1)
                    step(nc.vector.tensor_tensor(score[:, t * P:n], score[:, t * P:n], g.causal[:], ALU.add))
                    step(nc.vector.tensor_reduce(mx[:, t:t + 1], score[:, 0:n], AX, ALU.max))
                    nc.vector.tensor_scalar(nmx[:, t:t + 1], mx[:, t:t + 1], -SC, None, ALU.mult).then_inc(masked, 1)

                top(0)
                for t in range(T):
                    n = (t + 1) * P
                    dve.wait_ge(probs, ONE + e * T + t + 1)
                    step(nc.vector.reciprocal(r[:, t:t + 1], total[:, t:t + 1]))
                    step(nc.vector.tensor_tensor(r[:, t:t + 1], r[:, t:t + 1],
                                                 g.gate[:, t:t + 1, bass.ds(e, 1)].rearrange("p t o -> p (t o)"), ALU.mult))
                    nc.vector.tensor_scalar(prob[:, t % 2, 0:n], prob[:, t % 2, 0:n], r[:, t:t + 1], None,
                                            ALU.mult).then_inc(scaled, 1)
                    if t + 1 < T:
                        top(t + 1)
                    for j0 in range(0, t + 1, 4):
                        js = min(4, t + 1 - j0)
                        dve.wait_ge(flipped, ONE + e * NF + nf + 1)
                        if j0 == 0:
                            dve.wait_ge(summed, ONE + e * 2 * T + 2 * t)
                        nc.vector.tensor_copy(probT[:, j0:j0 + js, :],
                                              flip[nf % 3][0:P, 0:js * P].rearrange("p (j c) -> p j c", j=js)
                                              ).then_inc(unflipped, 1)
                        nf += 1
                assert step.n == LINKS, step.n


def stage_linear_mix(nc, g):
    PROJ = T + 3
    with ExitStack() as ctx:
        s = Scope(nc, ctx, "mix1")
        w, bq, bkv = s.sb("w", [128, KC, 384]), s.sb("bq", [128, PAIRS]), s.sb("bkv", [P, 2, 256])
        kv = s.sb("kv", [P, T, 257])
        klow = s.sb("klow", [P, T, 128])
        qT, qlow = s.sb("qT", [128, N]), s.sb("qlow", [128, N])
        state, ksum = s.sb("state", [128, 128]), s.sb("ksum", [128, 128])
        rden = s.sb("rden", [128, 2, 417])
        ring = [s.ps(f"ring{i}", [128, 512]) for i in range(4)]
        kv_ps = s.ps("kv_ps", [128, 512])
        den = [s.ps("den0", [128, 512])]
        num = [s.ps(f"num{i}", [128, 512]) for i in range(2)]
        names = ("w_in b_in made taken k_low k_exp q_low q_exp k_in q_in kv_made state_in den_made den_used num_made "
                 "num_used chain bkv_in bkv_used")
        (w_in, b_in, made, taken, k_low, k_exp, q_low, q_exp, k_in, q_in, kv_made, state_in, den_made, den_used, num_made,
         num_used, chain, bkv_in, bkv_used) = (s.sem(x) for x in names.split())
        block = ctx.enter_context(nc.Block())

        @block.sync
        def _(sp):
            sp.dma_start(w[:], g.mix1_w[0]).then_inc(w_in, 16)
            sp.dma_start(bq[:], g.mix1_bq).then_inc(b_in, 16)
            sp.dma_start(bkv[:, 0, :], g.mix1_bkv[0:1].broadcast_to([P, 256])).then_inc(bkv_in, 16)
            with sp.Fori(0, PAIRS - 1) as i:
                sp.wait_ge(taken, ONE + i * PROJ + PROJ)
                sp.dma_start(w[:], g.mix1_w[bass.ds(i + 1, 1)].rearrange("o p k f -> (o p) k f")).then_inc(w_in, 16)
                sp.dma_start(bkv[:, 0, :], g.mix1_bkv[bass.ds(i + 1, 1)].broadcast_to([P, 256])).then_inc(bkv_in, 16)

        @block.tensor
        def _(pe):
            for count in (kv_made, num_made):
                pe.sem_inc(count, 1)
            with pe.Fori(0, PAIRS) as i:
                pe.wait_ge(w_in, i * 16 + 16)
                for n in range(PROJ):
                    pe.wait_ge(taken, ONE + i * PROJ + max(n - 3, 0))
                    for k in range(KC):
                        if n < T:
                            last = nc.tensor.matmul(ring[n % 4][0:P, 0:256], g.XT[:, k, n * P:(n + 1) * P], w[:, k, 128:384],
                                                    start=(k == 0), stop=(k == KC - 1))
                        else:
                            c0, cn = CH[n - T]
                            last = nc.tensor.matmul(ring[n % 4][:, 0:cn], w[:, k, 0:128], g.XT[:, k, c0:c0 + cn],
                                                    start=(k == 0), stop=(k == KC - 1))
                    last.then_inc(made, 1)
                pe.wait_ge(k_in, i + 1)
                pe.wait_ge(state_in, ONE + i)
                for t in range(T):
                    last = nc.tensor.matmul(kv_ps[:, 0:129], kv[:, t, 0:128], kv[:, t, 128:257], start=(t == 0), stop=(t == T - 1))
                last.then_inc(kv_made, 1)
                pe.wait_ge(state_in, ONE + i + 1)
                pe.wait_ge(q_in, i + 1)
                for c, (c0, cn) in enumerate(CH):
                    pe.wait_ge(den_used, ONE + i * 3 + c)
                    nc.tensor.matmul(den[0][:, 0:cn], ksum[:], qT[:, c0:c0 + cn], start=True, stop=True).then_inc(den_made, 1)
                    pe.wait_ge(num_used, ONE + i * 3 + max(c - 1, 0))
                    nc.tensor.matmul(num[c % 2][:, 0:cn], state[:], qT[:, c0:c0 + cn], start=True, stop=True).then_inc(num_made, 1)

        @block.scalar
        def _(act):
            with act.Fori(0, PAIRS) as i:
                act.wait_ge(k_low, i + 1)
                nc.scalar.activation(klow[:], klow[:], ACT.Exp).then_inc(k_exp, 1)
                act.wait_ge(q_low, i + 1)
                nc.scalar.activation(qlow[:], qlow[:], ACT.Exp).then_inc(q_exp, 1)

        @block.vector
        def _(dve):
            for count in (taken, state_in, den_used, num_used):
                dve.sem_inc(count, 1)
            step = Chain(dve, chain)
            nc.vector.memset(kv[:, :, 256:257], 1.0)
            step(nc.vector.memset(state[:], 0.0))
            dve.wait_ge(b_in, 16)
            LINKS = 2
            with dve.Fori(0, PAIRS) as i:
                step = Chain(dve, chain, 1 + i * LINKS)
                dve.wait_ge(bkv_in, i * 16 + 16)
                dve.wait_ge(kv_made, ONE + i)
                for t in range(T):
                    dve.wait_ge(made, i * PROJ + t + 1)
                    nc.vector.tensor_tensor(kv[:, t, 0:256], ring[t % 4][0:P, 0:256], bkv[:, 0, :], ALU.add).then_inc(taken, 1)
                dve.wait_ge(taken, ONE + i * PROJ + T)
                nc.vector.tensor_scalar(klow[:], kv[:, :, 0:128], 0.0, None, ALU.min).then_inc(k_low, 1)
                dve.wait_ge(num_made, ONE + i * 3)
                b = bq[:, bass.ds(i, 1)]
                for c, (c0, cn) in enumerate(CH):
                    n = T + c
                    dve.wait_ge(made, i * PROJ + n + 1)
                    low = nc.vector.tensor_scalar(qlow[:, c0:c0 + cn], ring[n % 4][:, 0:cn], b, 0.0, ALU.add, ALU.min)
                    nc.vector.tensor_scalar(qT[:, c0:c0 + cn], ring[n % 4][:, 0:cn], b, 0.0, ALU.add, ALU.max).then_inc(taken, 1)
                low.then_inc(q_low, 1)
                dve.wait_ge(k_exp, i + 1)
                nc.vector.scalar_tensor_tensor(kv[:, :, 0:128], kv[:, :, 0:128], 0.0, klow[:], ALU.max, ALU.add).then_inc(k_in, 1)
                dve.wait_ge(q_exp, i + 1)
                dve.wait_ge(taken, ONE + i * PROJ + PROJ)
                nc.vector.tensor_tensor(qT[:], qT[:], qlow[:], ALU.add).then_inc(q_in, 1)
                dve.wait_ge(kv_made, ONE + i + 1)
                step(nc.vector.tensor_copy(state[0:64, 0:64], kv_ps[0:64, 0:64]))
                step(nc.vector.tensor_copy(state[64:128, 64:128], kv_ps[64:128, 64:128]))
                nc.vector.tensor_scalar(ksum[:], g.halves[:], kv_ps[:, 128:129], None, ALU.mult).then_inc(state_in, 1)
                for c, (c0, cn) in enumerate(CH):
                    dve.wait_ge(den_made, i * 3 + c + 1)
                    nc.vector.reciprocal(rden[:, c % 2, 0:cn], den[0][:, 0:cn]).then_inc(den_used, 1)
                    dve.wait_ge(den_used, ONE + i * 3 + c + 1)
                    dve.wait_ge(num_made, ONE + i * 3 + c + 1)
                    nc.vector.tensor_tensor(g.OT[:, bass.ds(i, 1), c0:c0 + cn].rearrange("p o c -> p (o c)"),
                                            num[c % 2][:, 0:cn], rden[:, c % 2, 0:cn], ALU.mult).then_inc(num_used, 1)
                assert step.n == LINKS


def stage_gat(nc, g, name, inT, spare, w_dram, att_dram, b_dram, last_layer):
    HN = N // 2
    with ExitStack() as ctx:
        s = Scope(nc, ctx, name)
        C = s.sb("C", [P, T, N])
        h = s.sb("h", [P, T, D + 2])
        att = s.sb("att", [P, 2, D])
        bf = s.sb("bf", [128, KC])
        a = s.sb("a", [P, 8, T])
        A_SRC, A_DST, HIGH, Z, MX, SHIFT, SHIFT2, A_SRC2 = range(8)
        rows = s.sb("rows", [128, 2, N])
        e = s.sb("e", [P, 4, HN])
        small = s.sb("small", [P, 2])
        w = spare[:].rearrange("p k n -> p (k n)")[:, 0:KC * D].rearrange("p (k m) -> p k m", k=KC)
        flat = e[:].rearrange("p a n -> p (a n)")
        diag = [flat[:, 0:N], flat[:, N:2 * N]]
        missing, high = flat[:, 0:N], flat[:, N:2 * N]
        bk = [s.ps(f"bk{i}", [128, 512]) for i in range(8)]
        names = ("w_in att_in c_in b_in made taken scored_dot chain high_in flipped diag_in spread spread_used raised weights_in "
                 "den_made den_in agg agg_used c_diag")
        (w_in, att_in, c_in, b_in, made, taken, scored_dot, chain, high_in, flipped, diag_in, spread, spread_used, raised,
         weights_in, den_made, den_in, agg, agg_used, c_diag) = (s.sem(x) for x in names.split())
        block = ctx.enter_context(nc.Block())

        @block.sync
        def _(sp):
            sp.dma_start(w, w_dram.rearrange("(k p) m -> p k m", p=128)).then_inc(w_in, 16)
            sp.dma_start(att[:, 0, :], bcast_rows(att_dram[0], P, D)).then_inc(att_in, 16)
            sp.dma_start(att[:, 1, :], bcast_rows(att_dram[1], P, D)).then_inc(att_in, 16)
            sp.dma_start(C[:], g.cnt_table[0:N * N].rearrange("(t p d) o -> p t (d o)", p=P, d=N)).then_inc(c_in, 16)
            if last_layer:
                sp.wait_ge(scored_dot, 2 * T)
                sp.dma_start(att[:, 0, :], bcast_rows(b_dram, P, D)).then_inc(b_in, 16)
            else:
                sp.dma_start(bf[:], b_dram).then_inc(b_in, 16)

        @block.tensor
        def _(pe):
            pe.wait_ge(w_in, 16)
            for n in range(2 * T):
                t, hf = divmod(n, 2)
                if n >= 4:
                    pe.wait_ge(taken, n - 3)
                for k in range(KC):
                    last = nc.tensor.matmul(bk[n % 4][0:P, 0:HALF], inT[:, k, t * P:(t + 1) * P],
                                            w[:, k, hf * HALF:(hf + 1) * HALF], start=(k == 0), stop=(k == KC - 1))
                last.then_inc(made, 1)
            pe.wait_ge(high_in, 1)
            pe.wait_ge(taken, 2 * T)
            for t in range(T):
                last = nc.tensor.transpose(bk[t // 4][0:P, t % 4 * P:(t % 4 + 1) * P], high[:, t * P:(t + 1) * P],
                                           g.ident[0:P, 0:P])
            last.then_inc(flipped, 1)
            for r in range(2):
                pe.wait_ge(diag_in, r + 1)
                for c, (c0, cn) in enumerate(CH):
                    nc.tensor.matmul(bk[(3 + 3 * r + c) % 8][:, 0:cn], g.ones[0:P, :], diag[r][:, c0:c0 + cn],
                                     start=True, stop=True).then_inc(spread, 1)
            if last_layer:
                pe.wait_ge(weights_in, 2 * T)
                for n in range(2 * T):
                    d, hf = divmod(n, 2)
                    cols = HALF + hf
                    if n >= 4:
                        pe.wait_ge(agg_used, n - 3)
                    for j in range(T):
                        last = nc.tensor.matmul(bk[1 + n % 4][0:P, 0:cols], C[:, j, d * P:(d + 1) * P],
                                                h[:, j, hf * HALF:hf * HALF + cols], start=(j == 0), stop=(j == T - 1))
                    last.then_inc(agg, 1)
            else:
                pe.wait_ge(spread_used, 6)
                pe.wait_ge(weights_in, 2 * T)
                for c, (c0, cn) in enumerate(CH):
                    for j in range(T):
                        last = nc.tensor.matmul(bk[c][:, 0:cn], g.ones[0:P, :], C[:, j, c0:c0 + cn],
                                                start=(j == 0), stop=(j == T - 1))
                    last.then_inc(den_made, 1)
                for n in range(3 * KC):
                    f, c = divmod(n, 3)
                    c0, cn = CH[c]
                    if n >= 4:
                        pe.wait_ge(agg_used, n - 3)
                    for j in range(T):
                        last = nc.tensor.matmul(bk[3 + n % 4][:, 0:cn], h[:, j, f * 128:(f + 1) * 128], C[:, j, c0:c0 + cn],
                                                start=(j == 0), stop=(j == T - 1))
                    last.then_inc(agg, 1)

        @block.scalar
        def _(act):
            for n in range(2 * T):
                t, hf = divmod(n, 2)
                act.wait_ge(made, n + 1)
                nc.scalar.activation(h[:, t, hf * HALF:(hf + 1) * HALF], bk[n % 4][0:P, 0:HALF], ACT.Copy).then_inc(taken, 1)
            for r in range(2):
                for c, (c0, cn) in enumerate(CH):
                    act.wait_ge(spread, 3 * r + c + 1)
                    nc.scalar.activation(rows[:, r, c0:c0 + cn], bk[(3 + 3 * r + c) % 8][:, 0:cn], ACT.Copy).then_inc(spread_used, 1)
            act.wait_ge(spread_used, 6)
            for n in range(2 * T):
                t, hf = divmod(n, 2)
                if n >= 2:
                    act.wait_ge(weights_in, n - 1)
                for r, col in enumerate((A_SRC, A_SRC2)):
                    last = nc.scalar.activation(e[:, 2 * (n % 2) + r, :], rows[0:P, r, hf * HN:(hf + 1) * HN], ACT.Exp,
                                                bias=a[:, col, t:t + 1])
                last.then_inc(raised, 1)
            if not last_layer:
                act.wait_ge(b_in, 16)
                for n in range(3 * KC):
                    f, c = divmod(n, 3)
                    c0, cn = CH[c]
                    act.wait_ge(agg_used, n + 1)
                    nc.scalar.activation(g.OT[:, f, c0:c0 + cn], g.OT[:, f, c0:c0 + cn], ACT.Relu, bias=bf[:, f:f + 1])

        @block.vector
        def _(dve):
            step = Chain(dve, chain)
            nc.vector.memset(h[:, :, D:D + 1], 1.0)
            dve.wait_ge(att_in, 32)
            for t in range(T):
                dve.wait_ge(taken, 2 * t + 2)
                for r in range(2):
                    if t:
                        dve.wait_ge(scored_dot, 2 * t + r - 1)
                    nc.vector.tensor_tensor_reduce(flat[:, r * N:r * N + D], h[:, t, 0:D], att[:, r, :], 1.0, 0.0, ALU.mult,
                                                   ALU.add, a[:, (A_SRC, A_DST)[r], t:t + 1]).then_inc(scored_dot, 1)
            dve.wait_ge(c_in, 16)
            for t in range(T):
                last = nc.vector.tensor_tensor(C[:, t, t * P:(t + 1) * P], C[:, t, t * P:(t + 1) * P],
                                               g.ident[0:P, 0:P], ALU.add)
            last.then_inc(c_diag, 1)
            dve.wait_ge(scored_dot, 2 * T)
            dve.wait_ge(c_diag, 1)
            nc.vector.tensor_scalar(a[:, A_SRC2, :], a[:, A_SRC, :], 0.2, None, ALU.mult)
            for t in range(T):
                step(nc.vector.tensor_scalar(missing, C[:, t, :], 0.5, NEG, ALU.is_lt, ALU.mult))
                if t == 0:
                    step(nc.vector.tensor_scalar(high, missing, a[:, A_SRC, 0:1], None, ALU.add))
                else:
                    ins = nc.vector.scalar_tensor_tensor(high, missing, a[:, A_SRC, t:t + 1], high, ALU.add, ALU.max)
                    if t < T - 1:
                        step(ins)
            ins.then_inc(high_in, 1)
            dve.wait_ge(flipped, 1)
            for b, k in enumerate((4, 4, 2)):
                last = nc.vector.tensor_reduce(a[:, HIGH, 4 * b:4 * b + k],
                                               bk[b][0:P, 0:k * P].rearrange("p (t c) -> p t c", t=k), AX, ALU.max)
            step(last)
            step(nc.vector.tensor_tensor(a[:, Z, :], a[:, HIGH, :], a[:, A_DST, :], ALU.add))
            step(nc.vector.scalar_tensor_tensor(a[:, MX, :], a[:, Z, :], 0.2, a[:, Z, :], ALU.mult, ALU.max))
            nc.vector.tensor_tensor(a[:, SHIFT, :], a[:, A_DST, :], a[:, MX, :], ALU.subtract)
            step(nc.vector.scalar_tensor_tensor(a[:, SHIFT2, :], a[:, A_DST, :], 0.2, a[:, MX, :], ALU.mult, ALU.subtract))
            ident = g.ident[0:P, 0:P].unsqueeze(1).broadcast_to([P, T, P])
            for r in range(2):
                nc.vector.tensor_tensor(diag[r].rearrange("p (t c) -> p t c", t=T), ident,
                                        a[:, SHIFT + r, :].unsqueeze(2).broadcast_to([P, T, P]), ALU.mult).then_inc(diag_in, 1)
            for n in range(2 * T):
                t, hf = divmod(n, 2)
                c = C[:, t, hf * HN:(hf + 1) * HN]
                e1, e2 = e[:, 2 * (n % 2), :], e[:, 2 * (n % 2) + 1, :]
                dve.wait_ge(raised, n + 1)
                step(nc.vector.tensor_tensor(e1, e1, e2, ALU.max))
                nc.vector.scalar_tensor_tensor(c, e1, 1.0, c, ALU.min, ALU.mult).then_inc(weights_in, 1)
            if last_layer:
                dve.wait_ge(b_in, 16)
                step(nc.vector.tensor_tensor(g.X[:], g.X[:], att[:, 0, :].unsqueeze(1).broadcast_to([P, T, D]), ALU.add))
                for d in range(T):
                    dve.wait_ge(agg, 2 * d + 2)
                    step(nc.vector.reciprocal(small[:, d % 2:d % 2 + 1], bk[1 + (2 * d + 1) % 4][0:P, HALF:HALF + 1]))
                    for hf in range(2):
                        x = g.X[:, d, hf * HALF:(hf + 1) * HALF]
                        nc.vector.scalar_tensor_tensor(x, bk[1 + (2 * d + hf) % 4][0:P, 0:HALF], small[:, d % 2:d % 2 + 1], x,
                                                       ALU.mult, ALU.add).then_inc(agg_used, 1)
            else:
                for c, (c0, cn) in enumerate(CH):
                    dve.wait_ge(den_made, c + 1)
                    last = nc.vector.reciprocal(rows[:, 0, c0:c0 + cn], bk[c][:, 0:cn])
                step(last)
                for n in range(3 * KC):
                    f, c = divmod(n, 3)
                    c0, cn = CH[c]
                    dve.wait_ge(agg, n + 1)
                    nc.vector.tensor_tensor(g.OT[:, f, c0:c0 + cn], bk[3 + n % 4][:, 0:cn], rows[:, 0, c0:c0 + cn],
                                            ALU.mult).then_inc(agg_used, 1)


def stage_route(nc, g):
    with ExitStack() as ctx:
        s = Scope(nc, ctx, "route")
        wg, zT, z = s.sb("wg", [128, KC, E1]), s.sb("zT", [E1, N]), s.sb("z", [P, T, E1])
        cmp_, same, rank = s.sb("cmp", [P, T, E1, E1]), s.sb("same", [P, T, E1, E1]), s.sb("rank", [P, T, E1])
        pick = s.sb("pick", [P, 2, T, E1])
        both = s.sb("both", [P, T, E1], BF16)
        tmp = s.sb("tmp", [P, T, E1])
        col = s.sb("col", [P, 8, T])
        L1_, L2_, DIFF, EX, ONE, SLOT, KEEP, AWAY = range(8)
        wt = s.sb("wt", [P, 2, T])
        diag, row, eq = s.sb("diag", [P, N]), s.sb("row", [P, N]), s.sb("eq", [P, 2, N])
        offset = s.sb("offset", [P, N])
        ahead = s.sb("ahead", [P, T, N], BF16)
        place = s.sb("place", [P, T, E1])
        names_i = s.sb("names_i", [P, E1])
        trash = s.sb("trash", [P, 2, T])
        put_i, token = s.sb("put_i", [P, 2, T], I32), s.sb("token", [P, T], I32)
        zero = s.sb("zero", [120, SLOTS // 120], I32)
        bk = [s.ps(f"bk{i}", [128, 512]) for i in range(8)]
        names = ("w_in made taken flipped chain asked answered diag_in spread row_in ahead_in placed iotas zeroed put_in zero_in loaded "
                 "z_in")
        (w_in, made, taken, flipped, chain, asked, answered, diag_in, spread, row_in, ahead_in, placed, iotas, zeroed,
         put_in, zero_in, loaded, z_in) = (s.sem(x) for x in names.split())
        block = ctx.enter_context(nc.Block())

        @block.sync
        def _(sp):
            sp.dma_start(wg[:], g.route_w.rearrange("(k p) m -> p k m", p=128)).then_inc(w_in, 16)
            sp.wait_ge(zero_in, 1)
            sp.dma_start(g.slot_token[0:SLOTS].rearrange("(p f) o -> p (f o)", p=120), zero[:]).then_inc(zeroed, 16)
            sp.wait_ge(g.slot_put, 2 * T * 16)
            sp.dma_start(g.slots[:].rearrange("p (e c) -> p e c", e=E1),
                         g.slot_token[0:SLOTS].rearrange("(e p c) o -> p e (c o)", e=E1, p=SUB)).then_inc(loaded, 16)
            sp.wait_ge(loaded, 16)

        @block.tensor
        def _(pe):
            pe.wait_ge(w_in, 16)
            for c, (c0, cn) in enumerate(CH):
                for k in range(KC):
                    last = nc.tensor.matmul(bk[c][0:E1, 0:cn], wg[:, k, :], g.XT[:, k, c0:c0 + cn], start=(k == 0), stop=(k == KC - 1))
                last.then_inc(made, 1)
            pe.wait_ge(taken, 3)
            for t in range(T):
                last = nc.tensor.transpose(bk[3][0:P, t * E1:(t + 1) * E1], zT[:, t * P:(t + 1) * P], g.ident[0:E1, 0:E1])
            last.then_inc(flipped, 1)
            pe.wait_ge(diag_in, 1)
            for c, (c0, cn) in enumerate(CH):
                nc.tensor.matmul(bk[4 + c][:, 0:cn], g.ones[0:P, :], diag[:, c0:c0 + cn], start=True, stop=True).then_inc(spread, 1)
            pe.wait_ge(ahead_in, T)
            for i in range(T):
                for j in range(T):
                    last = nc.tensor.matmul(bk[7][0:P, i * E1:(i + 1) * E1], ahead[:, j, i * P:(i + 1) * P], both[:, j, :],
                                            start=(j == 0), stop=(j == T - 1))
            last.then_inc(placed, 1)

        @block.scalar
        def _(act):
            for c, (c0, cn) in enumerate(CH):
                act.wait_ge(made, c + 1)
                nc.scalar.activation(zT[:, c0:c0 + cn], bk[c][0:E1, 0:cn], ACT.Copy).then_inc(taken, 1)
            act.wait_ge(asked, 1)
            nc.scalar.activation(col[:, EX, :], col[:, DIFF, :], ACT.Exp).then_inc(answered, 1)
            for c, (c0, cn) in enumerate(CH):
                act.wait_ge(spread, c + 1)
                nc.scalar.activation(row[:, c0:c0 + cn], bk[4 + c][0:P, 0:cn], ACT.Copy).then_inc(row_in, 1)

        @block.gpsimd
        def _(pool):
            nc.gpsimd.memset(zero[:], 0).then_inc(zero_in, 1)
            nc.gpsimd.iota(offset[:], pattern=[[1, N]], base=0, channel_multiplier=-1, allow_small_or_imprecise_dtypes=True)
            nc.gpsimd.iota(names_i[:], pattern=[[1, E1]], base=0, channel_multiplier=0, allow_small_or_imprecise_dtypes=True)
            nc.gpsimd.iota(trash[:], pattern=[[P, 2 * T]], base=SLOTS, channel_multiplier=1, allow_small_or_imprecise_dtypes=True)
            nc.gpsimd.iota(token[:], pattern=[[P, T]], base=0, channel_multiplier=1).then_inc(iotas, 1)
            pool.wait_ge(iotas, 1)
            pool.wait_ge(put_in, 2)
            pool.wait_ge(zeroed, 16)
            for k in range(2):
                for t in range(T):
                    pool.indirect_dma_start(out=g.slot_token, out_offset=bass.IndirectOffsetOnAxis(ap=put_i[:, k, t:t + 1], axis=0),
                                            in_=token[:, t:t + 1], in_offset=None).then_inc(g.slot_put, 16)

        @block.vector
        def _(dve):
            step = Chain(dve, chain)
            dve.wait_ge(flipped, 1)
            step(nc.vector.tensor_copy(z[:], bk[3][0:P, 0:T * E1].rearrange("p (t e) -> p t e", e=E1)))
            rank_of(nc, g, step, z, cmp_, same, rank, E1)
            nc.vector.tensor_scalar(both[:], rank[:], 1.5, None, ALU.is_lt)
            for k in range(2):
                step(nc.vector.tensor_scalar(pick[:, k, :, :], rank[:], float(k), None, ALU.is_equal))
                step(nc.vector.tensor_tensor(tmp[:], pick[:, k, :, :], z[:], ALU.mult))
                step(nc.vector.tensor_reduce(col[:, L1_ + k, :], tmp[:], AX, ALU.add))
            nc.vector.tensor_tensor(col[:, DIFF, :], col[:, L2_, :], col[:, L1_, :], ALU.subtract).then_inc(asked, 1)
            dve.wait_ge(answered, 1)
            step(nc.vector.tensor_scalar(col[:, ONE, :], col[:, EX, :], 1.0, None, ALU.add))
            step(nc.vector.reciprocal(wt[:, 0, :], col[:, ONE, :]))
            step(nc.vector.tensor_tensor(wt[:, 1, :], col[:, EX, :], wt[:, 0, :], ALU.mult))
            nc.vector.tensor_tensor(diag[:].rearrange("p (t c) -> p t c", t=T), g.ident[0:P, 0:P].unsqueeze(1).broadcast_to([P, T, P]),
                                    wt[:, 0, :].unsqueeze(2).broadcast_to([P, T, P]), ALU.mult).then_inc(diag_in, 1)
            dve.wait_ge(row_in, 3)
            dve.wait_ge(iotas, 1)
            for t in range(T):
                own = wt[:, 0, t:t + 1]
                step(nc.vector.tensor_scalar(eq[:, 0, :], row[:], own, None, ALU.is_equal))
                step(nc.vector.scalar_tensor_tensor(eq[:, 1, :], offset[:], t * P + 0.5, eq[:, 0, :], ALU.is_gt, ALU.mult))
                nc.vector.scalar_tensor_tensor(ahead[:, t, :], row[:], own, eq[:, 1, :], ALU.is_lt, ALU.add).then_inc(ahead_in, 1)
            dve.wait_ge(placed, 1)
            step(nc.vector.tensor_copy(place[:], bk[7][0:P, 0:T * E1].rearrange("p (t e) -> p t e", e=E1)))
            for k in range(2):
                step(nc.vector.tensor_tensor(tmp[:], pick[:, k, :, :], place[:], ALU.mult))
                step(nc.vector.tensor_reduce(col[:, DIFF, :], tmp[:], AX, ALU.add))
                step(nc.vector.tensor_scalar(col[:, KEEP, :], col[:, DIFF, :], CAP - 0.5, None, ALU.is_lt))
                step(nc.vector.tensor_tensor(tmp[:], pick[:, k, :, :], names_i[:].unsqueeze(1).broadcast_to([P, T, E1]), ALU.mult))
                step(nc.vector.tensor_reduce(col[:, EX, :], tmp[:], AX, ALU.add))
                step(nc.vector.scalar_tensor_tensor(col[:, SLOT, :], col[:, EX, :], float(CAP), col[:, DIFF, :], ALU.mult, ALU.add))
                step(nc.vector.tensor_tensor(col[:, AWAY, :], col[:, SLOT, :], trash[:, k, :], ALU.subtract))
                step(nc.vector.tensor_tensor(col[:, AWAY, :], col[:, AWAY, :], col[:, KEEP, :], ALU.mult))
                nc.vector.tensor_tensor(put_i[:, k, :], col[:, AWAY, :], trash[:, k, :], ALU.add)
                nc.vector.tensor_tensor(g.read_i[:, k, :], col[:, SLOT, :], col[:, KEEP, :], ALU.mult)
                nc.vector.tensor_tensor(g.share[:, k, :], wt[:, k, :], col[:, KEEP, :], ALU.mult).then_inc(put_in, 1)
                dve.wait_ge(put_in, k + 1)


def stage_experts1(nc, g):
    GH = 4
    NG = HB // GH
    with ExitStack() as ctx:
        s = Scope(nc, ctx, "exp1")
        w1 = s.sb("w1", [128, 2, GH, KC, 128])
        w2 = s.sb("w2", [128, 2, GH, D])
        b1, b2 = s.sb("b1", [128, E1, HB]), s.sb("b2", [128, E1, KC])
        idx = s.sb("idx", [SUB, NS], I32)
        xg = s.sb("xg", [SUB, NS, D])
        xT = s.sb("xT", [128, KC, CAP])
        hid = s.sb("hid", [128, 2, CAP])
        oT = s.sb("oT", [128, KC, CAP])
        y = s.sb("y", [SUB, NS, D])
        hp = [s.ps(f"hp{i}", [128, 512]) for i in range(2)]
        op = [s.ps(f"op{i}", [128, 512]) for i in range(KC)]
        w1_in, w2_in = [s.sem(f"w1_in{i}") for i in range(2)], [s.sem(f"w2_in{i}") for i in range(2)]
        names = "b_in used idx_in open xg_used flipped x_in made raised out_made o_in turned y_in stored y_free"
        (b_in, used, idx_in, opened, xg_used, flipped, x_in, made, raised, out_made, o_in, turned, y_in,
         stored, y_free) = (s.sem(x) for x in names.split())
        block = ctx.enter_context(nc.Block())

        @block.sync
        def _(sp):
            for count in (y_free,):
                sp.sem_inc(count, 1)
            def load(j, slot):
                one = lambda a: a[bass.ds(j, 1)].rearrange("o p g f -> (o p) g f")
                sp.dma_start(w1[:, slot].rearrange("p g k m -> p g (k m)"), one(g.exp1_w1)).then_inc(w1_in[slot], 16)
                sp.dma_start(w2[:, slot], one(g.exp1_w2)).then_inc(w2_in[slot], 16)

            load(0, 0)
            load(1, 1)
            sp.dma_start(b1[:], g.exp1_b1).then_inc(b_in, 16)
            sp.dma_start(b2[:], g.exp1_b2).then_inc(b_in, 16)
            with sp.Fori(0, E1 - 1) as e:
                for gi in range(NG):
                    sp.wait_ge(used, e * NG + gi + 1)
                    load(e * NG + gi + 2, gi % 2)
                sp.wait_ge(y_in, ONE + e * 2 * NS + 2 * NS)
                sp.dma_start(g.slot_out[bass.ds(e * CAP, CAP)].rearrange("(p c) d -> p c d", p=SUB), y[:]).then_inc(stored, 16)
                sp.wait_ge(stored, e * 16 + 16)
                sp.sem_inc(y_free, 1)
            for gi in range(NG - 2):
                sp.wait_ge(used, (E1 - 1) * NG + gi + 1)
                load((E1 - 1) * NG + gi + 2, gi % 2)
            sp.wait_ge(y_in, ONE + E1 * 2 * NS)
            sp.dma_start(g.slot_out[(E1 - 1) * CAP:E1 * CAP].rearrange("(p c) d -> p c d", p=SUB), y[:]).then_inc(stored, 16)
            sp.wait_ge(stored, E1 * 16)

        @block.gpsimd
        def _(pool):
            with pool.Fori(0, E1) as e:
                pool.wait_ge(xg_used, ONE + e)
                pool.sem_inc(opened, 1)
                nc.gpsimd.tensor_copy(idx[:], g.slots[:, bass.ds(e * NS, NS)]).then_inc(idx_in, 1)
                pool.wait_ge(idx_in, e + 1)
                pool.sem_inc(opened, 1)
                for c in range(NS):
                    pool.indirect_dma_start(out=xg[:, c, :], out_offset=None, in_=g.xn3,
                                            in_offset=bass.IndirectOffsetOnAxis(ap=idx[:, c:c + 1], axis=0)).then_inc(g.gathered, 16)

        @block.tensor
        def _(pe):
            with pe.Fori(0, E1) as e:
                pe.wait_ge(g.gathered, e * NS * 16 + NS * 16)
                pe.wait_ge(y_in, ONE + e * 2 * NS)
                for c in range(NS):
                    pe.wait_ge(x_in, ONE + e * NS + max(c - 1, 0))
                    for k in range(KC):
                        last = nc.tensor.transpose(hp[c % 2][:, k * SUB:(k + 1) * SUB], xg[:, c, k * 128:(k + 1) * 128],
                                                   g.ident[0:SUB, 0:SUB])
                    last.then_inc(flipped, 1)
                last_flip = e * NS + NS
                pe.wait_ge(x_in, ONE + last_flip)

                def hidden(j):
                    gi, r = divmod(j, GH)
                    if r == 0:
                        pe.wait_ge(w1_in[gi % 2], e * (NG // 2) * 16 + (gi // 2 + 1) * 16)
                    pe.wait_ge(raised, ONE + e * HB + max(j - 1, 0))
                    for k in range(KC):
                        last = nc.tensor.matmul(hp[j % 2][:, 0:CAP], w1[:, gi % 2, r, k, :], xT[:, k, :],
                                                start=(k == 0), stop=(k == KC - 1))
                    last.then_inc(made, 1)

                def out(j):
                    gi, r = divmod(j, GH)
                    if r == 0:
                        pe.wait_ge(w2_in[gi % 2], e * (NG // 2) * 16 + (gi // 2 + 1) * 16)
                    if j == 0:
                        pe.wait_ge(o_in, ONE + e * KC)
                    pe.wait_ge(raised, ONE + e * HB + j + 1)
                    for m in range(KC):
                        last = nc.tensor.matmul(op[m][:, 0:CAP], w2[:, gi % 2, r, m * 128:(m + 1) * 128], hid[:, j % 2, :],
                                                start=(j == 0), stop=(j == HB - 1))
                    if r == GH - 1:
                        last.then_inc(used, 1)

                hidden(0)
                for j in range(HB):
                    if j + 1 < HB:
                        hidden(j + 1)
                    out(j)
                for n in range(2 * NS):
                    c, hf = divmod(n, 2)
                    if n == 0:
                        pe.wait_ge(o_in, ONE + e * KC + KC)
                    pe.wait_ge(y_in, ONE + e * 2 * NS + max(n - 1, 0))
                    for k in range(3):
                        last = nc.tensor.transpose(hp[n % 2][0:SUB, k * 128:(k + 1) * 128], oT[:, 3 * hf + k, c * SUB:(c + 1) * SUB],
                                                   g.ident[:])
                    last.then_inc(turned, 1)

        @block.scalar
        def _(act):
            for count in (raised, o_in):
                act.sem_inc(count, 1)
            act.wait_ge(b_in, 32)
            with act.Fori(0, E1) as e:
                for j in range(HB):
                    act.wait_ge(made, e * HB + j + 1)
                    nc.scalar.activation(hid[:, j % 2, :], hp[j % 2][:, 0:CAP], ACT.Gelu,
                                         bias=b1[:, bass.ds(e, 1), j:j + 1].rearrange("p a b -> p (a b)")).then_inc(raised, 1)
                act.wait_ge(used, e * NG + NG)
                for m in range(KC):
                    nc.scalar.activation(oT[:, m, :], op[m][:, 0:CAP], ACT.Identity,
                                         bias=b2[:, bass.ds(e, 1), m:m + 1].rearrange("p a b -> p (a b)")).then_inc(o_in, 1)

        @block.vector
        def _(dve):
            for count in (x_in, y_in, xg_used):
                dve.sem_inc(count, 1)
            with dve.Fori(0, E1) as e:
                for c in range(NS):
                    dve.wait_ge(flipped, e * NS + c + 1)
                    ins = nc.vector.tensor_copy(xT[:, :, c * SUB:(c + 1) * SUB],
                                                hp[c % 2][:, 0:KC * SUB].rearrange("p (k c) -> p k c", k=KC))
                    ins.then_inc(x_in, 1)
                dve.wait_ge(x_in, ONE + e * NS + NS)
                dve.sem_inc(xg_used, 1)
                dve.wait_ge(y_free, ONE + e)
                for n in range(2 * NS):
                    c, hf = divmod(n, 2)
                    dve.wait_ge(turned, e * 2 * NS + n + 1)
                    nc.vector.tensor_copy(y[:, c, hf * HALF:(hf + 1) * HALF], hp[n % 2][0:SUB, 0:HALF]).then_inc(y_in, 1)


def stage_combine(nc, g):
    with ExitStack() as ctx:
        s = Scope(nc, ctx, "comb")
        SL = 4
        y = s.sb("y", [P, SL, D])
        got = g.got
        added, stored = s.sem("added"), s.sem("stored")
        block = ctx.enter_context(nc.Block())

        @block.gpsimd
        def _(pool):
            for n in range(2 * T):
                t, k = divmod(n, 2)
                if n >= SL:
                    pool.wait_ge(added, n - SL + 1)
                pool.indirect_dma_start(out=y[:, n % SL, :], out_offset=None, in_=g.slot_out,
                                        in_offset=bass.IndirectOffsetOnAxis(ap=g.read_i[:, k, t:t + 1], axis=0)).then_inc(got[n % SL], 16)

        @block.vector
        def _(dve):
            for n in range(2 * T):
                t, k = divmod(n, 2)
                dve.wait_ge(got[n % SL], 16 * (n // SL + 1))
                dve.wait_ge(added, n)
                nc.vector.scalar_tensor_tensor(g.X[:, t, :], y[:, n % SL, :], g.share[:, k, t:t + 1], g.X[:, t, :],
                                               ALU.mult, ALU.add).then_inc(added, 1)

        @block.sync
        def _(sp):
            for h in range(2):
                sp.wait_ge(added, T * (h + 1))
                sp.dma_start(g.out[h * N // 2:(h + 1) * N // 2].rearrange("(t p) d -> p t d", p=P),
                             g.X[:, h * T // 2:(h + 1) * T // 2, :]).then_inc(stored, 16)
            sp.wait_ge(stored, 32)


class Shared:

    def __init__(self, dram):
        self.x, self.edge_cols, self.edge_rows, self.edge_w, self.mix0_w = dram["x"], dram["edge_cols"], dram["edge_rows"], dram["edge_w"], dram["mix0_w"]
        self.mix0_proj, self.mix0_proj_b, self.gcn_wd, self.gcn_bd, self.gcn_wu = dram["mix0_proj"], dram["mix0_proj_b"], dram["gcn_wd"], dram["gcn_bd"], dram["gcn_wu"]
        self.gcn_bu, self.gcn_w1, self.gcn_b1, self.gcn_w2, self.gcn_b2 = dram["gcn_bu"], dram["gcn_w1"], dram["gcn_b1"], dram["gcn_w2"], dram["gcn_b2"]
        self.gate_w1, self.gate_b1, self.gate_w2, self.gate_b2, self.exp0_w = dram["gate_w1"], dram["gate_b1"], dram["gate_w2"], dram["gate_b2"], dram["exp0_w"]
        self.exp0_par, self.exp0_bv, self.mix1_w, self.mix1_bq, self.mix1_bkv = dram["exp0_par"], dram["exp0_bv"], dram["mix1_w"], dram["mix1_bq"], dram["mix1_bkv"]
        self.mix1_wo, self.mix1_bo, self.gat0_w, self.gat0_att, self.gat0_b = dram["mix1_wo"], dram["mix1_bo"], dram["gat0_w"], dram["gat0_att"], dram["gat0_b"]
        self.gat1_w, self.gat1_att, self.gat1_b, self.route_w, self.exp1_w1 = dram["gat1_w"], dram["gat1_att"], dram["gat1_b"], dram["route_w"], dram["exp1_w1"]
        self.exp1_w2, self.exp1_b1, self.exp1_b2, self.ffn0_wp, self.ffn0_bp = dram["exp1_w2"], dram["exp1_b1"], dram["exp1_b2"], dram["ffn0_wp"], dram["ffn0_bp"]
        self.out = dram["out"]


def setup(nc, dram, ctx):
    g = Shared(dram)
    sb = lambda n, sh, dt=F32: ctx.enter_context(nc.sbuf_tensor(n, sh, dt))
    sem = lambda name: ctx.enter_context(nc.semaphore(name))
    g.put_w, g.put_c, g.slot_put, g.gathered = sem("put_w"), sem("put_c"), sem("slot_put"), sem("gathered")
    g.got = [sem(f"got{i}") for i in range(4)]
    g.X = sb("X", [P, T, D])
    g.XT = sb("XT", [128, KC, N])
    g.OT = sb("OT", [128, KC, N])
    g.ident, g.ones = sb("ident", [128, 128]), sb("ones", [128, 128])
    g.halves = sb("halves", [128, 128])
    g.lower, g.causal = sb("lower", [P, P]), sb("causal", [P, P])
    g.before3, g.before8 = sb("before3", [P, E0 * E0]), sb("before8", [P, E1 * E1])
    g.slots, g.read_i = sb("slots", [SUB, E1 * NS], I32), sb("read_i", [P, 2, T], I32)
    g.share = sb("share", [P, 2, T])
    g.slot_token = nc.dram_tensor("slot_token", [SLOTS + 2 * N, 1], I32, kind="Internal").ap()
    g.slot_out = nc.dram_tensor("slot_out", [SLOTS, D], F32, kind="Internal").ap()
    g.xn3 = nc.dram_tensor("xn3", [N, D], F32, kind="Internal").ap()
    g.gate = sb("gate", [P, T, E0])
    g.zero_tail = sb("zero_tail", [1, TABLE - MAIN])
    g.two, g.eps = sb("two", [128, 1]), sb("eps", [128, 1])
    g.ew_table = nc.dram_tensor("ew_table", [TABLE, 1], F32, kind="Internal").ap()
    g.cnt_table = nc.dram_tensor("cnt_table", [TABLE, 1], F32, kind="Internal").ap()
    return g


def build_program(nc, dram):
    SEMAPHORES.clear()
    with ExitStack() as ctx:
        g = setup(nc, dram, ctx)
        todo = [
            lambda: stage_start(nc, g),
            lambda: stage_norm(nc, g, "norm0"),
            lambda: stage_poly_mix(nc, g),
            lambda: stage_tok_linear(nc, g, "proj0", g.OT, g.mix0_proj, g.mix0_proj_b),
            lambda: stage_gcn(nc, g),
            lambda: stage_norm(nc, g, "norm1"),
            lambda: stage_gate(nc, g),
            lambda: stage_experts0(nc, g),
            lambda: stage_tok_linear(nc, g, "proj1", g.OT, g.ffn0_wp, g.ffn0_bp),
            lambda: stage_clear(nc, g),
            lambda: stage_norm(nc, g, "norm2"),
            lambda: stage_linear_mix(nc, g),
            lambda: stage_tok_linear(nc, g, "proj2", g.OT, g.mix1_wo, g.mix1_bo),
            lambda: stage_gat(nc, g, "gat0", g.XT, g.OT, g.gat0_w, g.gat0_att, g.gat0_b, False),
            lambda: stage_gat(nc, g, "gat1", g.OT, g.XT, g.gat1_w, g.gat1_att, g.gat1_b, True),
            lambda: stage_norm(nc, g, "norm3", g.xn3),
            lambda: stage_route(nc, g),
            lambda: stage_experts1(nc, g),
            lambda: stage_combine(nc, g),
        ]
        for stage in todo:
            stage()


def lay_out(i):
    a = {k: np.asarray(v) for k, v in i.items()}
    con = np.ascontiguousarray
    pad = lambda v, fill: np.concatenate([v, np.full(PADDED - EDGES, fill, v.dtype)])
    src, dst, ew = pad(a["src"], N), pad(a["dst"], 0), pad(a["edge_weight"], 0)
    cols = lambda v: v.reshape(GROUPS, P).T
    heads = lambda wq, wk, wv: con(np.stack([m.reshape(KC, 128, PAIRS, 128).transpose(2, 1, 0, 3)
                                             for m in (wq, wk, wv)], 3).reshape(PAIRS, 128, KC, 384))
    qkv = a["L0_mix_qkv_w"].T
    feat = lambda b: b.reshape(-1, 128).T
    conv = np.zeros((E0, 4, D // E0), np.float32)
    conv[:, 1] = 1
    conv[0, 0:3], conv[0, 3] = a["L0_ffn_conv_w"][:, 0].T, a["L0_ffn_conv_b"]
    wqk, bqk = a["L0_ffn_Wqk"], a["L0_ffn_bqk"]
    exp0 = [np.concatenate([wqk[:, e * HE:(e + 1) * HE], wqk[:, D + e * HE:D + (e + 1) * HE], a["L0_ffn_Wv"][e]], 1)
            .reshape(KC, 128, 3 * HE).transpose(1, 0, 2) for e in range(E0)]
    par0 = [np.concatenate([feat(bqk[e * HE:(e + 1) * HE]), feat(bqk[D + e * HE:D + (e + 1) * HE]),
                            *(feat(c) for c in conv[e])], 1) for e in range(E0)]
    o = {
        "x": a["x"],
        "edge_cols": con(np.stack([cols(src), cols(dst)], 1)),
        "edge_rows": con(np.stack([src, dst])),
        "edge_w": con(ew),
        "mix0_w": heads(qkv[:, :D], qkv[:, D:2 * D], qkv[:, 2 * D:]),
        "mix0_proj": con(a["L0_mix_proj_w"].T),
        "mix0_proj_b": a["L0_mix_proj_b"],
        "gcn_wd": a["L0_gnn_Wd"], "gcn_bd": a["L0_gnn_bd"][:, None],
        "gcn_wu": a["L0_gnn_Wu"], "gcn_bu": feat(a["L0_gnn_bu"]),
        "gcn_w1": a["L0_gnn_W1"], "gcn_b1": a["L0_gnn_b1"],
        "gcn_w2": a["L0_gnn_W2"], "gcn_b2": a["L0_gnn_b2"],
        "gate_w1": a["L0_ffn_Wg1"], "gate_b1": a["L0_ffn_bg1"][:, None],
        "gate_w2": a["L0_ffn_Wg2"], "gate_b2": a["L0_ffn_bg2"],
        "exp0_w": np.stack(exp0), "exp0_par": np.stack(par0), "exp0_bv": a["L0_ffn_bv"],
        "mix1_w": heads(a["L1_mix_Wq"], a["L1_mix_Wk"], a["L1_mix_Wv"]),
        "mix1_bq": feat(a["L1_mix_bq"]),
        "mix1_bkv": np.concatenate([a["L1_mix_bk"].reshape(PAIRS, 128), a["L1_mix_bv"].reshape(PAIRS, 128)], 1),
        "mix1_wo": a["L1_mix_Wo"], "mix1_bo": a["L1_mix_bo"],
        "gat0_w": a["L1_gnn_W1"], "gat0_att": np.stack([a["L1_gnn_att_src1"], a["L1_gnn_att_dst1"]]),
        "gat0_b": feat(a["L1_gnn_b1"]),
        "gat1_w": a["L1_gnn_W2"], "gat1_att": np.stack([a["L1_gnn_att_src2"], a["L1_gnn_att_dst2"]]),
        "gat1_b": a["L1_gnn_b2"],
        "route_w": a["L1_ffn_Wg"],
        "exp1_w1": a["L1_ffn_W1"].reshape(E1, KC, 128, HB // 4, 4, 128).transpose(0, 3, 2, 4, 1, 5).reshape(E1 * HB // 4, 128, 4, D),
        "exp1_w2": a["L1_ffn_W2"].reshape(E1, HB // 4, 4, 128, D).transpose(0, 1, 3, 2, 4).reshape(E1 * HB // 4, 128, 4, D),
        "exp1_b1": a["L1_ffn_b1"].reshape(E1, HB, 128).transpose(2, 0, 1),
        "exp1_b2": a["L1_ffn_b2"].reshape(E1, KC, 128).transpose(2, 0, 1),
        "ffn0_wp": a["L0_ffn_Wp"], "ffn0_bp": a["L0_ffn_bp"],
    }
    return {k: con(v) for k, v in o.items()}


def kernel(**inputs):
    import concourse.bacc as _bacc
    from concourse import mybir as _mybir
    from concourse.bass_utils import run_bass_kernel_spmd as _run

    nc = _bacc.Bacc("TRN2", target_bir_lowering=False, num_devices=1)
    arrays = lay_out(inputs)
    dram = {k: nc.dram_tensor(f"in_{k}", v.shape, _mybir.dt.from_np(v.dtype), kind="ExternalInput").ap()
            for k, v in arrays.items()}
    dram["out"] = nc.dram_tensor("out", (N, D), F32, kind="ExternalOutput").ap()
    build_program(nc, dram)
    r = _run(nc, [{f"in_{k}": v for k, v in arrays.items()}], core_ids=[0])
    return r.results[0]["out"]
```

```python
from contextlib import ExitStack

import numpy as np

import concourse.bass as bass
from concourse import mybir

F32 = mybir.dt.float32
F32R = mybir.dt.float32r
BF16 = mybir.dt.bfloat16
I32 = mybir.dt.int32
ALU = mybir.AluOpType
ACT = mybir.ActivationFunctionType
AX = mybir.AxisListType.X

N, D = 1250, 768
P = 125
T = N // P
KC = D // 128
HALF = D // 2
CH = [(0, 418), (418, 416), (834, 416)]
EDGES = 20000
GPC = 16
CHUNKS = 10
GROUPS = GPC * CHUNKS
PADDED = GROUPS * P
CW = GPC * P
TRASH = N * N + P
MAIN = N * N + 500
TABLE = MAIN + 16
ZEROED = 2 * 4 * 16
NEG = -1e30
EPS = 1e-5
ONE = 1
H0 = 12
PAIRS = H0 // 2
HD = D // H0
E0 = 3
HE = D // E0
E1 = 8
HID = 4 * D
HB = HID // 128
CAP = int(1.25 * N * 2 / E1)
SUB = 78
NS = CAP // SUB
SLOTS = E1 * CAP
assert N == T * P and PADDED >= EDGES and NS * SUB == CAP and MAIN % P == 0


class Chain:

    def __init__(self, eng, sem, base=0):
        self.eng, self.sem, self.base, self.n = eng, sem, base, 0

    def __call__(self, ins):
        self.n += 1
        ins.then_inc(self.sem, 1)
        self.eng.wait_ge(self.sem, self.base + self.n)


SEMAPHORES = set()


class Scope:

    def __init__(self, nc, ctx, stage):
        self.nc, self.ctx, self.stage = nc, ctx, stage

    def sb(self, name, shape, dt=F32):
        return self.ctx.enter_context(self.nc.sbuf_tensor(f"{self.stage}_{name}", shape, dt))

    def ps(self, name, shape, dt=F32):
        return self.ctx.enter_context(self.nc.psum_tensor(f"{self.stage}_{name}", shape, dt))

    def sem(self, name):
        sem = self.ctx.enter_context(self.nc.semaphore(f"{self.stage}_{name}"))
        SEMAPHORES.add(sem.num)
        return sem


def bcast_rows(ap, p, n):
    return bass.AP(ap.tensor, ap.offset, [[0, p], [1, n]])


def stage_start(nc, g):
    with ExitStack() as ctx:
        s = Scope(nc, ctx, "start")
        zeros = g.OT[0:P].rearrange("p k n -> p (k n)")[:, 0:MAIN // P // 4]
        made, chain, x_in = s.sem("made"), s.sem("chain"), s.sem("x_in")
        block = ctx.enter_context(nc.Block())

        @block.vector
        def _(dve):
            nc.vector.memset(zeros, 0.0).then_inc(made, 1)
            nc.vector.memset(g.zero_tail[:], 0.0)
            nc.vector.memset(g.ones[:], 1.0)
            nc.vector.memset(g.two[:], 2.0)
            nc.vector.memset(g.eps[:], EPS)
            nc.vector.memset(g.halves[:], 0.0).then_inc(made, 1)
            dve.wait_ge(made, 2)
            nc.vector.memset(g.halves[0:64, 0:64], 1.0)
            nc.vector.memset(g.halves[64:128, 64:128], 1.0)
            for before, E in ((g.before3, E0), (g.before8, E1)):
                for e in range(E):
                    if e:
                        nc.vector.memset(before[:, e * E:e * E + e], 1.0)
                    nc.vector.memset(before[:, e * E + e:(e + 1) * E], 0.0)

        @block.gpsimd
        def _(pool):
            step = Chain(pool, chain)
            step(nc.gpsimd.memset(g.ident[:], 0.0))
            nc.gpsimd.affine_select(out=g.ident[:], in_=g.ident[:], compare_op=ALU.not_equal, fill=1.0, base=0,
                                    pattern=[[-1, 128]], channel_multiplier=1)
            step(nc.gpsimd.memset(g.lower[:], 1.0))
            nc.gpsimd.affine_select(out=g.lower[:], in_=g.lower[:], compare_op=ALU.is_gt, fill=0.0, base=0,
                                    pattern=[[-1, P]], channel_multiplier=1)
            step(nc.gpsimd.memset(g.causal[:], 0.0))
            nc.gpsimd.affine_select(out=g.causal[:], in_=g.causal[:], compare_op=ALU.is_ge, fill=NEG, base=0,
                                    pattern=[[-1, P]], channel_multiplier=1)

        @block.sync
        def _(sp):
            sp.dma_start(g.X[:], g.x.rearrange("(t p) d -> p t d", p=P)).then_inc(x_in, 16)
            sp.wait_ge(made, 1)
            for table in (g.ew_table, g.cnt_table):
                v = table[0:MAIN].rearrange("(q p) o -> q (p o)", q=4).rearrange("q (p f) -> q p f", p=P)
                for q in range(4):
                    sp.dma_start(v[q], zeros).then_inc(g.zeroed, 16)
            sp.wait_ge(x_in, 16)


def stage_norm(nc, g, name, keep=None):
    with ExitStack() as ctx:
        s = Scope(nc, ctx, name)
        xn = s.sb("xn", [P, T, D])
        stats = s.sb("stats", [P, T, 2, 6])
        mv = s.sb("mv", [P, T, 2])
        std = s.sb("std", [P, T])
        rstd = s.sb("rstd", [P, T])
        flip = [s.ps(f"flip{i}", [128, 512]) for i in range(4)]
        stats_in, var_in, std_in, rstd_in = s.sem("stats"), s.sem("var"), s.sem("std"), s.sem("rstd")
        normed, flipped, moved, kept = s.sem("normed"), s.sem("flipped"), s.sem("moved"), s.sem("kept")
        block = ctx.enter_context(nc.Block())

        @block.vector
        def _(dve):
            for t in range(T):
                for h in range(2):
                    last = nc.vector.bn_stats(stats[:, t, h, :], g.X[:, t, h * HALF:(h + 1) * HALF])
            last.then_inc(stats_in, 1)
            dve.wait_ge(stats_in, 1)
            for t in range(T):
                last = nc.vector.bn_aggr(mv[:, t, :], stats[:, t, :, :])
            last.then_inc(var_in, 1)
            dve.wait_ge(std_in, 1)
            nc.vector.reciprocal(rstd[:], std[:]).then_inc(rstd_in, 1)
            dve.wait_ge(rstd_in, 1)
            for t in range(T):
                nc.vector.tensor_scalar(xn[:, t, :], g.X[:, t, :], mv[:, t, 0:1], rstd[:, t:t + 1],
                                        ALU.subtract, ALU.mult).then_inc(normed, 1)

        @block.scalar
        def _(act):
            act.wait_ge(var_in, 1)
            nc.scalar.activation(std[:], mv[:, :, 1], ACT.Sqrt, bias=g.eps[0:P, :]).then_inc(std_in, 1)
            for n in range(2 * T):
                t, h = divmod(n, 2)
                act.wait_ge(flipped, n + 1)
                nc.scalar.activation(g.XT[:, 3 * h:3 * h + 3, t * P:(t + 1) * P],
                                     flip[n % 4][:, 0:3 * P].rearrange("p (k c) -> p k c", k=3),
                                     ACT.Copy).then_inc(moved, 1)

        @block.tensor
        def _(pe):
            for n in range(2 * T):
                t, h = divmod(n, 2)
                if h == 0:
                    pe.wait_ge(normed, t + 1)
                if n >= 4:
                    pe.wait_ge(moved, n - 3)
                for k in range(3):
                    f = (3 * h + k) * 128
                    last = nc.tensor.transpose(flip[n % 4][:, k * P:(k + 1) * P], xn[:, t, f:f + 128],
                                               g.ident[0:P, 0:P])
                last.then_inc(flipped, 1)

        @block.sync
        def _(sp):
            if keep is not None:
                sp.wait_ge(normed, T)
                sp.dma_start(keep.rearrange("(t p) d -> p t d", p=P), xn[:]).then_inc(kept, 16)
                sp.wait_ge(kept, 16)


def stage_poly_mix(nc, g):
    NSCORE = 2 * 3 * T
    NEV = 6 + T + NSCORE
    with ExitStack() as ctx:
        s = Scope(nc, ctx, "mix0")
        w = s.sb("w", [128, KC, 384])
        k2 = s.sb("k2", [128, 2, N], F32R)
        q2 = s.sb("q2", [128, 2, 2, N], F32R)
        v1 = s.sb("v1", [P, T, 2, 128])
        attn = s.sb("attn", [P, 4, 418])
        rden = s.sb("rden", [128, 2, 418])
        key_cols, keys, ew_cols = s.sb("key_cols", [P, 2, GROUPS], I32), s.sb("keys", [P, GROUPS]), None
        rows_i, rows_w = s.sb("rows_i", [P, 2, CW], I32), s.sb("rows_w", [P, CW])
        key_row, same, part = s.sb("key_row", [P, CW]), s.sb("same", [P, CW]), s.sb("part", [P, CW])
        val_w, val_c = s.sb("val_w", [P, 2, GPC]), s.sb("val_c", [P, 2, GPC])
        dup, away, idxf = s.sb("dup", [P, GPC]), s.sb("away", [P, GPC]), s.sb("idxf", [P, GPC])
        idx = s.sb("idx", [P, 2, GPC], I32)
        trash_i, trash = s.sb("trash_i", [P, 1], I32), s.sb("trash", [P, 1])
        ring = [s.ps(f"ring{i}", [128, 512]) for i in range(4)]
        out = [s.ps(f"out{i}", [128, 512]) for i in range(2)]
        w_in, made, taken, weighed, normed, high_in = (s.sem(x) for x in ("w_in", "made", "taken", "weighed", "normed", "high_in"))
        cols_in, rows_in, rows_used, ready, chain = (s.sem(x) for x in ("cols_in", "rows_in", "rows_used", "ready", "chain"))
        trash_in, ones_in, landed = (s.sem(x) for x in ("trash_in", "ones_in", "landed"))
        put_w, put_c = g.put_w, g.put_c
        QS = HD ** -0.5 / 2
        CHUNKED = CHUNKS // 2
        assert CHUNKED == PAIRS - 1

        def halves(h):
            return slice(64 * h, 64 * h + 64), slice(64 - 64 * h, 128 - 64 * h)

        block = ctx.enter_context(nc.Block())

        @block.sync
        def _(sp):
            sp.dma_start(w[:], g.mix0_w[0]).then_inc(w_in, 16)
            sp.dma_start(key_cols[:], g.edge_cols).then_inc(cols_in, 16)

            def load_rows(c):
                for n in range(2):
                    sp.dma_start(rows_i[:, n, :], bass.AP(g.edge_rows.tensor, c * CW + n * PADDED, [[0, P], [1, CW]])
                                 ).then_inc(rows_in, 16)
                sp.dma_start(rows_w[:], bass.AP(g.edge_w.tensor, c * CW, [[0, P], [1, CW]])).then_inc(rows_in, 16)

            load_rows(0)
            def load_next(i):
                sp.wait_ge(rows_used, i * 2 + 1)
                load_rows(i * 2 + 1)
                sp.wait_ge(made, i * NEV + 6 + T)
                sp.dma_start(w[:], g.mix0_w[bass.ds(i + 1, 1)].rearrange("o p k f -> (o p) k f")).then_inc(w_in, 16)

            with sp.Fori(0, CHUNKED - 1) as i:
                load_next(i)
                sp.wait_ge(rows_used, i * 2 + 2)
                load_rows(i * 2 + 2)
            load_next(CHUNKED - 1)

        @block.tensor
        def _(pe):
            for count in (weighed,):
                pe.sem_inc(count, 1)
            pe.wait_ge(ones_in, 1)
            with pe.Fori(0, PAIRS) as i:
                pe.wait_ge(w_in, i * 16 + 16)

                def room(n):
                    pe.wait_ge(taken, ONE + i * NEV + max(n - 3, 0))

                n = 0
                for m in range(2):
                    for c0, cn in CH:
                        room(n)
                        for k in range(KC):
                            last = nc.tensor.matmul(ring[n % 4][:, 0:cn], w[:, k, m * 128:(m + 1) * 128],
                                                    g.XT[:, k, c0:c0 + cn], start=(k == 0), stop=(k == KC - 1))
                        last.then_inc(made, 1)
                        n += 1
                for t in range(T):
                    room(n)
                    for k in range(KC):
                        last = nc.tensor.matmul(ring[n % 4][0:P, 0:128], g.XT[:, k, t * P:(t + 1) * P],
                                                w[:, k, 256:384], start=(k == 0), stop=(k == KC - 1))
                    last.then_inc(made, 1)
                    n += 1

                def score(m):
                    h, c, j = m // (3 * T), m // T % 3, m % T
                    c0, cn = CH[c]
                    if m == 0:
                        pe.wait_ge(taken, ONE + i * NEV + 6 + T)
                    else:
                        room(6 + T + m)
                    for part in range(2):
                        last = nc.tensor.matmul(ring[(6 + T + m) % 4][0:P, 0:cn], k2[:, h, j * P:(j + 1) * P],
                                                q2[:, part, h, c0:c0 + cn], start=(part == 0), stop=(part == 1))
                    last.then_inc(made, 1)

                def weigh(m):
                    h, c, j = m // (3 * T), m // T % 3, m % T
                    cn = CH[c][1]
                    if j == 0:
                        pe.wait_ge(normed, ONE + i * 6 + max(m // T - 1, 0))
                    pe.wait_ge(taken, ONE + i * NEV + 6 + T + m + 1)
                    nc.tensor.matmul(out[m // T % 2][:, 0:cn], v1[:, j, h, :], attn[:, m % 4, 0:cn],
                                     start=(j == 0), stop=(j == T - 1)).then_inc(weighed, 1)

                for m in range(NSCORE + 2):
                    if m < NSCORE:
                        score(m)
                    if m >= 2:
                        weigh(m - 2)

        @block.scalar
        def _(act):
            for count in (taken,):
                act.sem_inc(count, 1)
            with act.Fori(0, PAIRS) as i:
                n = 0
                for m in range(2):
                    for c0, cn in CH:
                        act.wait_ge(made, i * NEV + n + 1)
                        for h in range(2):
                            own, other = halves(h)
                            src = ring[n % 4][own, 0:cn]
                            if m == 0:
                                nc.scalar.activation(q2[other, 0, h, c0:c0 + cn], src, ACT.Copy, scale=QS)
                                last = nc.scalar.activation(q2[own, 0, h, c0:c0 + cn], src, ACT.Copy, scale=QS)
                            else:
                                last = nc.scalar.activation(k2[own, h, c0:c0 + cn], src, ACT.Copy)
                        last.then_inc(high_in, 1)
                        n += 1
                act.wait_ge(taken, ONE + i * NEV + 6)
                for t in range(T):
                    act.wait_ge(made, i * NEV + n + 1)
                    nc.scalar.activation(v1[:, t, 0, 0:64], ring[n % 4][0:P, 0:64], ACT.Copy)
                    nc.scalar.activation(v1[:, t, 1, 64:128], ring[n % 4][0:P, 64:128], ACT.Copy).then_inc(taken, 1)
                    n += 1
                for m in range(NSCORE):
                    cn = CH[m // T % 3][1]
                    act.wait_ge(made, i * NEV + n + 1)
                    act.wait_ge(weighed, ONE + i * NSCORE + max(m - 3, 0))
                    nc.scalar.activation(attn[:, m % 4, 0:cn], ring[n % 4][0:P, 0:cn], ACT.Relu,
                                         bias=g.two[0:P, :]).then_inc(taken, 1)
                    n += 1

        @block.vector
        def _(dve):
            for count in (normed,):
                dve.sem_inc(count, 1)
            nc.vector.memset(v1[:, :, 0, 64:128], 1.0)
            nc.vector.memset(v1[:, :, 1, 0:64], 1.0).then_inc(ones_in, 1)
            dve.wait_ge(cols_in, 16)
            dve.wait_ge(trash_in, 1)
            first = Chain(dve, chain)
            nc.vector.tensor_copy(trash[:], trash_i[:])
            first(nc.vector.scalar_tensor_tensor(keys[:], key_cols[:, 0, :], float(N), key_cols[:, 1, :],
                                                 ALU.mult, ALU.add))
            LINKS = 2 * 7 + 6

            def pair(i, chunks):
                step = Chain(dve, chain, 1 + i * LINKS)

                def chunk(b):
                    cols = keys[:, bass.ds((i * 2 + b) * GPC, GPC)]
                    rows = lambda a: a[:].rearrange("p (g e) -> p g e", g=GPC)
                    dve.wait_ge(rows_in, i * 96 + 48 * (b + 1))
                    step(nc.vector.scalar_tensor_tensor(key_row[:], rows_i[:, 0, :], float(N), rows_i[:, 1, :],
                                                        ALU.mult, ALU.add))
                    step(nc.vector.tensor_tensor(rows(same), rows(key_row),
                                                 cols.unsqueeze(2).broadcast_to([P, GPC, P]), ALU.is_equal))
                    step(nc.vector.tensor_tensor(part[:], same[:], rows_w[:], ALU.mult))
                    dve.wait_ge(landed, i * 4 * GPC + b * 2 * GPC + 2)
                    nc.vector.tensor_reduce(val_w[:, b, :], rows(part), AX, ALU.add).then_inc(rows_used, 1)
                    step(nc.vector.tensor_reduce(val_c[:, b, :], rows(same), AX, ALU.add))
                    step(nc.vector.tensor_tensor(rows(part), rows(same),
                                                 g.lower[:].unsqueeze(1).broadcast_to([P, GPC, P]), ALU.mult))
                    nc.vector.tensor_scalar(away[:], cols, trash[:, 0:1], -1.0, ALU.subtract, ALU.mult)
                    step(nc.vector.tensor_reduce(dup[:], rows(part), AX, ALU.max))
                    step(nc.vector.tensor_tensor(away[:], away[:], dup[:], ALU.mult))
                    nc.vector.tensor_tensor(idx[:, b, :], away[:], cols, ALU.add).then_inc(ready, 1)

                def norm(hc):
                    h, (c0, cn) = hc // 3, CH[hc % 3]
                    num, den = halves(h)
                    dve.wait_ge(weighed, ONE + i * NSCORE + T * (hc + 1))
                    step(nc.vector.reciprocal(rden[num, hc % 2, 0:cn], out[hc % 2][den, 0:cn]))
                    dve.wait_ge(g.zeroed, ZEROED)
                    nc.vector.tensor_tensor(g.OT[num, bass.ds(i, 1), c0:c0 + cn].rearrange("p o c -> p (o c)"),
                                            out[hc % 2][num, 0:cn], rden[num, hc % 2, 0:cn], ALU.mult).then_inc(normed, 1)

                dve.wait_ge(taken, ONE + i * NEV)
                for n in range(6):
                    m, c = divmod(n, 3)
                    c0, cn = CH[c]
                    dve.wait_ge(high_in, i * 6 + n + 1)
                    for h in range(2):
                        own, other = halves(h)
                        src = ring[n % 4][own, 0:cn]
                        if m == 0:
                            high = q2[own, 0, h, c0:c0 + cn].bitcast(F32)
                            for rows_ in (own, other):
                                last = nc.vector.scalar_tensor_tensor(q2[rows_, 1, h, c0:c0 + cn], src, QS, high,
                                                                      ALU.mult, ALU.subtract)
                        else:
                            last = nc.vector.tensor_tensor(k2[other, h, c0:c0 + cn], src,
                                                           k2[own, h, c0:c0 + cn].bitcast(F32), ALU.subtract)
                    last.then_inc(taken, 1)
                if chunks:
                    chunk(0)
                norm(0)
                norm(1)
                if chunks:
                    chunk(1)
                for hc in range(2, 6):
                    norm(hc)
                assert step.n == (LINKS if chunks else 6), step.n

            with dve.Fori(0, CHUNKED) as i:
                pair(i, True)
            pair(CHUNKED, False)

        @block.gpsimd
        def _(pool):
            nc.gpsimd.iota(trash_i[:], pattern=[[0, 1]], base=TRASH, channel_multiplier=1).then_inc(trash_in, 1)
            pool.wait_ge(g.zeroed, ZEROED)
            pool.dma_start(g.ew_table[MAIN:TABLE].rearrange("(a n) o -> a (n o)", a=1), g.zero_tail[:]).then_inc(put_w, 16)
            pool.dma_start(g.cnt_table[MAIN:TABLE].rearrange("(a n) o -> a (n o)", a=1), g.zero_tail[:]).then_inc(put_c, 16)
            pool.sem_inc(landed, 2 * GPC)
            with pool.Fori(0, CHUNKED) as i:
                for b in range(2):
                    pool.wait_ge(ready, i * 2 + b + 1)
                    for n in range(GPC):
                        done = 16 + (i * 2 * GPC + b * GPC + n) * 16
                        cell = bass.IndirectOffsetOnAxis(ap=idx[:, b, n:n + 1], axis=0)
                        for table, val, put in ((g.ew_table, val_w, put_w), (g.cnt_table, val_c, put_c)):
                            pool.wait_ge(put, done)
                            pool.sem_inc(landed, 1)
                            pool.indirect_dma_start(out=table, out_offset=cell, in_=val[:, b, n:n + 1], in_offset=None,
                                                    compute_op=ALU.add).then_inc(put, 16)
            pool.wait_ge(put_w, 16 + GROUPS * 16)
            pool.wait_ge(put_c, 16 + GROUPS * 16)


def stage_clear(nc, g):
    done = sorted(SEMAPHORES)
    with ExitStack() as ctx:
        block = ctx.enter_context(nc.Block())

        @block.gpsimd
        def _(pool):
            pool.sem_clear(range(done[0], done[-1] + 1))


def stage_tok_linear(nc, g, name, src, w_dram, bias):
    with ExitStack() as ctx:
        s = Scope(nc, ctx, name)
        w, b = s.sb("w", [128, KC, D]), s.sb("b", [P, D])
        w_high, w_low = s.sb("w_high", [128, KC, D], F32R), s.sb("w_low", [128, KC, D], F32R)
        high, low = s.sb("high", [128, 3, KC, P + 1], F32R), s.sb("low", [128, 3, KC, P + 1], F32R)
        acc = [s.ps(f"acc{i}", [P, 512]) for i in range(4)]
        w_in, b_in, biased, made, added = (s.sem(x) for x in ("w_in", "b_in", "biased", "made", "added"))
        w_high_in, w_low_in, high_in, low_in = (s.sem(x) for x in ("w_high_in", "w_low_in", "high_in", "low_in"))
        block = ctx.enter_context(nc.Block())

        @block.sync
        def _(sp):
            sp.dma_start(w[:], w_dram.rearrange("(k p) m -> p k m", p=128)).then_inc(w_in, 16)
            sp.dma_start(b[:], bcast_rows(bias, P, D)).then_inc(b_in, 16)

        @block.tensor
        def _(pe):
            for n in range(2 * T):
                t, h = divmod(n, 2)
                if h == 0:
                    pe.wait_ge(high_in, t + 1)
                    pe.wait_ge(low_in, t + 1)
                if n >= 4:
                    pe.wait_ge(added, n - 3)
                for k in range(KC):
                    if n == 0:
                        pe.wait_ge(w_high_in, k + 1)
                        pe.wait_ge(w_low_in, k + 1)
                    cols = slice(h * HALF, (h + 1) * HALF)
                    for m, (x, y) in enumerate(((high, w_high), (high, w_low), (low, w_high))):
                        last = nc.tensor.matmul(acc[n % 4][:, 0:HALF], x[:, t % 3, k, 0:P], y[:, k, cols],
                                                start=(k + m == 0), stop=(k == KC - 1 and m == 2))
                last.then_inc(made, 1)

        @block.scalar
        def _(act):
            def take(t):
                if t >= 3:
                    act.wait_ge(made, 2 * (t - 2))
                nc.scalar.activation(high[:, t % 3, :, 0:P], src[:, :, t * P:(t + 1) * P], ACT.Copy).then_inc(high_in, 1)

            for t in range(2):
                take(t)
            act.wait_ge(w_in, 16)
            for k in range(KC):
                nc.scalar.activation(w_high[:, k, :], w[:, k, :], ACT.Copy).then_inc(w_high_in, 1)
            for t in range(2, T):
                take(t)

        @block.vector
        def _(dve):
            def take(t):
                if t >= 3:
                    dve.wait_ge(made, 2 * (t - 2))
                dve.wait_ge(high_in, t + 1)
                nc.vector.tensor_tensor(low[:, t % 3, :, 0:P], src[:, :, t * P:(t + 1) * P],
                                        high[:, t % 3, :, 0:P].bitcast(F32), ALU.subtract).then_inc(low_in, 1)

            for t in range(2):
                take(t)
            for k in range(KC):
                dve.wait_ge(w_high_in, k + 1)
                nc.vector.tensor_tensor(w_low[:, k, :], w[:, k, :], w_high[:, k, :].bitcast(F32), ALU.subtract).then_inc(w_low_in, 1)
            take(2)
            dve.wait_ge(b_in, 16)
            nc.vector.tensor_tensor(g.X[:], g.X[:], b[:].unsqueeze(1).broadcast_to([P, T, D]), ALU.add).then_inc(biased, 1)
            dve.wait_ge(biased, 1)
            for n in range(2 * T):
                t, h = divmod(n, 2)
                dve.wait_ge(made, n + 1)
                x = g.X[:, t, h * HALF:(h + 1) * HALF]
                nc.vector.tensor_tensor(x, acc[n % 4][:, 0:HALF], x, ALU.add).then_inc(added, 1)
                if h == 1 and t + 3 < T:
                    take(t + 3)


def stage_gcn(nc, g):
    H = 256
    R = 24
    with ExitStack() as ctx:
        s = Scope(nc, ctx, "gcn")
        A = s.sb("A", [P, T, N])
        wd, wu, w1, w2 = s.sb("wd", [128, KC, R]), s.sb("wu", [R, D]), s.sb("w1", [128, KC, H]), s.sb("w2", [128, 2, D])
        bd, bu, b1, b2 = s.sb("bd", [R, 1]), s.sb("bu", [128, KC]), s.sb("b1", [P, H]), s.sb("b2", [P, D])
        down = s.sb("down", [R, N])
        h1, h2, sumT = s.sb("h1", [P, T, H]), s.sb("h2", [P, T, H]), s.sb("sumT", [128, 2, N])
        act_in = s.sb("act_in", [P, 2, H])
        deg, std, dinv = s.sb("deg", [P, N]), s.sb("std", [P, T]), s.sb("dinv", [P, T])
        uT = g.OT
        ring = [s.ps(f"ring{i}", [128, 512]) for i in range(4)]
        deg_ps = s.ps("deg_ps", [P, 512])
        A_in, wd_in, wu_in, w1_in, w2_in, b_in = (s.sem(x) for x in ("A_in", "wd_in", "wu_in", "w1_in", "w2_in", "b_in"))
        made, taken, h1_in, h2_in = (s.sem(x) for x in ("made", "taken", "h1_in", "h2_in"))
        chain, deg_in, degs, std_in, dinv_in, biased = (s.sem(x) for x in ("chain", "deg_in", "degs", "std_in", "dinv_in", "biased"))
        block = ctx.enter_context(nc.Block())
        D0 = 3
        U0 = D0 + 3 * KC
        H1 = U0 + T
        H2 = H1 + T
        S0 = H2 + 6

        @block.sync
        def _(sp):
            sp.dma_start(wd[:], g.gcn_wd.rearrange("(k p) m -> p k m", p=128)).then_inc(wd_in, 16)
            sp.dma_start(bd[:], g.gcn_bd).then_inc(b_in, 16)
            sp.dma_start(wu[:], g.gcn_wu).then_inc(wu_in, 16)
            sp.dma_start(bu[:], g.gcn_bu).then_inc(b_in, 16)
            sp.dma_start(w1[:], g.gcn_w1.rearrange("(k p) m -> p k m", p=128)).then_inc(w1_in, 16)
            sp.dma_start(b1[:], bcast_rows(g.gcn_b1, P, H)).then_inc(b_in, 16)
            sp.dma_start(b2[:], bcast_rows(g.gcn_b2, P, D)).then_inc(b_in, 16)
            sp.dma_start(A[:], g.ew_table[0:N * N].rearrange("(t p d) o -> p t (d o)", p=P, d=N)).then_inc(A_in, 16)
            sp.dma_start(w2[:], g.gcn_w2.rearrange("(k p) m -> p k m", p=128)).then_inc(w2_in, 16)

        @block.tensor
        def _(pe):
            n = [0]

            def tile(rows, cols):
                if n[0] >= 4:
                    pe.wait_ge(taken, n[0] - 3)
                return ring[n[0] % 4][0:rows, 0:cols]

            def done(ins):
                ins.then_inc(made, 1)
                n[0] += 1

            pe.wait_ge(wd_in, 16)
            for c0, cn in CH:
                o = tile(R, cn)
                for k in range(KC):
                    last = nc.tensor.matmul(o, wd[:, k, :], g.XT[:, k, c0:c0 + cn], start=(k == 0), stop=(k == KC - 1))
                done(last)
            pe.wait_ge(wu_in, 16)
            pe.wait_ge(taken, D0)
            for m in range(KC):
                for c0, cn in CH:
                    done(nc.tensor.matmul(tile(128, cn), wu[:, m * 128:(m + 1) * 128], down[:, c0:c0 + cn],
                                          start=True, stop=True))
            pe.wait_ge(w1_in, 16)
            pe.wait_ge(taken, U0)
            for t in range(T):
                o = tile(P, H)
                for k in range(KC):
                    last = nc.tensor.matmul(o, uT[:, k, t * P:(t + 1) * P], w1[:, k, :], start=(k == 0), stop=(k == KC - 1))
                done(last)
            pe.wait_ge(deg_in, 1)
            for t in range(T):
                last = nc.tensor.matmul(deg_ps[:, t:t + 1], deg[:, t * P:(t + 1) * P], g.ones[0:P, 0:1],
                                        start=True, stop=True)
            last.then_inc(degs, 1)
            pe.wait_ge(h1_in, T)
            for d in range(T):
                o = tile(P, H)
                for j in range(T):
                    last = nc.tensor.matmul(o, A[:, j, d * P:(d + 1) * P], h1[:, j, :], start=(j == 0), stop=(j == T - 1))
                done(last)
            pe.wait_ge(h2_in, T)
            for f in range(2):
                for c0, cn in CH:
                    o = tile(128, cn)
                    for j in range(T):
                        last = nc.tensor.matmul(o, h2[:, j, f * 128:(f + 1) * 128], A[:, j, c0:c0 + cn],
                                                start=(j == 0), stop=(j == T - 1))
                    done(last)
            pe.wait_ge(w2_in, 16)
            pe.wait_ge(taken, S0)
            for t in range(T):
                for h in range(2):
                    o = tile(P, HALF)
                    for k in range(2):
                        last = nc.tensor.matmul(o, sumT[:, k, t * P:(t + 1) * P], w2[:, k, h * HALF:(h + 1) * HALF],
                                                start=(k == 0), stop=(k == 1))
                    done(last)

        @block.scalar
        def _(act):
            act.wait_ge(b_in, 4 * 16)
            for n, (c0, cn) in enumerate(CH):
                act.wait_ge(made, n + 1)
                nc.scalar.activation(down[:, c0:c0 + cn], ring[n % 4][0:R, 0:cn], ACT.Relu, bias=bd[:]).then_inc(taken, 1)
            act.wait_ge(degs, 1)
            nc.scalar.activation(std[:], deg_ps[:, 0:T], ACT.Sqrt).then_inc(std_in, 1)
            for f in range(6):
                n = H2 + f
                c0, cn = CH[f % 3]
                act.wait_ge(made, n + 1)
                act.wait_ge(taken, n)
                nc.scalar.activation(sumT[:, f // 3, c0:c0 + cn], ring[n % 4][:, 0:cn], ACT.Copy).then_inc(taken, 1)

        @block.vector
        def _(dve):
            step = Chain(dve, chain)
            dve.wait_ge(taken, D0)
            dve.wait_ge(b_in, 4 * 16)
            for n in range(D0, U0):
                m, c = divmod(n - D0, 3)
                c0, cn = CH[c]
                dve.wait_ge(made, n + 1)
                nc.vector.scalar_tensor_tensor(uT[:, m, c0:c0 + cn], ring[n % 4][:, 0:cn], bu[:, m:m + 1],
                                               g.XT[:, m, c0:c0 + cn], ALU.add, ALU.add).then_inc(taken, 1)
            dve.wait_ge(A_in, 16)
            for t in range(T):
                last = nc.vector.tensor_tensor(A[:, t, t * P:(t + 1) * P], A[:, t, t * P:(t + 1) * P],
                                               g.ident[0:P, 0:P], ALU.add)
            step(last)
            nc.vector.tensor_reduce(deg[:], A[:].rearrange("p t d -> p d t"), AX, ALU.add).then_inc(deg_in, 1)
            for n in range(U0, H1):
                dve.wait_ge(made, n + 1)
                nc.vector.tensor_copy(h1[:, n - U0, :], ring[n % 4][0:P, 0:H]).then_inc(taken, 1)
            dve.wait_ge(std_in, 1)
            step(nc.vector.reciprocal(dinv[:], std[:]))
            dve.wait_ge(taken, H1)
            for t in range(T):
                nc.vector.tensor_scalar(h1[:, t, :], h1[:, t, :], dinv[:, t:t + 1], None, ALU.mult).then_inc(h1_in, 1)
            nc.vector.tensor_tensor(g.X[:], g.X[:], b2[:].unsqueeze(1).broadcast_to([P, T, D]), ALU.add).then_inc(biased, 1)
            for n in range(H1, H2):
                d = n - H1
                dve.wait_ge(made, n + 1)
                nc.vector.scalar_tensor_tensor(act_in[:, d % 2, :], ring[n % 4][0:P, 0:H], dinv[:, d:d + 1], b1[:],
                                               ALU.mult, ALU.add).then_inc(taken, 1)
                dve.wait_ge(taken, n + 1)
                nc.vector.tensor_scalar(h2[:, d, :], act_in[:, d % 2, :], 0.0, dinv[:, d:d + 1], ALU.max, ALU.mult).then_inc(h2_in, 1)
            dve.wait_ge(biased, 1)
            for n in range(S0, S0 + 2 * T):
                t, h = divmod(n - S0, 2)
                dve.wait_ge(made, n + 1)
                x = g.X[:, t, h * HALF:(h + 1) * HALF]
                nc.vector.scalar_tensor_tensor(x, ring[n % 4][0:P, 0:HALF], dinv[:, t:t + 1], x, ALU.mult, ALU.add).then_inc(taken, 1)


def stage_gate(nc, g):
    with ExitStack() as ctx:
        s = Scope(nc, ctx, "gate")
        w1, w2, b1, b2 = s.sb("w1", [128, KC, 32]), s.sb("w2", [32, E0]), s.sb("b1", [32, 1]), s.sb("b2", [P, E0])
        hT = s.sb("hT", [32, N])
        z, ez = s.sb("z", [P, T, E0]), s.sb("ez", [P, T, E0])
        col = s.sb("col", [P, T])
        cmp_, same = s.sb("cmp", [P, T, E0, E0]), s.sb("same", [P, T, E0, E0])
        ps = [s.ps(f"ps{i}", [128, 512]) for i in range(3)]
        logits = s.ps("logits", [P, 512])
        w_in, made, h_in, logits_in, chain, asked, answered = (s.sem(x) for x in ("w_in", "made", "h_in", "logits_in", "chain", "asked", "answered"))
        block = ctx.enter_context(nc.Block())

        @block.sync
        def _(sp):
            sp.dma_start(w1[:], g.gate_w1.rearrange("(k p) m -> p k m", p=128)).then_inc(w_in, 16)
            sp.dma_start(w2[:], g.gate_w2).then_inc(w_in, 16)
            sp.dma_start(b1[:], g.gate_b1).then_inc(w_in, 16)
            sp.dma_start(b2[:], bcast_rows(g.gate_b2, P, E0)).then_inc(w_in, 16)

        @block.tensor
        def _(pe):
            pe.wait_ge(w_in, 64)
            for c, (c0, cn) in enumerate(CH):
                for k in range(KC):
                    last = nc.tensor.matmul(ps[c][0:32, 0:cn], w1[:, k, :], g.XT[:, k, c0:c0 + cn],
                                            start=(k == 0), stop=(k == KC - 1))
                last.then_inc(made, 1)
            pe.wait_ge(h_in, 3)
            for t in range(T):
                last = nc.tensor.matmul(logits[:, t * E0:(t + 1) * E0], hT[:, t * P:(t + 1) * P], w2[:], start=True, stop=True)
            last.then_inc(logits_in, 1)

        @block.scalar
        def _(act):
            for c, (c0, cn) in enumerate(CH):
                act.wait_ge(made, c + 1)
                nc.scalar.activation(hT[:, c0:c0 + cn], ps[c][0:32, 0:cn], ACT.Relu, bias=b1[:]).then_inc(h_in, 1)
            for r in range(2):
                act.wait_ge(asked, r + 1)
                nc.scalar.activation(ez[:], z[:], ACT.Exp).then_inc(answered, 1)

        @block.vector
        def _(dve):
            step = Chain(dve, chain)
            per_token = col[:].unsqueeze(2).broadcast_to([P, T, E0])
            dve.wait_ge(logits_in, 1)
            step(nc.vector.tensor_tensor(z[:], logits[:, 0:T * E0].rearrange("p (t e) -> p t e", e=E0),
                                         b2[:].unsqueeze(1).broadcast_to([P, T, E0]), ALU.add))
            step(nc.vector.tensor_reduce(col[:], z[:], AX, ALU.max))
            nc.vector.tensor_tensor(z[:], z[:], per_token, ALU.subtract).then_inc(asked, 1)
            dve.wait_ge(answered, 1)
            step(nc.vector.tensor_reduce(col[:], ez[:], AX, ALU.add))
            step(nc.vector.reciprocal(col[:], col[:]))
            step(nc.vector.tensor_tensor(z[:], ez[:], per_token, ALU.mult))
            rank_of(nc, g, step, z, cmp_, same, g.gate, E0)
            step(nc.vector.tensor_scalar(g.gate[:], g.gate[:], 1.5, None, ALU.is_lt))
            step(nc.vector.tensor_reduce(col[:], z[:], AX, ALU.max))
            nc.vector.tensor_tensor(z[:], z[:], per_token, ALU.subtract).then_inc(asked, 1)
            dve.wait_ge(answered, 2)
            step(nc.vector.tensor_tensor(g.gate[:], g.gate[:], ez[:], ALU.mult))
            step(nc.vector.tensor_reduce(col[:], g.gate[:], AX, ALU.add))
            step(nc.vector.reciprocal(col[:], col[:]))
            step(nc.vector.tensor_tensor(g.gate[:], g.gate[:], per_token, ALU.mult))


def rank_of(nc, g, step, z, cmp_, same, rank, E):
    shape = [P, T, E, E]
    other, own = z[:].unsqueeze(2).broadcast_to(shape), z[:].unsqueeze(3).broadcast_to(shape)
    nc.vector.tensor_tensor(cmp_[:], other, own, ALU.is_gt)
    step(nc.vector.tensor_tensor(same[:], other, own, ALU.is_equal))
    before = {E0: g.before3, E1: g.before8}[E][:].rearrange("p (a b) -> p a b", a=E).unsqueeze(1).broadcast_to(shape)
    step(nc.vector.tensor_tensor(same[:], same[:], before, ALU.mult))
    step(nc.vector.tensor_tensor(cmp_[:], cmp_[:], same[:], ALU.add))
    step(nc.vector.tensor_reduce(rank[:], cmp_[:], AX, ALU.add))


def stage_experts0(nc, g):
    SC = HE ** -0.5
    KCH = [(0, 512), (512, 512), (1024, N - 1024)]
    with ExitStack() as ctx:
        s = Scope(nc, ctx, "exp0")
        w, par, bv = s.sb("w", [128, KC, 3 * HE]), s.sb("par", [128, 12]), s.sb("bv", [P, HE])
        q, qc = s.sb("q", [128, 2, N + 2]), s.sb("qc", [128, 2, N])
        kT, v = s.sb("kT", [128, 2, N]), s.sb("v", [P, T, HE])
        prob, probT = s.sb("prob", [P, 2, N]), s.sb("probT", [P, T, P])
        mx, nmx, total, r = s.sb("mx", [P, T]), s.sb("nmx", [P, T]), s.sb("total", [P, T]), s.sb("r", [P, T])
        score = s.ps("score", [P, 3 * 512])
        flip = [s.ps(f"flip{i}", [128, 512]) for i in range(3)]
        y = [s.ps(f"y{i}", [128, 512]) for i in range(2)]
        PROJ = 12 + T
        names = "w_in made taken scored masked probs scaled flipped unflipped summed stored chain q_in conv_in edges b_in"
        (w_in, made, taken, scored, masked, probs, scaled, flipped, unflipped, summed, stored, chain, q_in, conv_in,
         edges, b_in) = (s.sem(x) for x in names.split())
        NF = sum(-(-(t + 1) // 4) for t in range(T))
        ring = [flip[0], flip[1], flip[2], y[0]]
        block = ctx.enter_context(nc.Block())

        @block.sync
        def _(sp):
            sp.dma_start(w[:], g.exp0_w[0]).then_inc(w_in, 16)
            sp.dma_start(par[:], g.exp0_par[0]).then_inc(b_in, 16)
            sp.dma_start(bv[:], bass.AP(g.exp0_bv.tensor, 0, [[0, P], [1, HE]])).then_inc(b_in, 16)
            with sp.Fori(0, E0 - 1) as e:
                sp.wait_ge(taken, ONE + e * PROJ + PROJ)
                sp.dma_start(w[:], g.exp0_w[bass.ds(e + 1, 1)].rearrange("o p k f -> (o p) k f")).then_inc(w_in, 16)
                sp.wait_ge(conv_in, e * 2 + 2)
                sp.dma_start(par[:], g.exp0_par[bass.ds(e + 1, 1)].rearrange("o p f -> (o p) f")).then_inc(b_in, 16)
                sp.dma_start(bv[:], g.exp0_bv[bass.ds(e + 1, 1)].broadcast_to([P, HE])).then_inc(b_in, 16)

        @block.tensor
        def _(pe):
            for count in (summed, flipped):
                pe.sem_inc(count, 1)
            with pe.Fori(0, E0) as e:
                pe.wait_ge(w_in, e * 16 + 16)
                pe.wait_ge(stored, ONE + e * 2 * T)
                pe.wait_ge(unflipped, ONE + e * NF)
                n = 0

                def room():
                    pe.wait_ge(taken, ONE + e * PROJ + max(n - 3, 0))

                for m in range(4):
                    for c0, cn in CH:
                        room()
                        for k in range(KC):
                            last = nc.tensor.matmul(ring[n % 4][:, 0:cn],
                                                    w[:, k, m * 128:(m + 1) * 128], g.XT[:, k, c0:c0 + cn],
                                                    start=(k == 0), stop=(k == KC - 1))
                        last.then_inc(made, 1)
                        n += 1
                for t in range(T):
                    room()
                    for k in range(KC):
                        last = nc.tensor.matmul(ring[n % 4][0:P, 0:HE], g.XT[:, k, t * P:(t + 1) * P], w[:, k, 2 * HE:3 * HE],
                                                start=(k == 0), stop=(k == KC - 1))
                    last.then_inc(made, 1)
                    n += 1
                pe.wait_ge(taken, ONE + e * PROJ + PROJ)
                pe.wait_ge(conv_in, e * 2 + 2)

                def scores(t):
                    pe.wait_ge(probs, ONE + e * T + t)
                    for c0, cn in KCH:
                        cn = min(cn, (t + 1) * P - c0)
                        if cn <= 0:
                            continue
                        for m in range(2):
                            last = nc.tensor.matmul(score[:, c0:c0 + cn], qc[:, m, t * P:(t + 1) * P], kT[:, m, c0:c0 + cn],
                                                    start=(m == 0), stop=(m == 1))
                    last.then_inc(scored, 1)

                nf = 0
                scores(0)
                for t in range(T):
                    if t + 1 < T:
                        scores(t + 1)
                    pe.wait_ge(scaled, e * T + t + 1)
                    for j0 in range(0, t + 1, 4):
                        js = range(j0, min(j0 + 4, t + 1))
                        pe.wait_ge(unflipped, ONE + e * NF + max(nf - 2, 0))
                        for j in js:
                            last = nc.tensor.transpose(flip[nf % 3][0:P, (j - j0) * P:(j - j0 + 1) * P],
                                                       prob[:, t % 2, j * P:(j + 1) * P], g.ident[0:P, 0:P])
                        last.then_inc(flipped, 1)
                        nf += 1
                    pe.wait_ge(unflipped, ONE + e * NF + nf)
                    pe.wait_ge(stored, ONE + e * 2 * T + 2 * t)
                    for m in range(2):
                        for j in range(t + 1):
                            last = nc.tensor.matmul(y[m][:, 0:P], v[:, j, m * 128:(m + 1) * 128], probT[:, j, :],
                                                    start=(j == 0), stop=(j == t))
                        last.then_inc(summed, 1)
                assert nf == NF

        @block.scalar
        def _(act):
            for count in (stored, taken, probs):
                act.sem_inc(count, 1)
            def put_y(e, t, m):
                act.wait_ge(summed, ONE + e * 2 * T + 2 * t + m + 1)
                nc.scalar.activation(g.OT[:, bass.ds(e * 2 + m, 1), t * P:(t + 1) * P].rearrange("p o c -> p (o c)"),
                                     y[m][:, 0:P], ACT.Copy).then_inc(stored, 1)

            act.wait_ge(edges, 1)
            with act.Fori(0, E0) as e:
                act.wait_ge(b_in, e * 32 + 32)
                for n in range(12):
                    m, c = divmod(n, 3)
                    c0, cn = CH[c]
                    act.wait_ge(made, e * PROJ + n + 1)
                    dst = q[:, m, 1 + c0:1 + c0 + cn] if m < 2 else kT[:, m - 2, c0:c0 + cn]
                    nc.scalar.activation(dst, ring[n % 4][:, 0:cn], ACT.Identity, bias=par[:, m:m + 1]).then_inc(taken, 1)
                for t in range(T):
                    act.wait_ge(masked, e * T + t + 1)
                    act.wait_ge(flipped, ONE + e * NF + sum(-(-(u + 1) // 4) for u in range(t - 1)))
                    nc.scalar.activation(prob[:, t % 2, 0:(t + 1) * P], score[:, 0:(t + 1) * P], ACT.Exp,
                                         bias=nmx[:, t:t + 1], scale=SC, accum_out=total[:, t:t + 1]).then_inc(probs, 1)
                    for m in range(2):
                        if t:
                            put_y(e, t - 1, m)
                for m in range(2):
                    put_y(e, T - 1, m)

        @block.vector
        def _(dve):
            for count in (unflipped,):
                dve.sem_inc(count, 1)
            nc.vector.memset(q[:, :, 0:1], 0.0)
            nc.vector.memset(q[:, :, N + 1:N + 2], 0.0).then_inc(edges, 1)
            LINKS = 4 + T * 4
            with dve.Fori(0, E0) as e:
                step = Chain(dve, chain, e * LINKS)
                dve.wait_ge(b_in, e * 32 + 32)
                dve.wait_ge(taken, ONE + e * PROJ + 12)
                for n in range(12, PROJ):
                    dve.wait_ge(made, e * PROJ + n + 1)
                    nc.vector.tensor_tensor(v[:, n - 12, :], ring[n % 4][0:P, 0:HE], bv[:], ALU.add).then_inc(taken, 1)
                for m in range(2):
                    step(nc.vector.tensor_scalar(qc[:, m, :], q[:, m, 0:N], par[:, 4 + m:5 + m], par[:, 10 + m:11 + m],
                                                 ALU.mult, ALU.add))
                    step(nc.vector.scalar_tensor_tensor(qc[:, m, :], q[:, m, 1:N + 1], par[:, 6 + m:7 + m], qc[:, m, :],
                                                        ALU.mult, ALU.add))
                    nc.vector.scalar_tensor_tensor(qc[:, m, :], q[:, m, 2:N + 2], par[:, 8 + m:9 + m], qc[:, m, :],
                                                   ALU.mult, ALU.add).then_inc(conv_in, 1)
                nf = 0

                def top(t):
                    n = (t + 1) * P
                    dve.wait_ge(scored, e * T + t + 1)
                    step(nc.vector.tensor_tensor(score[:, t * P:n], score[:, t * P:n], g.causal[:], ALU.add))
                    step(nc.vector.tensor_reduce(mx[:, t:t + 1], score[:, 0:n], AX, ALU.max))
                    nc.vector.tensor_scalar(nmx[:, t:t + 1], mx[:, t:t + 1], -SC, None, ALU.mult).then_inc(masked, 1)

                top(0)
                for t in range(T):
                    n = (t + 1) * P
                    dve.wait_ge(probs, ONE + e * T + t + 1)
                    step(nc.vector.reciprocal(r[:, t:t + 1], total[:, t:t + 1]))
                    step(nc.vector.tensor_tensor(r[:, t:t + 1], r[:, t:t + 1],
                                                 g.gate[:, t:t + 1, bass.ds(e, 1)].rearrange("p t o -> p (t o)"), ALU.mult))
                    nc.vector.tensor_scalar(prob[:, t % 2, 0:n], prob[:, t % 2, 0:n], r[:, t:t + 1], None,
                                            ALU.mult).then_inc(scaled, 1)
                    if t + 1 < T:
                        top(t + 1)
                    for j0 in range(0, t + 1, 4):
                        js = min(4, t + 1 - j0)
                        dve.wait_ge(flipped, ONE + e * NF + nf + 1)
                        if j0 == 0:
                            dve.wait_ge(summed, ONE + e * 2 * T + 2 * t)
                        nc.vector.tensor_copy(probT[:, j0:j0 + js, :],
                                              flip[nf % 3][0:P, 0:js * P].rearrange("p (j c) -> p j c", j=js)
                                              ).then_inc(unflipped, 1)
                        nf += 1
                assert step.n == LINKS, step.n


def stage_linear_mix(nc, g):
    PROJ = T + 3
    with ExitStack() as ctx:
        s = Scope(nc, ctx, "mix1")
        w, bq, bkv = s.sb("w", [128, KC, 384]), s.sb("bq", [128, PAIRS]), s.sb("bkv", [P, 2, 256])
        kv = s.sb("kv", [P, T, 257])
        klow = s.sb("klow", [P, T, 128])
        qT, qlow = s.sb("qT", [128, N]), s.sb("qlow", [128, N])
        state, ksum = s.sb("state", [128, 128]), s.sb("ksum", [128, 128])
        rden = s.sb("rden", [128, 2, 418])
        ring = [s.ps(f"ring{i}", [128, 512]) for i in range(4)]
        kv_ps = s.ps("kv_ps", [128, 512])
        den = [s.ps("den0", [128, 512])]
        num = [s.ps(f"num{i}", [128, 512]) for i in range(2)]
        names = ("w_in b_in made taken k_low k_exp q_low q_exp k_in q_in kv_made state_in den_made den_used num_made "
                 "num_used chain bkv_in bkv_used")
        (w_in, b_in, made, taken, k_low, k_exp, q_low, q_exp, k_in, q_in, kv_made, state_in, den_made, den_used, num_made,
         num_used, chain, bkv_in, bkv_used) = (s.sem(x) for x in names.split())
        block = ctx.enter_context(nc.Block())

        @block.sync
        def _(sp):
            sp.dma_start(w[:], g.mix1_w[0]).then_inc(w_in, 16)
            sp.dma_start(bq[:], g.mix1_bq).then_inc(b_in, 16)
            sp.dma_start(bkv[:, 0, :], g.mix1_bkv[0:1].broadcast_to([P, 256])).then_inc(bkv_in, 16)
            with sp.Fori(0, PAIRS - 1) as i:
                sp.wait_ge(taken, ONE + i * PROJ + PROJ)
                sp.dma_start(w[:], g.mix1_w[bass.ds(i + 1, 1)].rearrange("o p k f -> (o p) k f")).then_inc(w_in, 16)
                sp.dma_start(bkv[:, 0, :], g.mix1_bkv[bass.ds(i + 1, 1)].broadcast_to([P, 256])).then_inc(bkv_in, 16)

        @block.tensor
        def _(pe):
            for count in (kv_made, num_made):
                pe.sem_inc(count, 1)
            with pe.Fori(0, PAIRS) as i:
                pe.wait_ge(w_in, i * 16 + 16)
                for n in range(PROJ):
                    pe.wait_ge(taken, ONE + i * PROJ + max(n - 3, 0))
                    for k in range(KC):
                        if n < T:
                            last = nc.tensor.matmul(ring[n % 4][0:P, 0:256], g.XT[:, k, n * P:(n + 1) * P], w[:, k, 128:384],
                                                    start=(k == 0), stop=(k == KC - 1))
                        else:
                            c0, cn = CH[n - T]
                            last = nc.tensor.matmul(ring[n % 4][:, 0:cn], w[:, k, 0:128], g.XT[:, k, c0:c0 + cn],
                                                    start=(k == 0), stop=(k == KC - 1))
                    last.then_inc(made, 1)
                pe.wait_ge(k_in, i + 1)
                pe.wait_ge(state_in, ONE + i)
                for t in range(T):
                    last = nc.tensor.matmul(kv_ps[:, 0:129], kv[:, t, 0:128], kv[:, t, 128:257], start=(t == 0), stop=(t == T - 1))
                last.then_inc(kv_made, 1)
                pe.wait_ge(state_in, ONE + i + 1)
                pe.wait_ge(q_in, i + 1)
                for c, (c0, cn) in enumerate(CH):
                    pe.wait_ge(den_used, ONE + i * 3 + c)
                    nc.tensor.matmul(den[0][:, 0:cn], ksum[:], qT[:, c0:c0 + cn], start=True, stop=True).then_inc(den_made, 1)
                    pe.wait_ge(num_used, ONE + i * 3 + max(c - 1, 0))
                    nc.tensor.matmul(num[c % 2][:, 0:cn], state[:], qT[:, c0:c0 + cn], start=True, stop=True).then_inc(num_made, 1)

        @block.scalar
        def _(act):
            with act.Fori(0, PAIRS) as i:
                act.wait_ge(k_low, i + 1)
                nc.scalar.activation(klow[:], klow[:], ACT.Exp).then_inc(k_exp, 1)
                act.wait_ge(q_low, i + 1)
                nc.scalar.activation(qlow[:], qlow[:], ACT.Exp).then_inc(q_exp, 1)

        @block.vector
        def _(dve):
            for count in (taken, state_in, den_used, num_used):
                dve.sem_inc(count, 1)
            step = Chain(dve, chain)
            nc.vector.memset(kv[:, :, 256:257], 1.0)
            step(nc.vector.memset(state[:], 0.0))
            dve.wait_ge(b_in, 16)
            LINKS = 2
            with dve.Fori(0, PAIRS) as i:
                step = Chain(dve, chain, 1 + i * LINKS)
                dve.wait_ge(bkv_in, i * 16 + 16)
                dve.wait_ge(kv_made, ONE + i)
                for t in range(T):
                    dve.wait_ge(made, i * PROJ + t + 1)
                    nc.vector.tensor_tensor(kv[:, t, 0:256], ring[t % 4][0:P, 0:256], bkv[:, 0, :], ALU.add).then_inc(taken, 1)
                dve.wait_ge(taken, ONE + i * PROJ + T)
                nc.vector.tensor_scalar(klow[:], kv[:, :, 0:128], 0.0, None, ALU.min).then_inc(k_low, 1)
                dve.wait_ge(num_made, ONE + i * 3)
                b = bq[:, bass.ds(i, 1)]
                for c, (c0, cn) in enumerate(CH):
                    n = T + c
                    dve.wait_ge(made, i * PROJ + n + 1)
                    low = nc.vector.tensor_scalar(qlow[:, c0:c0 + cn], ring[n % 4][:, 0:cn], b, 0.0, ALU.add, ALU.min)
                    nc.vector.tensor_scalar(qT[:, c0:c0 + cn], ring[n % 4][:, 0:cn], b, 0.0, ALU.add, ALU.max).then_inc(taken, 1)
                low.then_inc(q_low, 1)
                dve.wait_ge(k_exp, i + 1)
                nc.vector.scalar_tensor_tensor(kv[:, :, 0:128], kv[:, :, 0:128], 0.0, klow[:], ALU.max, ALU.add).then_inc(k_in, 1)
                dve.wait_ge(q_exp, i + 1)
                dve.wait_ge(taken, ONE + i * PROJ + PROJ)
                nc.vector.tensor_tensor(qT[:], qT[:], qlow[:], ALU.add).then_inc(q_in, 1)
                dve.wait_ge(kv_made, ONE + i + 1)
                step(nc.vector.tensor_copy(state[0:64, 0:64], kv_ps[0:64, 0:64]))
                step(nc.vector.tensor_copy(state[64:128, 64:128], kv_ps[64:128, 64:128]))
                nc.vector.tensor_scalar(ksum[:], g.halves[:], kv_ps[:, 128:129], None, ALU.mult).then_inc(state_in, 1)
                for c, (c0, cn) in enumerate(CH):
                    dve.wait_ge(den_made, i * 3 + c + 1)
                    nc.vector.reciprocal(rden[:, c % 2, 0:cn], den[0][:, 0:cn]).then_inc(den_used, 1)
                    dve.wait_ge(den_used, ONE + i * 3 + c + 1)
                    dve.wait_ge(num_made, ONE + i * 3 + c + 1)
                    nc.vector.tensor_tensor(g.OT[:, bass.ds(i, 1), c0:c0 + cn].rearrange("p o c -> p (o c)"),
                                            num[c % 2][:, 0:cn], rden[:, c % 2, 0:cn], ALU.mult).then_inc(num_used, 1)
                assert step.n == LINKS


def stage_gat(nc, g, name, inT, spare, w_dram, att_dram, b_dram, last_layer, next_w=None):
    HN = N // 2
    SCORE_AT, FLIP_AT, SPREAD_AT = 2, 10, 12
    with ExitStack() as ctx:
        s = Scope(nc, ctx, name)
        C = s.sb("C", [P, T, N])
        h = s.sb("h", [P, T, D + 2])
        att = s.sb("att", [128, 2, D])
        u = s.sb("u", [128, KC, 2])
        bf = s.sb("bf", [128, KC])
        a = s.sb("a", [P, 8, T])
        A_SRC, A_DST, HIGH, Z, MX, SHIFT, SHIFT2, A_SRC2 = range(8)
        rows = s.sb("rows", [128, 2, N])
        e = s.sb("e", [P, 4, HN])
        small = s.sb("small", [P, 2])
        in_place = lambda buf: buf[:].rearrange("p k n -> p (k n)")[:, 0:KC * D].rearrange("p (k m) -> p k m", k=KC)
        w = in_place(spare)
        flat = e[:].rearrange("p a n -> p (a n)")
        diag = [flat[:, 0:N], flat[:, N:2 * N]]
        missing, high = flat[:, 0:N], flat[:, N:2 * N]
        bk = [s.ps(f"bk{i}", [128, 512]) for i in range(8)]
        names = ("w_in att_in c_in b_in made taken u_in scored chain high_in flipped diag_in spread spread_used raised "
                 "weights_in den_made agg agg_used c_diag next_in")
        (w_in, att_in, c_in, b_in, made, taken, u_in, scored, chain, high_in, flipped, diag_in, spread, spread_used, raised,
         weights_in, den_made, agg, agg_used, c_diag, next_in) = (s.sem(x) for x in names.split())
        block = ctx.enter_context(nc.Block())

        @block.sync
        def _(sp):
            for r in range(2):
                sp.dma_start(att[:, r, :], bcast_rows(att_dram[r], 128, D)).then_inc(att_in, 16)
            if w_dram is not None:
                sp.dma_start(w, w_dram.rearrange("(k p) m -> p k m", p=128)).then_inc(w_in, 16)
            sp.dma_start(C[:], g.cnt_table[0:N * N].rearrange("(t p d) o -> p t (d o)", p=P, d=N)).then_inc(c_in, 16)
            if last_layer:
                sp.wait_ge(u_in, 2 * KC)
                sp.dma_start(att[:, 0, :], bcast_rows(b_dram, 128, D)).then_inc(b_in, 16)
            else:
                sp.dma_start(bf[:], b_dram).then_inc(b_in, 16)
            if next_w is not None:
                sp.wait_ge(made, 2 * T)
                sp.wait_ge(scored, 1)
                sp.dma_start(in_place(inT), next_w.rearrange("(k p) m -> p k m", p=128)).then_inc(next_in, 16)
                sp.wait_ge(next_in, 16)

        @block.tensor
        def _(pe):
            if w_dram is not None:
                pe.wait_ge(w_in, 16)
            for n in range(2 * T):
                t, hf = divmod(n, 2)
                if n >= 3:
                    pe.wait_ge(taken, n - 2)
                for k in range(KC):
                    last = nc.tensor.matmul(bk[n % 3][0:P, 0:HALF], inT[:, k, t * P:(t + 1) * P],
                                            w[:, k, hf * HALF:(hf + 1) * HALF], start=(k == 0), stop=(k == KC - 1))
                last.then_inc(made, 1)
                if n == SCORE_AT:
                    pe.wait_ge(u_in, 2 * KC)
                    for t in range(T):
                        for k in range(KC):
                            last = nc.tensor.matmul(bk[7][0:P, 2 * t:2 * t + 2], inT[:, k, t * P:(t + 1) * P], u[:, k, :],
                                                    start=(k == 0), stop=(k == KC - 1))
                    last.then_inc(scored, 1)
                if n == FLIP_AT:
                    pe.wait_ge(high_in, 1)
                    for t in range(T):
                        last = nc.tensor.transpose(bk[3 + t // 4][0:P, t % 4 * P:(t % 4 + 1) * P], high[:, t * P:(t + 1) * P],
                                                   g.ident[0:P, 0:P])
                    last.then_inc(flipped, 1)
                if n == SPREAD_AT:
                    for m in range(6):
                        r, c = divmod(m, 3)
                        c0, cn = CH[c]
                        pe.wait_ge(diag_in, r + 1)
                        if m == 5:
                            pe.wait_ge(spread_used, 1)
                        nc.tensor.matmul(bk[3 + m % 5][:, 0:cn], g.ones[0:P, :], diag[r][:, c0:c0 + cn],
                                         start=True, stop=True).then_inc(spread, 1)
            pe.wait_ge(spread_used, 6)
            pe.wait_ge(taken, 2 * T)
            if last_layer:
                pe.wait_ge(weights_in, 2 * T)
                for n in range(2 * T):
                    d, hf = divmod(n, 2)
                    cols = HALF + hf
                    if n >= 4:
                        pe.wait_ge(agg_used, n - 3)
                    for j in range(T):
                        last = nc.tensor.matmul(bk[1 + n % 4][0:P, 0:cols], C[:, j, d * P:(d + 1) * P],
                                                h[:, j, hf * HALF:hf * HALF + cols], start=(j == 0), stop=(j == T - 1))
                    last.then_inc(agg, 1)
            else:
                pe.wait_ge(weights_in, 2 * T)
                for c, (c0, cn) in enumerate(CH):
                    for j in range(T):
                        last = nc.tensor.matmul(bk[c][:, 0:cn], g.ones[0:P, :], C[:, j, c0:c0 + cn],
                                                start=(j == 0), stop=(j == T - 1))
                    last.then_inc(den_made, 1)
                for n in range(3 * KC):
                    f, c = divmod(n, 3)
                    c0, cn = CH[c]
                    if n >= 4:
                        pe.wait_ge(agg_used, n - 3)
                    for j in range(T):
                        last = nc.tensor.matmul(bk[3 + n % 4][:, 0:cn], h[:, j, f * 128:(f + 1) * 128], C[:, j, c0:c0 + cn],
                                                start=(j == 0), stop=(j == T - 1))
                    last.then_inc(agg, 1)

        @block.scalar
        def _(act):
            def take(n):
                t, hf = divmod(n, 2)
                act.wait_ge(made, n + 1)
                nc.scalar.activation(h[:, t, hf * HALF:(hf + 1) * HALF], bk[n % 3][0:P, 0:HALF], ACT.Copy).then_inc(taken, 1)

            for n in range(SPREAD_AT + 1):
                take(n)
            for m in range(6):
                r, c = divmod(m, 3)
                c0, cn = CH[c]
                act.wait_ge(spread, m + 1)
                nc.scalar.activation(rows[:, r, c0:c0 + cn], bk[3 + m % 5][:, 0:cn], ACT.Copy).then_inc(spread_used, 1)
            act.wait_ge(spread_used, 6)
            left = SPREAD_AT + 1
            for n in range(2 * T):
                t, hf = divmod(n, 2)
                if n >= 2:
                    act.wait_ge(weights_in, n - 1)
                for r, col in enumerate((A_SRC, A_SRC2)):
                    last = nc.scalar.activation(e[:, 2 * (n % 2) + r, :], rows[0:P, r, hf * HN:(hf + 1) * HN], ACT.Exp,
                                                bias=a[:, col, t:t + 1])
                last.then_inc(raised, 1)
                if n % 3 == 2 and left < 2 * T:
                    take(left)
                    left += 1
            while left < 2 * T:
                take(left)
                left += 1
            if not last_layer:
                act.wait_ge(b_in, 16)
                for n in range(3 * KC):
                    f, c = divmod(n, 3)
                    c0, cn = CH[c]
                    act.wait_ge(agg_used, n + 1)
                    nc.scalar.activation(g.OT[:, f, c0:c0 + cn], g.OT[:, f, c0:c0 + cn], ACT.Relu, bias=bf[:, f:f + 1])

        @block.vector
        def _(dve):
            step = Chain(dve, chain)
            nc.vector.memset(h[:, :, D:D + 1], 1.0)
            dve.wait_ge(att_in, 32)
            if w_dram is not None:
                dve.wait_ge(w_in, 16)
            for n in range(2 * KC):
                k, r = divmod(n, 2)
                if n >= 2:
                    dve.wait_ge(u_in, n - 1)
                nc.vector.tensor_tensor_reduce(rows[:, r, 0:D], w[:, k, :], att[:, r, :], 1.0, 0.0, ALU.mult, ALU.add,
                                               u[:, k, r:r + 1]).then_inc(u_in, 1)
            dve.wait_ge(c_in, 16)
            for t in range(T):
                last = nc.vector.tensor_tensor(C[:, t, t * P:(t + 1) * P], C[:, t, t * P:(t + 1) * P],
                                               g.ident[0:P, 0:P], ALU.add)
            last.then_inc(c_diag, 1)
            dve.wait_ge(scored, 1)
            dve.wait_ge(c_diag, 1)
            step(nc.vector.tensor_copy(a[:, 0:2, :], bk[7][0:P, 0:2 * T].rearrange("p (t r) -> p r t", r=2)))
            nc.vector.tensor_scalar(a[:, A_SRC2, :], a[:, A_SRC, :], 0.2, None, ALU.mult)
            for t in range(T):
                step(nc.vector.tensor_scalar(missing, C[:, t, :], 0.5, NEG, ALU.is_lt, ALU.mult))
                if t == 0:
                    step(nc.vector.tensor_scalar(high, missing, a[:, A_SRC, 0:1], None, ALU.add))
                else:
                    ins = nc.vector.scalar_tensor_tensor(high, missing, a[:, A_SRC, t:t + 1], high, ALU.add, ALU.max)
                    if t < T - 1:
                        step(ins)
            ins.then_inc(high_in, 1)
            dve.wait_ge(flipped, 1)
            for b, k in enumerate((4, 4, 2)):
                last = nc.vector.tensor_reduce(a[:, HIGH, 4 * b:4 * b + k],
                                               bk[3 + b][0:P, 0:k * P].rearrange("p (t c) -> p t c", t=k), AX, ALU.max)
            step(last)
            step(nc.vector.tensor_tensor(a[:, Z, :], a[:, HIGH, :], a[:, A_DST, :], ALU.add))
            step(nc.vector.scalar_tensor_tensor(a[:, MX, :], a[:, Z, :], 0.2, a[:, Z, :], ALU.mult, ALU.max))
            nc.vector.tensor_tensor(a[:, SHIFT, :], a[:, A_DST, :], a[:, MX, :], ALU.subtract)
            step(nc.vector.scalar_tensor_tensor(a[:, SHIFT2, :], a[:, A_DST, :], 0.2, a[:, MX, :], ALU.mult, ALU.subtract))
            ident = g.ident[0:P, 0:P].unsqueeze(1).broadcast_to([P, T, P])
            for r in range(2):
                nc.vector.tensor_tensor(diag[r].rearrange("p (t c) -> p t c", t=T), ident,
                                        a[:, SHIFT + r, :].unsqueeze(2).broadcast_to([P, T, P]), ALU.mult).then_inc(diag_in, 1)
            for n in range(2 * T):
                t, hf = divmod(n, 2)
                c = C[:, t, hf * HN:(hf + 1) * HN]
                e1, e2 = e[:, 2 * (n % 2), :], e[:, 2 * (n % 2) + 1, :]
                dve.wait_ge(raised, n + 1)
                step(nc.vector.tensor_tensor(e1, e1, e2, ALU.max))
                nc.vector.scalar_tensor_tensor(c, e1, 1.0, c, ALU.min, ALU.mult).then_inc(weights_in, 1)
            if last_layer:
                dve.wait_ge(b_in, 16)
                step(nc.vector.tensor_tensor(g.X[:], g.X[:], att[0:P, 0, :].unsqueeze(1).broadcast_to([P, T, D]), ALU.add))
                for d in range(T):
                    dve.wait_ge(agg, 2 * d + 2)
                    step(nc.vector.reciprocal(small[:, d % 2:d % 2 + 1], bk[1 + (2 * d + 1) % 4][0:P, HALF:HALF + 1]))
                    for hf in range(2):
                        x = g.X[:, d, hf * HALF:(hf + 1) * HALF]
                        nc.vector.scalar_tensor_tensor(x, bk[1 + (2 * d + hf) % 4][0:P, 0:HALF], small[:, d % 2:d % 2 + 1], x,
                                                       ALU.mult, ALU.add).then_inc(agg_used, 1)
            else:
                for c, (c0, cn) in enumerate(CH):
                    dve.wait_ge(den_made, c + 1)
                    last = nc.vector.reciprocal(rows[:, 0, c0:c0 + cn], bk[c][:, 0:cn])
                step(last)
                for n in range(3 * KC):
                    f, c = divmod(n, 3)
                    c0, cn = CH[c]
                    dve.wait_ge(agg, n + 1)
                    nc.vector.tensor_tensor(g.OT[:, f, c0:c0 + cn], bk[3 + n % 4][:, 0:cn], rows[:, 0, c0:c0 + cn],
                                            ALU.mult).then_inc(agg_used, 1)


def stage_route(nc, g):
    with ExitStack() as ctx:
        s = Scope(nc, ctx, "route")
        wg, zT, z = s.sb("wg", [128, KC, E1]), s.sb("zT", [E1, N]), s.sb("z", [P, T, E1])
        cmp_, same, rank = s.sb("cmp", [P, T, E1, E1]), s.sb("same", [P, T, E1, E1]), s.sb("rank", [P, T, E1])
        pick = s.sb("pick", [P, 2, T, E1])
        both = s.sb("both", [P, T, E1], BF16)
        tmp = s.sb("tmp", [P, T, E1])
        col = s.sb("col", [P, 8, T])
        L1_, L2_, DIFF, EX, ONE, SLOT, KEEP, AWAY = range(8)
        wt = s.sb("wt", [P, 2, T])
        diag, row, eq = s.sb("diag", [P, N]), s.sb("row", [P, N]), s.sb("eq", [P, 2, N])
        offset = s.sb("offset", [P, N])
        ahead = s.sb("ahead", [P, T, N], BF16)
        place = s.sb("place", [P, T, E1])
        names_i = s.sb("names_i", [P, E1])
        trash = s.sb("trash", [P, 2, T])
        put_i, token = s.sb("put_i", [P, 2, T], I32), s.sb("token", [P, T], I32)
        zero = s.sb("zero", [120, SLOTS // 120], I32)
        bk = [s.ps(f"bk{i}", [128, 512]) for i in range(8)]
        names = ("w_in made taken flipped chain asked answered diag_in spread row_in ahead_in placed iotas zeroed put_in zero_in loaded "
                 "z_in")
        (w_in, made, taken, flipped, chain, asked, answered, diag_in, spread, row_in, ahead_in, placed, iotas, zeroed,
         put_in, zero_in, loaded, z_in) = (s.sem(x) for x in names.split())
        block = ctx.enter_context(nc.Block())

        @block.sync
        def _(sp):
            sp.dma_start(wg[:], g.route_w.rearrange("(k p) m -> p k m", p=128)).then_inc(w_in, 16)
            sp.wait_ge(zero_in, 1)
            sp.dma_start(g.slot_token[0:SLOTS].rearrange("(p f) o -> p (f o)", p=120), zero[:]).then_inc(zeroed, 16)
            sp.wait_ge(g.slot_put, 2 * T * 16)
            sp.dma_start(g.slots[:].rearrange("p (e c) -> p e c", e=E1),
                         g.slot_token[0:SLOTS].rearrange("(e p c) o -> p e (c o)", e=E1, p=SUB)).then_inc(loaded, 16)
            sp.wait_ge(loaded, 16)

        @block.tensor
        def _(pe):
            pe.wait_ge(w_in, 16)
            for c, (c0, cn) in enumerate(CH):
                for k in range(KC):
                    last = nc.tensor.matmul(bk[c][0:E1, 0:cn], wg[:, k, :], g.XT[:, k, c0:c0 + cn], start=(k == 0), stop=(k == KC - 1))
                last.then_inc(made, 1)
            pe.wait_ge(taken, 3)
            for t in range(T):
                last = nc.tensor.transpose(bk[3][0:P, t * E1:(t + 1) * E1], zT[:, t * P:(t + 1) * P], g.ident[0:E1, 0:E1])
            last.then_inc(flipped, 1)
            pe.wait_ge(diag_in, 1)
            for c, (c0, cn) in enumerate(CH):
                nc.tensor.matmul(bk[4 + c][:, 0:cn], g.ones[0:P, :], diag[:, c0:c0 + cn], start=True, stop=True).then_inc(spread, 1)
            pe.wait_ge(ahead_in, T)
            for i in range(T):
                for j in range(T):
                    last = nc.tensor.matmul(bk[7][0:P, i * E1:(i + 1) * E1], ahead[:, j, i * P:(i + 1) * P], both[:, j, :],
                                            start=(j == 0), stop=(j == T - 1))
            last.then_inc(placed, 1)

        @block.scalar
        def _(act):
            for c, (c0, cn) in enumerate(CH):
                act.wait_ge(made, c + 1)
                nc.scalar.activation(zT[:, c0:c0 + cn], bk[c][0:E1, 0:cn], ACT.Copy).then_inc(taken, 1)
            act.wait_ge(asked, 1)
            nc.scalar.activation(col[:, EX, :], col[:, DIFF, :], ACT.Exp).then_inc(answered, 1)
            for c, (c0, cn) in enumerate(CH):
                act.wait_ge(spread, c + 1)
                nc.scalar.activation(row[:, c0:c0 + cn], bk[4 + c][0:P, 0:cn], ACT.Copy).then_inc(row_in, 1)

        @block.gpsimd
        def _(pool):
            nc.gpsimd.memset(zero[:], 0).then_inc(zero_in, 1)
            nc.gpsimd.iota(offset[:], pattern=[[1, N]], base=0, channel_multiplier=-1, allow_small_or_imprecise_dtypes=True)
            nc.gpsimd.iota(names_i[:], pattern=[[1, E1]], base=0, channel_multiplier=0, allow_small_or_imprecise_dtypes=True)
            nc.gpsimd.iota(trash[:], pattern=[[P, 2 * T]], base=SLOTS, channel_multiplier=1, allow_small_or_imprecise_dtypes=True)
            nc.gpsimd.iota(token[:], pattern=[[P, T]], base=0, channel_multiplier=1).then_inc(iotas, 1)
            pool.wait_ge(iotas, 1)
            pool.wait_ge(put_in, 2)
            pool.wait_ge(zeroed, 16)
            for k in range(2):
                for t in range(T):
                    pool.indirect_dma_start(out=g.slot_token, out_offset=bass.IndirectOffsetOnAxis(ap=put_i[:, k, t:t + 1], axis=0),
                                            in_=token[:, t:t + 1], in_offset=None).then_inc(g.slot_put, 16)

        @block.vector
        def _(dve):
            step = Chain(dve, chain)
            dve.wait_ge(flipped, 1)
            step(nc.vector.tensor_copy(z[:], bk[3][0:P, 0:T * E1].rearrange("p (t e) -> p t e", e=E1)))
            rank_of(nc, g, step, z, cmp_, same, rank, E1)
            nc.vector.tensor_scalar(both[:], rank[:], 1.5, None, ALU.is_lt)
            for k in range(2):
                step(nc.vector.tensor_scalar(pick[:, k, :, :], rank[:], float(k), None, ALU.is_equal))
                step(nc.vector.tensor_tensor(tmp[:], pick[:, k, :, :], z[:], ALU.mult))
                step(nc.vector.tensor_reduce(col[:, L1_ + k, :], tmp[:], AX, ALU.add))
            nc.vector.tensor_tensor(col[:, DIFF, :], col[:, L2_, :], col[:, L1_, :], ALU.subtract).then_inc(asked, 1)
            dve.wait_ge(answered, 1)
            step(nc.vector.tensor_scalar(col[:, ONE, :], col[:, EX, :], 1.0, None, ALU.add))
            step(nc.vector.reciprocal(wt[:, 0, :], col[:, ONE, :]))
            step(nc.vector.tensor_tensor(wt[:, 1, :], col[:, EX, :], wt[:, 0, :], ALU.mult))
            nc.vector.tensor_tensor(diag[:].rearrange("p (t c) -> p t c", t=T), g.ident[0:P, 0:P].unsqueeze(1).broadcast_to([P, T, P]),
                                    wt[:, 0, :].unsqueeze(2).broadcast_to([P, T, P]), ALU.mult).then_inc(diag_in, 1)
            dve.wait_ge(row_in, 3)
            dve.wait_ge(iotas, 1)
            for t in range(T):
                own = wt[:, 0, t:t + 1]
                step(nc.vector.tensor_scalar(eq[:, 0, :], row[:], own, None, ALU.is_equal))
                step(nc.vector.scalar_tensor_tensor(eq[:, 1, :], offset[:], t * P + 0.5, eq[:, 0, :], ALU.is_gt, ALU.mult))
                nc.vector.scalar_tensor_tensor(ahead[:, t, :], row[:], own, eq[:, 1, :], ALU.is_lt, ALU.add).then_inc(ahead_in, 1)
            dve.wait_ge(placed, 1)
            step(nc.vector.tensor_copy(place[:], bk[7][0:P, 0:T * E1].rearrange("p (t e) -> p t e", e=E1)))
            for k in range(2):
                step(nc.vector.tensor_tensor(tmp[:], pick[:, k, :, :], place[:], ALU.mult))
                step(nc.vector.tensor_reduce(col[:, DIFF, :], tmp[:], AX, ALU.add))
                step(nc.vector.tensor_scalar(col[:, KEEP, :], col[:, DIFF, :], CAP - 0.5, None, ALU.is_lt))
                step(nc.vector.tensor_tensor(tmp[:], pick[:, k, :, :], names_i[:].unsqueeze(1).broadcast_to([P, T, E1]), ALU.mult))
                step(nc.vector.tensor_reduce(col[:, EX, :], tmp[:], AX, ALU.add))
                step(nc.vector.scalar_tensor_tensor(col[:, SLOT, :], col[:, EX, :], float(CAP), col[:, DIFF, :], ALU.mult, ALU.add))
                step(nc.vector.tensor_tensor(col[:, AWAY, :], col[:, SLOT, :], trash[:, k, :], ALU.subtract))
                step(nc.vector.tensor_tensor(col[:, AWAY, :], col[:, AWAY, :], col[:, KEEP, :], ALU.mult))
                nc.vector.tensor_tensor(put_i[:, k, :], col[:, AWAY, :], trash[:, k, :], ALU.add)
                nc.vector.tensor_tensor(g.read_i[:, k, :], col[:, SLOT, :], col[:, KEEP, :], ALU.mult)
                nc.vector.tensor_tensor(g.share[:, k, :], wt[:, k, :], col[:, KEEP, :], ALU.mult).then_inc(put_in, 1)
                dve.wait_ge(put_in, k + 1)


def stage_experts1(nc, g):
    GH = 2
    NG = HB // GH
    with ExitStack() as ctx:
        s = Scope(nc, ctx, "exp1")
        raw = s.sb("raw", [128, 2, 2, GH * D])
        whi, wlo = s.sb("whi", [128, 2, 2, GH * D], F32R), s.sb("wlo", [128, 2, 2, GH * D], F32R)
        b1, b2 = s.sb("b1", [128, E1, HB]), s.sb("b2", [128, E1, KC])
        idx = s.sb("idx", [SUB, NS], I32)
        flat = [b[:].rearrange("p k n -> p (k n)") for b in (g.XT, g.OT)]
        xg = flat[0][0:SUB, 0:NS * D].rearrange("p (c d) -> p c d", c=NS)
        oT = flat[1][:, 0:KC * CAP].rearrange("p (k c) -> p k c", k=KC)
        y = flat[1][0:SUB, KC * CAP:KC * CAP + NS * D].rearrange("p (c d) -> p c d", c=NS)
        xhi, xlo = s.sb("xhi", [128, KC, CAP], F32R), s.sb("xlo", [128, KC, CAP], F32R)
        hid = s.sb("hid", [128, 2, CAP])
        hhi, hlo = s.sb("hhi", [128, 2, CAP], F32R), s.sb("hlo", [128, 2, CAP], F32R)
        hp = [s.ps(f"hp{i}", [128, 512]) for i in range(2)]
        op = [s.ps(f"op{i}", [128, 512]) for i in range(KC)]
        w_in = [[s.sem(f"w{m + 1}_in{i}") for i in range(2)] for m in range(2)]
        names = ("b_in used idx_in opened xg_free flipped x_in made gelus raised o_in turned y_in stored y_free w_hi w_lo h_hi x_hi")
        (b_in, used, idx_in, opened, xg_free, flipped, x_in, made, gelus, raised, o_in, turned, y_in,
         stored, y_free, w_hi, w_lo, h_hi, x_hi) = (s.sem(x) for x in names.split())
        block = ctx.enter_context(nc.Block())

        @block.sync
        def _(sp):
            sp.sem_inc(y_free, 1)

            def load(j, slot):
                for m, src in enumerate((g.exp1_w1, g.exp1_w2)):
                    sp.dma_start(raw[:, slot, m, :], src[bass.ds(j, 1)].rearrange("o p f -> (o p) f")).then_inc(w_in[m][slot], 16)

            def expert(e, last):
                for gi in range(NG - 2 if last else NG):
                    sp.wait_ge(w_lo, e * NG + gi + 1)
                    load(e * NG + gi + 2, gi % 2)
                sp.wait_ge(y_in, ONE + e * 2 * NS + 2 * NS)
                sp.dma_start(g.slot_out[bass.ds(e * CAP, CAP)].rearrange("(p c) d -> p c d", p=SUB), y).then_inc(stored, 16)
                sp.wait_ge(stored, e * 16 + 16)
                sp.sem_inc(y_free, 1)

            load(0, 0)
            load(1, 1)
            sp.dma_start(b1[:], g.exp1_b1).then_inc(b_in, 16)
            sp.dma_start(b2[:], g.exp1_b2).then_inc(b_in, 16)
            with sp.Fori(0, E1 - 1) as e:
                expert(e, False)
            expert(E1 - 1, True)

        @block.gpsimd
        def _(pool):
            def gather(e):
                nc.gpsimd.tensor_copy(idx[:], g.slots[:, bass.ds(e * NS, NS)]).then_inc(idx_in, 1)
                pool.wait_ge(idx_in, e + 1)
                pool.sem_inc(opened, 1)
                for c in range(NS):
                    pool.indirect_dma_start(out=xg[:, c, :], out_offset=None, in_=g.xn3,
                                            in_offset=bass.IndirectOffsetOnAxis(ap=idx[:, c:c + 1], axis=0)).then_inc(g.gathered, 16)

            gather(0)
            with pool.Fori(0, E1 - 1) as e:
                pool.wait_ge(xg_free, e + 1)
                pool.sem_inc(opened, 1)
                gather(e + 1)

        @block.tensor
        def _(pe):
            for count in (flipped, used):
                pe.sem_inc(count, 1)

            def three(out, hi, lo, rhi, rlo, first, last):
                nc.tensor.matmul(out, hi, rhi, start=first, stop=False)
                nc.tensor.matmul(out, hi, rlo, start=False, stop=False)
                return nc.tensor.matmul(out, lo, rhi, start=False, stop=last)

            def turn_in(e):
                pe.wait_ge(g.gathered, e * NS * 16 + NS * 16)
                for c in range(NS):
                    pe.wait_ge(x_in, ONE + e * NS + max(c - 1, 0))
                    for k in range(KC):
                        last = nc.tensor.transpose(hp[c % 2][:, k * SUB:(k + 1) * SUB], xg[:, c, k * 128:(k + 1) * 128],
                                                   g.ident[0:SUB, 0:SUB])
                    last.then_inc(flipped, 1)

            def hidden(e, j):
                gi, r = divmod(j, GH)
                if r == 0:
                    pe.wait_ge(w_lo, e * NG + gi + 1)
                pe.wait_ge(gelus, ONE + e * HB + max(j - 1, 0))
                for k in range(KC):
                    at = slice((r * KC + k) * 128, (r * KC + k + 1) * 128)
                    last = three(hp[j % 2][:, 0:CAP], whi[:, gi % 2, 0, at], wlo[:, gi % 2, 0, at], xhi[:, k, :], xlo[:, k, :],
                                 k == 0, k == KC - 1)
                last.then_inc(made, 1)

            def out(e, j):
                gi, r = divmod(j, GH)
                pe.wait_ge(raised, ONE + e * HB + j + 1)
                for m in range(KC):
                    at = slice(r * D + m * 128, r * D + (m + 1) * 128)
                    last = three(op[m][:, 0:CAP], whi[:, gi % 2, 1, at], wlo[:, gi % 2, 1, at], hhi[:, j % 2, :], hlo[:, j % 2, :],
                                 j == 0, j == HB - 1)
                if r == GH - 1:
                    last.then_inc(used, 1)

            def expert(e, last_one):
                pe.wait_ge(x_in, ONE + e * NS + NS)
                pe.wait_ge(y_in, ONE + e * 2 * NS)
                hidden(e, 0)
                for j in range(HB):
                    if j + 1 < HB:
                        hidden(e, j + 1)
                    if j == 0:
                        pe.wait_ge(o_in, ONE + e * KC)
                    out(e, j)
                if not last_one:
                    turn_in(e + 1)
                    pe.wait_ge(x_in, ONE + (e + 1) * NS + NS)
                pe.wait_ge(o_in, ONE + e * KC + KC)
                for n in range(2 * NS):
                    c, hf = divmod(n, 2)
                    pe.wait_ge(y_in, ONE + e * 2 * NS + max(n - 1, 0))
                    for k in range(3):
                        last = nc.tensor.transpose(hp[n % 2][0:SUB, k * 128:(k + 1) * 128], oT[:, 3 * hf + k, c * SUB:(c + 1) * SUB],
                                                   g.ident[:])
                    last.then_inc(turned, 1)

            turn_in(0)
            with pe.Fori(0, E1 - 1) as e:
                expert(e, False)
            expert(E1 - 1, True)

        @block.scalar
        def _(act):
            for count in (gelus, o_in, y_in):
                act.sem_inc(count, 1)

            def high(e, gi):
                for m in range(2):
                    act.wait_ge(w_in[m][gi % 2], e * (NG // 2) * 16 + (gi // 2 + 1) * 16)
                    last = nc.scalar.activation(whi[:, gi % 2, m, :], raw[:, gi % 2, m, :], ACT.Copy)
                last.then_inc(w_hi, 1)

            def expert(e, last_one):
                for j in range(HB):
                    gi, r = divmod(j, GH)
                    act.wait_ge(made, e * HB + j + 1)
                    act.wait_ge(raised, ONE + e * HB + max(j - 1, 0))
                    nc.scalar.activation(hid[:, j % 2, :], hp[j % 2][:, 0:CAP], ACT.Gelu,
                                         bias=b1[:, bass.ds(e, 1), j:j + 1].rearrange("p a b -> p (a b)")).then_inc(gelus, 1)
                    act.wait_ge(gelus, ONE + e * HB + j + 1)
                    nc.scalar.activation(hhi[:, j % 2, :], hid[:, j % 2, :], ACT.Copy).then_inc(h_hi, 1)
                    if r == 0 and not (last_one and gi == NG - 1):
                        act.wait_ge(used, ONE + e * NG + gi)
                        high(e, gi + 1)
                act.wait_ge(used, ONE + e * NG + NG)
                for m in range(KC):
                    nc.scalar.activation(oT[:, m, :], op[m][:, 0:CAP], ACT.Identity,
                                         bias=b2[:, bass.ds(e, 1), m:m + 1].rearrange("p a b -> p (a b)")).then_inc(o_in, 1)
                act.wait_ge(y_free, ONE + e)
                for n in range(2 * NS):
                    c, hf = divmod(n, 2)
                    act.wait_ge(turned, e * 2 * NS + n + 1)
                    nc.scalar.activation(y[:, c, hf * HALF:(hf + 1) * HALF], hp[n % 2][0:SUB, 0:HALF], ACT.Copy).then_inc(y_in, 1)

            act.wait_ge(b_in, 32)
            high(0, 0)
            with act.Fori(0, E1 - 1) as e:
                expert(e, False)
            expert(E1 - 1, True)

        @block.vector
        def _(dve):
            for count in (x_in, raised):
                dve.sem_inc(count, 1)

            def low(e, gi):
                dve.wait_ge(w_hi, e * NG + gi + 1)
                for m in range(2):
                    last = nc.vector.tensor_tensor(wlo[:, gi % 2, m, :], raw[:, gi % 2, m, :],
                                                   whi[:, gi % 2, m, :].bitcast(F32), ALU.subtract)
                last.then_inc(w_lo, 1)

            def take_in(e):
                for c in range(NS):
                    dve.wait_ge(flipped, ONE + e * NS + c + 1)
                    src = hp[c % 2][:, 0:KC * SUB].rearrange("p (k c) -> p k c", k=KC)
                    at = slice(c * SUB, (c + 1) * SUB)
                    nc.vector.tensor_copy(xhi[:, :, at], src).then_inc(x_hi, 1)
                    dve.wait_ge(x_hi, e * NS + c + 1)
                    nc.vector.tensor_tensor(xlo[:, :, at], src, xhi[:, :, at].bitcast(F32), ALU.subtract).then_inc(x_in, 1)
                dve.wait_ge(x_in, ONE + e * NS + NS)
                dve.sem_inc(xg_free, 1)

            def expert(e, last_one):
                for j in range(HB):
                    gi, r = divmod(j, GH)
                    dve.wait_ge(h_hi, e * HB + j + 1)
                    nc.vector.tensor_tensor(hlo[:, j % 2, :], hid[:, j % 2, :], hhi[:, j % 2, :].bitcast(F32),
                                            ALU.subtract).then_inc(raised, 1)
                    if r == 0 and not (last_one and gi == NG - 1):
                        low(e, gi + 1)
                if not last_one:
                    take_in(e + 1)

            take_in(0)
            low(0, 0)
            with dve.Fori(0, E1 - 1) as e:
                expert(e, False)
            expert(E1 - 1, True)


def stage_combine(nc, g):
    with ExitStack() as ctx:
        s = Scope(nc, ctx, "comb")
        SL = 4
        y = s.sb("y", [P, SL, D])
        got = g.got
        added, stored = s.sem("added"), s.sem("stored")
        block = ctx.enter_context(nc.Block())

        @block.gpsimd
        def _(pool):
            for n in range(2 * T):
                t, k = divmod(n, 2)
                if n >= SL:
                    pool.wait_ge(added, n - SL + 1)
                pool.indirect_dma_start(out=y[:, n % SL, :], out_offset=None, in_=g.slot_out,
                                        in_offset=bass.IndirectOffsetOnAxis(ap=g.read_i[:, k, t:t + 1], axis=0)).then_inc(got[n % SL], 16)

        @block.vector
        def _(dve):
            for n in range(2 * T):
                t, k = divmod(n, 2)
                dve.wait_ge(got[n % SL], 16 * (n // SL + 1))
                dve.wait_ge(added, n)
                nc.vector.scalar_tensor_tensor(g.X[:, t, :], y[:, n % SL, :], g.share[:, k, t:t + 1], g.X[:, t, :],
                                               ALU.mult, ALU.add).then_inc(added, 1)

        @block.sync
        def _(sp):
            for h in range(2):
                sp.wait_ge(added, T * (h + 1))
                sp.dma_start(g.out[h * N // 2:(h + 1) * N // 2].rearrange("(t p) d -> p t d", p=P),
                             g.X[:, h * T // 2:(h + 1) * T // 2, :]).then_inc(stored, 16)
            sp.wait_ge(stored, 32)


class Shared:

    def __init__(self, dram):
        self.x, self.edge_cols, self.edge_rows, self.edge_w, self.mix0_w = dram["x"], dram["edge_cols"], dram["edge_rows"], dram["edge_w"], dram["mix0_w"]
        self.mix0_proj, self.mix0_proj_b, self.gcn_wd, self.gcn_bd, self.gcn_wu = dram["mix0_proj"], dram["mix0_proj_b"], dram["gcn_wd"], dram["gcn_bd"], dram["gcn_wu"]
        self.gcn_bu, self.gcn_w1, self.gcn_b1, self.gcn_w2, self.gcn_b2 = dram["gcn_bu"], dram["gcn_w1"], dram["gcn_b1"], dram["gcn_w2"], dram["gcn_b2"]
        self.gate_w1, self.gate_b1, self.gate_w2, self.gate_b2, self.exp0_w = dram["gate_w1"], dram["gate_b1"], dram["gate_w2"], dram["gate_b2"], dram["exp0_w"]
        self.exp0_par, self.exp0_bv, self.mix1_w, self.mix1_bq, self.mix1_bkv = dram["exp0_par"], dram["exp0_bv"], dram["mix1_w"], dram["mix1_bq"], dram["mix1_bkv"]
        self.mix1_wo, self.mix1_bo, self.gat0_w, self.gat0_att, self.gat0_b = dram["mix1_wo"], dram["mix1_bo"], dram["gat0_w"], dram["gat0_att"], dram["gat0_b"]
        self.gat1_w, self.gat1_att, self.gat1_b, self.route_w, self.exp1_w1 = dram["gat1_w"], dram["gat1_att"], dram["gat1_b"], dram["route_w"], dram["exp1_w1"]
        self.exp1_w2, self.exp1_b1, self.exp1_b2, self.ffn0_wp, self.ffn0_bp = dram["exp1_w2"], dram["exp1_b1"], dram["exp1_b2"], dram["ffn0_wp"], dram["ffn0_bp"]
        self.out = dram["out"]


def setup(nc, dram, ctx):
    g = Shared(dram)
    sb = lambda n, sh, dt=F32: ctx.enter_context(nc.sbuf_tensor(n, sh, dt))
    sem = lambda name: ctx.enter_context(nc.semaphore(name))
    g.put_w, g.put_c, g.slot_put, g.gathered = sem("put_w"), sem("put_c"), sem("slot_put"), sem("gathered")
    g.zeroed = sem("zeroed")
    g.got = [sem(f"got{i}") for i in range(4)]
    g.X = sb("X", [P, T, D])
    g.XT = sb("XT", [128, KC, N])
    g.OT = sb("OT", [128, KC, N])
    g.ident, g.ones = sb("ident", [128, 128]), sb("ones", [128, 128])
    g.halves = sb("halves", [128, 128])
    g.lower, g.causal = sb("lower", [P, P]), sb("causal", [P, P])
    g.before3, g.before8 = sb("before3", [P, E0 * E0]), sb("before8", [P, E1 * E1])
    g.slots, g.read_i = sb("slots", [SUB, E1 * NS], I32), sb("read_i", [P, 2, T], I32)
    g.share = sb("share", [P, 2, T])
    g.slot_token = nc.dram_tensor("slot_token", [SLOTS + 2 * N, 1], I32, kind="Internal").ap()
    g.slot_out = nc.dram_tensor("slot_out", [SLOTS, D], F32, kind="Internal").ap()
    g.xn3 = nc.dram_tensor("xn3", [N, D], F32, kind="Internal").ap()
    g.gate = sb("gate", [P, T, E0])
    g.zero_tail = sb("zero_tail", [1, TABLE - MAIN])
    g.two, g.eps = sb("two", [128, 1]), sb("eps", [128, 1])
    g.ew_table = nc.dram_tensor("ew_table", [TABLE, 1], F32, kind="Internal").ap()
    g.cnt_table = nc.dram_tensor("cnt_table", [TABLE, 1], F32, kind="Internal").ap()
    return g


def build_program(nc, dram):
    SEMAPHORES.clear()
    with ExitStack() as ctx:
        g = setup(nc, dram, ctx)
        todo = [
            lambda: stage_start(nc, g),
            lambda: stage_norm(nc, g, "norm0"),
            lambda: stage_poly_mix(nc, g),
            lambda: stage_tok_linear(nc, g, "proj0", g.OT, g.mix0_proj, g.mix0_proj_b),
            lambda: stage_gcn(nc, g),
            lambda: stage_norm(nc, g, "norm1"),
            lambda: stage_gate(nc, g),
            lambda: stage_experts0(nc, g),
            lambda: stage_tok_linear(nc, g, "proj1", g.OT, g.ffn0_wp, g.ffn0_bp),
            lambda: stage_clear(nc, g),
            lambda: stage_norm(nc, g, "norm2"),
            lambda: stage_linear_mix(nc, g),
            lambda: stage_tok_linear(nc, g, "proj2", g.OT, g.mix1_wo, g.mix1_bo),
            lambda: stage_gat(nc, g, "gat0", g.XT, g.OT, g.gat0_w, g.gat0_att, g.gat0_b, False, g.gat1_w),
            lambda: stage_gat(nc, g, "gat1", g.OT, g.XT, None, g.gat1_att, g.gat1_b, True),
            lambda: stage_norm(nc, g, "norm3", g.xn3),
            lambda: stage_route(nc, g),
            lambda: stage_experts1(nc, g),
            lambda: stage_combine(nc, g),
        ]
        for stage in todo:
            stage()


def lay_out(i):
    a = {k: np.asarray(v) for k, v in i.items()}
    con = np.ascontiguousarray
    pad = lambda v, fill: np.concatenate([v, np.full(PADDED - EDGES, fill, v.dtype)])
    src, dst, ew = pad(a["src"], N), pad(a["dst"], 0), pad(a["edge_weight"], 0)
    cols = lambda v: v.reshape(GROUPS, P).T
    heads = lambda wq, wk, wv: con(np.stack([m.reshape(KC, 128, PAIRS, 128).transpose(2, 1, 0, 3)
                                             for m in (wq, wk, wv)], 3).reshape(PAIRS, 128, KC, 384))
    qkv = a["L0_mix_qkv_w"].T
    feat = lambda b: b.reshape(-1, 128).T
    conv = np.zeros((E0, 4, D // E0), np.float32)
    conv[:, 1] = 1
    conv[0, 0:3], conv[0, 3] = a["L0_ffn_conv_w"][:, 0].T, a["L0_ffn_conv_b"]
    wqk, bqk = a["L0_ffn_Wqk"], a["L0_ffn_bqk"]
    exp0 = [np.concatenate([wqk[:, e * HE:(e + 1) * HE], wqk[:, D + e * HE:D + (e + 1) * HE], a["L0_ffn_Wv"][e]], 1)
            .reshape(KC, 128, 3 * HE).transpose(1, 0, 2) for e in range(E0)]
    par0 = [np.concatenate([feat(bqk[e * HE:(e + 1) * HE]), feat(bqk[D + e * HE:D + (e + 1) * HE]),
                            *(feat(c) for c in conv[e])], 1) for e in range(E0)]
    o = {
        "x": a["x"],
        "edge_cols": con(np.stack([cols(src), cols(dst)], 1)),
        "edge_rows": con(np.stack([src, dst])),
        "edge_w": con(ew),
        "mix0_w": heads(qkv[:, :D], qkv[:, D:2 * D], qkv[:, 2 * D:]),
        "mix0_proj": con(a["L0_mix_proj_w"].T),
        "mix0_proj_b": a["L0_mix_proj_b"],
        "gcn_wd": a["L0_gnn_Wd"], "gcn_bd": a["L0_gnn_bd"][:, None],
        "gcn_wu": a["L0_gnn_Wu"], "gcn_bu": feat(a["L0_gnn_bu"]),
        "gcn_w1": a["L0_gnn_W1"], "gcn_b1": a["L0_gnn_b1"],
        "gcn_w2": a["L0_gnn_W2"], "gcn_b2": a["L0_gnn_b2"],
        "gate_w1": a["L0_ffn_Wg1"], "gate_b1": a["L0_ffn_bg1"][:, None],
        "gate_w2": a["L0_ffn_Wg2"], "gate_b2": a["L0_ffn_bg2"],
        "exp0_w": np.stack(exp0), "exp0_par": np.stack(par0), "exp0_bv": a["L0_ffn_bv"],
        "mix1_w": heads(a["L1_mix_Wq"], a["L1_mix_Wk"], a["L1_mix_Wv"]),
        "mix1_bq": feat(a["L1_mix_bq"]),
        "mix1_bkv": np.concatenate([a["L1_mix_bk"].reshape(PAIRS, 128), a["L1_mix_bv"].reshape(PAIRS, 128)], 1),
        "mix1_wo": a["L1_mix_Wo"], "mix1_bo": a["L1_mix_bo"],
        "gat0_w": a["L1_gnn_W1"], "gat0_att": np.stack([a["L1_gnn_att_src1"], a["L1_gnn_att_dst1"]]),
        "gat0_b": feat(a["L1_gnn_b1"]),
        "gat1_w": a["L1_gnn_W2"], "gat1_att": np.stack([a["L1_gnn_att_src2"], a["L1_gnn_att_dst2"]]),
        "gat1_b": a["L1_gnn_b2"],
        "route_w": a["L1_ffn_Wg"],
        "exp1_w1": a["L1_ffn_W1"].reshape(E1, KC, 128, HB // 2, 2, 128).transpose(0, 3, 2, 4, 1, 5).reshape(E1 * HB // 2, 128, 2 * D),
        "exp1_w2": a["L1_ffn_W2"].reshape(E1, HB // 2, 2, 128, D).transpose(0, 1, 3, 2, 4).reshape(E1 * HB // 2, 128, 2 * D),
        "exp1_b1": a["L1_ffn_b1"].reshape(E1, HB, 128).transpose(2, 0, 1),
        "exp1_b2": a["L1_ffn_b2"].reshape(E1, KC, 128).transpose(2, 0, 1),
        "ffn0_wp": a["L0_ffn_Wp"], "ffn0_bp": a["L0_ffn_bp"],
    }
    return {k: con(v) for k, v in o.items()}


def kernel(**inputs):
    import concourse.bacc as _bacc
    from concourse import mybir as _mybir
    from concourse.bass_utils import run_bass_kernel_spmd as _run

    nc = _bacc.Bacc("TRN2", target_bir_lowering=False, num_devices=1)
    arrays = lay_out(inputs)
    dram = {k: nc.dram_tensor(f"in_{k}", v.shape, _mybir.dt.from_np(v.dtype), kind="ExternalInput").ap()
            for k, v in arrays.items()}
    dram["out"] = nc.dram_tensor("out", (N, D), F32, kind="ExternalOutput").ap()
    build_program(nc, dram)
    r = _run(nc, [{f"in_{k}": v for k, v in arrays.items()}], core_ids=[0])
    return r.results[0]["out"]
```
